# Optimizing a Trainium2 kernel written in Bass

```python
import numpy as np
import jax
import jax.numpy as jnp

def _softmax(x, axis=-1):
    return jax.nn.softmax(x, axis=axis)

def _gelu(x):
    return jax.nn.gelu(x, approximate=True)

def _silu(x):
    return jax.nn.silu(x)

def _sigmoid(x):
    return jax.nn.sigmoid(x)

def _layernorm(x, axis=-1, eps=1e-05):
    m = jnp.mean(x, axis=axis, keepdims=True)
    v = jnp.var(x, axis=axis, keepdims=True)
    return (x - m) / jnp.sqrt(v + eps)

def _scatter_add(tgt, idx, src, axis=0):
    return tgt.at[idx].add(src)

def _segment_sum(src, seg, n):
    return jax.ops.segment_sum(src, seg, n)
kernel_name = 'mk_gnn_resnorm_d4_gnn_r32_ac6399'

def setup_inputs(seed: int=0):
    np.random.seed(seed)
    _w = jnp.asarray

    def _rec_inputs():
        import jax
        import jax.numpy as jnp
        _gk = jax.random.key(seed)
        x = -0.0002117 + 1 * jax.random.normal(jax.random.fold_in(_gk, 1), (3125, 256), jnp.float32)
        src = jax.random.randint(jax.random.fold_in(_gk, 2), (50000,), 0, 3125, jnp.int32)
        dst = jnp.minimum((3125 * jax.random.uniform(jax.random.fold_in(_gk, 3), (50000,)) ** 2.0).astype(jnp.int32), 99999)
        _o = jnp.argsort(dst, stable=True)
        src = src[_o]
        dst = dst[_o]
        edge_weight = jax.random.uniform(jax.random.fold_in(_gk, 13), (50000,), jnp.float32, 0.0, 1)
        return (x, src, dst, edge_weight)
    x, src, dst, edge_weight = _rec_inputs()

    def _L0_gnn_setup():
        import jax, jax.numpy as jnp
        import numpy as np
        N = 3125
        D_IN = 256
        D_OUT = 256
        E = 100000
        key = jax.random.key(seed)
        ks = jax.random.split(key, 9)
        x = jax.random.normal(ks[0], (N, D_IN), dtype=jnp.float32)
        edge_src = jax.random.randint(ks[1], (E,), 0, N, dtype=jnp.int32)
        edge_dst = jax.random.randint(ks[2], (E,), 0, N, dtype=jnp.int32)
        edge_weight = jax.random.uniform(ks[3], (E,), dtype=jnp.float32)
        eps = jnp.zeros((1,), dtype=jnp.float32)
        lim1 = 1.0 / np.sqrt(D_IN)
        w1 = jax.random.uniform(ks[4], (D_IN, D_OUT), minval=-lim1, maxval=lim1, dtype=jnp.float32)
        b1 = jax.random.uniform(ks[5], (D_OUT,), minval=-lim1, maxval=lim1, dtype=jnp.float32)
        lim2 = 1.0 / np.sqrt(D_OUT)
        w2 = jax.random.uniform(ks[6], (D_OUT, D_OUT), minval=-lim2, maxval=lim2, dtype=jnp.float32)
        b2 = jax.random.uniform(ks[7], (D_OUT,), minval=-lim2, maxval=lim2, dtype=jnp.float32)
        return {'x': x, 'edge_src': edge_src, 'edge_dst': edge_dst, 'edge_weight': edge_weight, 'eps': eps, 'w1': w1, 'b1': b1, 'w2': w2, 'b2': b2}
    _L0_gnn_all = _L0_gnn_setup()
    _L0_gnn_in = {k: v for k, v in _L0_gnn_all.items() if k in ('eps', 'w1', 'b1', 'w2', 'b2')}
    del _L0_gnn_all

    def _L1_gnn_setup():
        import jax, jax.numpy as jnp
        import numpy as np
        NEG = -1000.0
        SLOPE = 0.01
        N_NODES, N_EDGES, D_IN, D_OUT, N_HEADS = (3125, 50000, 256, 64, 4)
        key = jax.random.key(seed)
        k0, k1, k2, k3, k4 = jax.random.split(key, 5)
        h = jax.random.normal(k0, (N_NODES, D_IN), jnp.float32)
        src = jax.random.randint(k1, (N_EDGES,), 0, N_NODES)
        dst = jax.random.randint(k2, (N_EDGES,), 0, N_NODES)
        W = jax.random.normal(k3, (N_HEADS, D_IN, D_OUT), jnp.float32) / np.sqrt(D_IN)
        att = jax.random.normal(k4, (N_HEADS, 2 * D_OUT), jnp.float32) / np.sqrt(2.0 * D_OUT)
        return {'h': h, 'W': W, 'att': att, 'src': src, 'dst': dst}
    _L1_gnn_all = _L1_gnn_setup()
    _L1_gnn_in = {k: v for k, v in _L1_gnn_all.items() if k in ('W', 'att')}
    del _L1_gnn_all

    def _L2_gnn_setup():
        import jax, jax.numpy as jnp
        import numpy as np
        N = 50000
        E = 25000
        F_IN = 256
        HID = 64
        HEADS = 4

        def _segment_softmax(logits, seg, num_segments):
            m = jax.ops.segment_max(logits, seg, num_segments=num_segments)
            e = jnp.exp(logits - m[seg])
            z = jax.ops.segment_sum(e, seg, num_segments=num_segments)
            return e / z[seg]

        def _gat_layer(x, src, dst, W, a_src, a_dst, b, num_nodes):
            H, C = a_src.shape
            h = (x @ W).reshape(num_nodes, H, C)
            al_s = jnp.einsum('nhc,hc->nh', h, a_src)
            al_d = jnp.einsum('nhc,hc->nh', h, a_dst)
            logits = jax.nn.leaky_relu(al_s[src] + al_d[dst], 0.2)
            alpha = _segment_softmax(logits, dst, num_nodes)
            msg = h[src] * alpha[:, :, None]
            out = jax.ops.segment_sum(msg, dst, num_segments=num_nodes)
            return out.reshape(num_nodes, H * C) + b
        key = jax.random.key(seed)
        ks = jax.random.split(key, 12)
        s = 0.05
        x = jax.random.normal(ks[0], (N, F_IN), dtype=jnp.float32)
        edge_index = jax.random.randint(ks[1], (2, E), 0, N, dtype=jnp.int64)
        W1 = jax.random.normal(ks[2], (F_IN, HEADS * HID), dtype=jnp.float32) * s
        att_src1 = jax.random.normal(ks[3], (HEADS, HID), dtype=jnp.float32) * s
        att_dst1 = jax.random.normal(ks[4], (HEADS, HID), dtype=jnp.float32) * s
        b1 = jnp.zeros((HEADS * HID,), dtype=jnp.float32)
        W2 = jax.random.normal(ks[5], (HEADS * HID, HID), dtype=jnp.float32) * s
        att_src2 = jax.random.normal(ks[6], (1, HID), dtype=jnp.float32) * s
        att_dst2 = jax.random.normal(ks[7], (1, HID), dtype=jnp.float32) * s
        b2 = jnp.zeros((HID,), dtype=jnp.float32)
        Wf = jax.random.normal(ks[8], (HID, F_IN), dtype=jnp.float32) * s
        bf = jnp.zeros((F_IN,), dtype=jnp.float32)
        return {'x': x, 'edge_index': edge_index, 'W1': W1, 'att_src1': att_src1, 'att_dst1': att_dst1, 'b1': b1, 'W2': W2, 'att_src2': att_src2, 'att_dst2': att_dst2, 'b2': b2, 'Wf': Wf, 'bf': bf}
    _L2_gnn_all = _L2_gnn_setup()
    _L2_gnn_in = {k: v for k, v in _L2_gnn_all.items() if k in ('W1', 'att_src1', 'att_dst1', 'b1', 'W2', 'att_src2', 'att_dst2', 'b2', 'Wf', 'bf')}
    del _L2_gnn_all

    def _L3_gnn_setup():
        import jax, jax.numpy as jnp
        import numpy as np
        N = 10000
        E = 10000
        D = 256
        EPS = 1e-05

        def layer_norm(x, g, b):
            mu = jnp.mean(x, axis=-1, keepdims=True)
            var = jnp.mean(jnp.square(x - mu), axis=-1, keepdims=True)
            return (x - mu) * jax.lax.rsqrt(var + EPS) * g + b

        def linear(x, w, b):
            return x @ w + b
        key = jax.random.key(seed)
        ks = jax.random.split(key, 20)
        s = 1.0 / np.sqrt(D)
        inp = {'x': jax.random.normal(ks[0], (N, D), jnp.float32), 'edge_index': jax.random.randint(ks[1], (2, E), 0, N, jnp.int64), 'edge_weight': jax.random.normal(ks[2], (E,), jnp.float32), 'wq': jax.random.normal(ks[3], (D, D), jnp.float32) * s, 'bq': jnp.zeros((D,), jnp.float32), 'wk': jax.random.normal(ks[4], (D, D), jnp.float32) * s, 'bk': jnp.zeros((D,), jnp.float32), 'wv': jax.random.normal(ks[5], (D, D), jnp.float32) * s, 'bv': jnp.zeros((D,), jnp.float32), 'ws': jax.random.normal(ks[6], (D, D), jnp.float32) * s, 'bs': jnp.zeros((D,), jnp.float32), 'we': jax.random.normal(ks[7], (1, 1), jnp.float32), 'be': jnp.zeros((1,), jnp.float32), 'g1': jnp.ones((D,), jnp.float32), 'b1': jnp.zeros((D,), jnp.float32), 'g2': jnp.ones((D,), jnp.float32), 'b2': jnp.zeros((D,), jnp.float32), 'w_ff1': jax.random.normal(ks[8], (D, 2 * D), jnp.float32) * s, 'b_ff1': jnp.zeros((2 * D,), jnp.float32), 'w_ff2': jax.random.normal(ks[9], (2 * D, D), jnp.float32) * (1.0 / np.sqrt(2 * D)), 'b_ff2': jnp.zeros((D,), jnp.float32)}
        return inp
    _L3_gnn_all = _L3_gnn_setup()
    _L3_gnn_in = {k: v for k, v in _L3_gnn_all.items() if k in ('wq', 'bq', 'wk', 'bk', 'wv', 'bv', 'ws', 'bs', 'we', 'be', 'g1', 'b1', 'g2', 'b2', 'w_ff1', 'b_ff1', 'w_ff2', 'b_ff2')}
    del _L3_gnn_all
    return {'x': x, 'src': src, 'dst': dst, 'edge_weight': edge_weight, 'L0_gnn_eps': _L0_gnn_in['eps'], 'L0_gnn_w1': _L0_gnn_in['w1'], 'L0_gnn_b1': _L0_gnn_in['b1'], 'L0_gnn_w2': _L0_gnn_in['w2'], 'L0_gnn_b2': _L0_gnn_in['b2'], 'L1_gnn_W': _L1_gnn_in['W'], 'L1_gnn_att': _L1_gnn_in['att'], 'L2_gnn_W1': _L2_gnn_in['W1'], 'L2_gnn_att_src1': _L2_gnn_in['att_src1'], 'L2_gnn_att_dst1': _L2_gnn_in['att_dst1'], 'L2_gnn_b1': _L2_gnn_in['b1'], 'L2_gnn_W2': _L2_gnn_in['W2'], 'L2_gnn_att_src2': _L2_gnn_in['att_src2'], 'L2_gnn_att_dst2': _L2_gnn_in['att_dst2'], 'L2_gnn_b2': _L2_gnn_in['b2'], 'L2_gnn_Wf': _L2_gnn_in['Wf'], 'L2_gnn_bf': _L2_gnn_in['bf'], 'L3_gnn_wq': _L3_gnn_in['wq'], 'L3_gnn_bq': _L3_gnn_in['bq'], 'L3_gnn_wk': _L3_gnn_in['wk'], 'L3_gnn_bk': _L3_gnn_in['bk'], 'L3_gnn_wv': _L3_gnn_in['wv'], 'L3_gnn_bv': _L3_gnn_in['bv'], 'L3_gnn_ws': _L3_gnn_in['ws'], 'L3_gnn_bs': _L3_gnn_in['bs'], 'L3_gnn_we': _L3_gnn_in['we'], 'L3_gnn_be': _L3_gnn_in['be'], 'L3_gnn_g1': _L3_gnn_in['g1'], 'L3_gnn_b1': _L3_gnn_in['b1'], 'L3_gnn_g2': _L3_gnn_in['g2'], 'L3_gnn_b2': _L3_gnn_in['b2'], 'L3_gnn_w_ff1': _L3_gnn_in['w_ff1'], 'L3_gnn_b_ff1': _L3_gnn_in['b_ff1'], 'L3_gnn_w_ff2': _L3_gnn_in['w_ff2'], 'L3_gnn_b_ff2': _L3_gnn_in['b_ff2']}

def reference(x, src, dst, edge_weight, L0_gnn_eps, L0_gnn_w1, L0_gnn_b1, L0_gnn_w2, L0_gnn_b2, L1_gnn_W, L1_gnn_att, L2_gnn_W1, L2_gnn_att_src1, L2_gnn_att_dst1, L2_gnn_b1, L2_gnn_W2, L2_gnn_att_src2, L2_gnn_att_dst2, L2_gnn_b2, L2_gnn_Wf, L2_gnn_bf, L3_gnn_wq, L3_gnn_bq, L3_gnn_wk, L3_gnn_bk, L3_gnn_wv, L3_gnn_bv, L3_gnn_ws, L3_gnn_bs, L3_gnn_we, L3_gnn_be, L3_gnn_g1, L3_gnn_b1, L3_gnn_g2, L3_gnn_b2, L3_gnn_w_ff1, L3_gnn_b_ff1, L3_gnn_w_ff2, L3_gnn_b_ff2):
    import jax
    import jax.numpy as jnp

    def _L0_gnn_ref(x, edge_src, edge_dst, edge_weight, eps, w1, b1, w2, b2):
        import jax, jax.numpy as jnp
        import numpy as np
        N = 3125
        D_IN = 256
        D_OUT = 256
        E = 100000
        msgs = edge_weight[:, None] * x[edge_src]
        agg = jax.ops.segment_sum(msgs, edge_dst, num_segments=N)
        h = (1.0 + eps[0]) * x + agg
        h = jax.nn.relu(h @ w1 + b1)
        return h @ w2 + b2

    def _L1_gnn_ref(h, W, att, src, dst):
        import jax, jax.numpy as jnp
        import numpy as np
        NEG = -1000.0
        SLOPE = 0.01
        N_NODES, N_EDGES, D_IN, D_OUT, N_HEADS = (3125, 50000, 256, 64, 4)
        N = h.shape[0]
        H, _, F = W.shape
        z = jnp.einsum('nd,hdf->nhf', h, W)
        a_src, a_dst = (att[:, :F], att[:, F:])
        es = jnp.einsum('nhf,hf->nh', z, a_src)
        ed = jnp.einsum('nhf,hf->nh', z, a_dst)
        e = jax.nn.leaky_relu(es[src] + ed[dst], SLOPE)
        e = jnp.where(e == 0.0, NEG, e)
        m = jax.ops.segment_max(e, dst, num_segments=N)
        m = jnp.where(jnp.isfinite(m), m, 0.0)
        ex = jnp.exp(e - m[dst])
        denom = jax.ops.segment_sum(ex, dst, num_segments=N)
        safe = jnp.where(denom[dst] > 0.0, denom[dst], 1.0)
        alpha = ex / safe
        out = jax.ops.segment_sum(alpha[:, :, None] * z[src], dst, num_segments=N)
        return out.reshape(N, H * F)

    def _L2_gnn_ref(x, edge_index, W1, att_src1, att_dst1, b1, W2, att_src2, att_dst2, b2, Wf, bf):
        import jax, jax.numpy as jnp
        import numpy as np
        N = 50000
        E = 25000
        F_IN = 256
        HID = 64
        HEADS = 4

        def _segment_softmax(logits, seg, num_segments):
            m = jax.ops.segment_max(logits, seg, num_segments=num_segments)
            e = jnp.exp(logits - m[seg])
            z = jax.ops.segment_sum(e, seg, num_segments=num_segments)
            return e / z[seg]

        def _gat_layer(x, src, dst, W, a_src, a_dst, b, num_nodes):
            H, C = a_src.shape
            h = (x @ W).reshape(num_nodes, H, C)
            al_s = jnp.einsum('nhc,hc->nh', h, a_src)
            al_d = jnp.einsum('nhc,hc->nh', h, a_dst)
            logits = jax.nn.leaky_relu(al_s[src] + al_d[dst], 0.2)
            alpha = _segment_softmax(logits, dst, num_nodes)
            msg = h[src] * alpha[:, :, None]
            out = jax.ops.segment_sum(msg, dst, num_segments=num_nodes)
            return out.reshape(num_nodes, H * C) + b
        num_nodes = x.shape[0]
        loop = jnp.arange(num_nodes, dtype=edge_index.dtype)
        src = jnp.concatenate([edge_index[0], loop])
        dst = jnp.concatenate([edge_index[1], loop])
        h = jax.nn.relu(_gat_layer(x, src, dst, W1, att_src1, att_dst1, b1, num_nodes))
        h = _gat_layer(h, src, dst, W2, att_src2, att_dst2, b2, num_nodes)
        return h @ Wf + bf

    def _L3_gnn_ref(x, edge_index, edge_weight, wq, bq, wk, bk, wv, bv, ws, bs, we, be, g1, b1, g2, b2, w_ff1, b_ff1, w_ff2, b_ff2):
        import jax, jax.numpy as jnp
        import numpy as np
        N = 10000
        E = 10000
        D = 256
        EPS = 1e-05

        def layer_norm(x, g, b):
            mu = jnp.mean(x, axis=-1, keepdims=True)
            var = jnp.mean(jnp.square(x - mu), axis=-1, keepdims=True)
            return (x - mu) * jax.lax.rsqrt(var + EPS) * g + b

        def linear(x, w, b):
            return x @ w + b
        n = x.shape[0]
        scale = x.shape[-1] ** (-0.5)
        q = linear(x, wq, bq)
        k = linear(x, wk, bk)
        v = linear(x, wv, bv)
        src, dst = (edge_index[0], edge_index[1])
        scores = jnp.sum(q[dst] * k[src], axis=-1) * scale
        scores = scores + (edge_weight[:, None] @ we + be)[:, 0]
        seg_max = jax.ops.segment_max(scores, dst, num_segments=n)
        exp_s = jnp.exp(scores - seg_max[dst])
        denom = jax.ops.segment_sum(exp_s, dst, num_segments=n)
        attn = exp_s / jnp.maximum(denom[dst], 1e-12)
        message = v[src] * attn[:, None]
        out = jax.ops.segment_sum(message, dst, num_segments=n)
        x = layer_norm(x + out + linear(x, ws, bs), g1, b1)
        ffn = linear(jax.nn.gelu(linear(x, w_ff1, b_ff1)), w_ff2, b_ff2)
        x = layer_norm(x + ffn, g2, b2)
        return x
    edge_index = jnp.stack([src, dst])
    x = _layernorm(x + _L0_gnn_ref(x, src, dst, edge_weight, L0_gnn_eps, L0_gnn_w1, L0_gnn_b1, L0_gnn_w2, L0_gnn_b2), axis=-1)
    x = _layernorm(x + _L1_gnn_ref(x, L1_gnn_W, L1_gnn_att, src, dst), axis=-1)
    x = _layernorm(x + _L2_gnn_ref(x, edge_index, L2_gnn_W1, L2_gnn_att_src1, L2_gnn_att_dst1, L2_gnn_b1, L2_gnn_W2, L2_gnn_att_src2, L2_gnn_att_dst2, L2_gnn_b2, L2_gnn_Wf, L2_gnn_bf), axis=-1)
    x = _layernorm(x + _L3_gnn_ref(x, edge_index, edge_weight, L3_gnn_wq, L3_gnn_bq, L3_gnn_wk, L3_gnn_bk, L3_gnn_wv, L3_gnn_bv, L3_gnn_ws, L3_gnn_bs, L3_gnn_we, L3_gnn_be, L3_gnn_g1, L3_gnn_b1, L3_gnn_g2, L3_gnn_b2, L3_gnn_w_ff1, L3_gnn_b_ff1, L3_gnn_w_ff2, L3_gnn_b_ff2), axis=-1)
    return x

_drawn_inputs = setup_inputs


def setup_inputs(seed=0):
    import zlib

    import numpy as np

    out = dict(_drawn_inputs(seed))
    spreads = {'L2_gnn_b1': (0.0, 0.446),
     'L2_gnn_b2': (0.0, 0.1),
     'L2_gnn_bf': (0.0, 0.1),
     'L3_gnn_bq': (0.0, 0.693),
     'L3_gnn_bk': (0.0, 2.0),
     'L3_gnn_bv': (0.0, 0.1),
     'L3_gnn_bs': (0.0, 0.1),
     'L3_gnn_g1': (1.0, 0.2),
     'L3_gnn_b1': (0.0, 0.1),
     'L3_gnn_g2': (1.0, 0.2),
     'L3_gnn_b2': (0.0, 0.1),
     'L3_gnn_b_ff1': (0.0, 0.1),
     'L3_gnn_b_ff2': (0.0, 0.1)}
    factors = {'L0_gnn_b1': 3.975,
     'L2_gnn_att_src1': 8.0,
     'L2_gnn_att_dst1': 61.355,
     'L2_gnn_att_src2': 48.238,
     'L2_gnn_att_dst2': 64.0}
    for name, (base, spread) in spreads.items():
        noise = np.random.default_rng([zlib.crc32(name.encode()), seed]).standard_normal(out[name].shape)
        drawn = base * np.exp(spread * noise) if base else spread * noise
        out[name] = jnp.asarray(drawn.astype(out[name].dtype))
    for name, factor in factors.items():
        out[name] = (out[name] * factor).astype(out[name].dtype)
    return out
```

```python
from contextlib import ExitStack

import numpy as np

import concourse.bass as bass
from concourse import mybir

F32 = mybir.dt.float32
I32 = mybir.dt.int32
ALU = mybir.AluOpType
ACT = mybir.ActivationFunctionType
AX = mybir.AxisListType.X
DVE_ENGINE = (mybir.EngineType.DVE,)
PE_ENGINE = (mybir.EngineType.PE,)

P = 128
N, E, D = 3125, 50000, 256
KC = D // P
BLOCKS = -(-N // P)
FULL = N // P
REST = N - FULL * P
TILES = -(-E // P)
G = 4
EP = -(-TILES // G)
ROW = G * P
EFULL = E // ROW
EREST = E - EFULL * ROW
STEPS = EP * G + BLOCKS - 1
SPARTS = STEPS // G
U = 16
ITERS = STEPS // U
HALF = U // 2
V = 5
VITERS = BLOCKS // V
HEADS, HID = 4, 64
FF = 2 * D
BIG = 1e30
NODST = 4000.0
EPS = 1e-5
ACCW = D + 2 * HEADS + 1
assert STEPS % U == 0 and STEPS % G == 0 and BLOCKS % V == 0 and TILES + BLOCKS - 1 <= STEPS


class Signal:

    def __init__(self, sem, totals):
        self.sem, self.base, total = sem, {}, 0
        for stage, n in totals.items():
            self.base[stage], total = total, total + n

    def at(self, stage, n):
        return self.base[stage] + n


def due(n):
    return not isinstance(n, int) or n > 0


def each(eng, iters, body):
    body(0)
    with eng.Fori(1, iters - 1) as it:
        body(it)
    body(iters - 1)


def is_last(it, iters):
    return isinstance(it, int) and it == iters - 1


def is_first(it):
    return isinstance(it, int) and it == 0


def build(nc, x, src, dst, edge_weight, L0_gnn_eps, L0_gnn_w1, L0_gnn_b1, L0_gnn_w2, L0_gnn_b2,
          L1_gnn_W, L1_gnn_att, L2_gnn_W1, L2_gnn_att_src1, L2_gnn_att_dst1, L2_gnn_b1, L2_gnn_W2,
          L2_gnn_att_src2, L2_gnn_att_dst2, L2_gnn_b2, L2_gnn_Wf, L2_gnn_bf, L3_gnn_wq, L3_gnn_bq,
          L3_gnn_wk, L3_gnn_bk, L3_gnn_wv, L3_gnn_bv, L3_gnn_ws, L3_gnn_bs, L3_gnn_we, L3_gnn_be,
          L3_gnn_g1, L3_gnn_b1, L3_gnn_g2, L3_gnn_b2, L3_gnn_w_ff1, L3_gnn_b_ff1, L3_gnn_w_ff2,
          L3_gnn_b_ff2, out):
    ctx = ExitStack()
    with ctx:
        def sb(name, shape, dt=F32):
            return ctx.enter_context(nc.sbuf_tensor(name, shape, dt))

        def sem(name):
            return ctx.enter_context(nc.semaphore(name))

        def dram(name, shape):
            return nc.dram_tensor(name, shape, F32, kind="Internal").ap()

        rows_total = BLOCKS * P
        t_z1, t_s1 = dram("t_z1", [rows_total, D]), dram("t_s1", [rows_total, HEADS])
        t_z2, t_s2 = dram("t_z2", [rows_total, D]), dram("t_s2", [rows_total, HEADS])
        t_z3, t_s3 = dram("t_z3", [rows_total, HID]), dram("t_s3", [rows_total, 1])
        t_k, t_v = dram("t_k", [rows_total, D]), dram("t_v", [rows_total, D])

        X = sb("X", [P, BLOCKS, D])
        ACC = sb("ACC", [P, BLOCKS, ACCW])
        Y = sb("Y", [P, BLOCKS, D])
        Yf = Y[:].rearrange("p b d -> p (b d)")
        tab = sb("tab", [P, BLOCKS, 2 * HEADS])
        mean = sb("mean", [P, BLOCKS])
        rstd = sb("rstd", [P, BLOCKS])
        nodeA = sb("nodeA", [P, BLOCKS, HEADS])
        nodeB = sb("nodeB", [P, BLOCKS, HEADS])
        nodeC = sb("nodeC", [P, BLOCKS, HEADS])

        rows = sb("rows", [P, U, D + 1])
        idx = sb("idx", [P, 2, HALF], I32)
        srcK = sb("srcK", [P, STEPS + U], I32)
        dloc = sb("dloc", [P, STEPS])
        wK = sb("wK", [P, STEPS])
        valid = sb("valid", [P, STEPS])
        blockI = sb("blockI", [1, STEPS], I32)
        LG = sb("LG", [P, STEPS, HEADS])
        PX = sb("PX", [P, STEPS, 2 * HEADS + 1])
        M = sb("M", [P, 4, P])
        R = sb("R", [P, 4, ACCW])
        MT = R[:, 0, 0:2 * P].rearrange("p (s e) -> p s e", s=2)
        junk = sb("junk", [P, 2, D])

        rowbuf = sb("rowbuf", [P, 3, HEADS * ROW])
        LT, FT, BT = (rowbuf[0:SPARTS, i, :].rearrange("p (h j) -> p h j", h=HEADS) for i in range(3))
        breakF = sb("breakF", [SPARTS, ROW])
        breakB = sb("breakB", [SPARTS, ROW])
        first = sb("first", [SPARTS, ROW])
        brk = sb("brk", [SPARTS, 2, HEADS])
        spanF = sb("spanF", [HEADS, SPARTS])
        spanB = sb("spanB", [HEADS, SPARTS])
        carryF = sb("carryF", [HEADS, SPARTS + 1])
        carryB = sb("carryB", [HEADS, SPARTS + 1])
        startF = sb("startF", [SPARTS, HEADS])
        startB = sb("startB", [SPARTS, HEADS])
        flat = rowbuf[:].rearrange("p a b -> p (a b)")
        inT = flat[:, 0:V * D].rearrange("p (v k n) -> p v k n", v=V, k=KC)
        hidT = flat[:, V * D:V * (D + FF)].rearrange("p (v m n) -> p v m n", v=V, m=FF // P)
        ZW = D + 2 * HEADS
        zrow = flat[:, V * (D + FF):V * (D + FF + ZW)].rearrange("p (v c) -> p v c", v=V)
        assert V * (D + FF + ZW) <= 3 * HEADS * ROW

        at = [0]

        def temp(parts, words, dt=F32):
            v = Yf[0:parts, at[0]:at[0] + words]
            at[0] += words
            return v.bitcast(dt) if dt != F32 else v

        step_ge = temp(EP, (G + 1) * STEPS).rearrange("p (g k) -> p g k", g=G + 1)
        pick = temp(EP, G * STEPS).rearrange("p (g k) -> p g k", g=G)
        dstT, srcT, wT = temp(EP, ROW), temp(EP, ROW), temp(EP, ROW)
        dstI, srcI = temp(EP, ROW, I32), temp(EP, ROW, I32)
        assert at[0] <= BLOCKS * D
        dstM = LG[:, :, 0]
        stepB = LG[:, :, 1]
        vtmp = LG[:, :, 2]
        DT = LT[:, 0, :]
        nextI = sb("nextI", [EP, 1], I32)
        brk1 = sb("brk1", [SPARTS, 2])
        maskneg = sb("maskneg", [P, STEPS])
        onePeps = sb("onePeps", [P, 1])
        stat = sb("stat", [P, BLOCKS, 6])
        root = sb("root", [P, BLOCKS])
        ACC3 = ACC[:, :, 0:D]
        BLOCK_SHIFT = P.bit_length() - 1
        tileI = sb("tileI", [EP, G + 1], I32)
        tileC = sb("tileC", [EP, G + 1])

        iota = sb("iota", [P, P])
        stepno = junk[:].rearrange("p a d -> p (a d)")[:, 0:STEPS]
        tileno = sb("tileno", [EP, G + 1])
        part = sb("part", [P, 3])
        ident = sb("ident", [P, P])
        up = sb("up", [P, P])
        down = sb("down", [P, P])
        ones = sb("ones", [P, P])

        w1, w2 = sb("w1", [P, KC, D]), sb("w2", [P, KC, D])
        wz1, wz2 = sb("wz1", [P, KC, ZW]), sb("wz2", [P, KC, ZW])
        wz3 = sb("wz3", [P, KC, HID + 2])
        wf = sb("wf", [HID, D])
        wq, wk = sb("wq", [P, KC, D]), sb("wk", [P, KC, D])
        wv, ws = sb("wv", [P, KC, D]), sb("ws", [P, KC, D])
        wff1, wff2 = sb("wff1", [P, KC, FF]), sb("wff2", [P, FF // P, D])
        ACCf = ACC[:].rearrange("p b c -> p (b c)")
        att = ACCf[:, 0:4 * D].rearrange("p (a d) -> p a d", a=4)
        att2 = ACCf[:, 4 * D:4 * D + 2 * HID].rearrange("p (a d) -> p a d", a=2)
        bias = {}
        vectors = [("b2", L0_gnn_b2), ("b3", L2_gnn_b1), ("bf", L2_gnn_bf), ("bq", L3_gnn_bq),
                   ("bk", L3_gnn_bk), ("bv", L3_gnn_bv), ("bs", L3_gnn_bs), ("g1", L3_gnn_g1),
                   ("h1", L3_gnn_b1), ("g2", L3_gnn_g2), ("h2", L3_gnn_b2), ("bff2", L3_gnn_b_ff2),
                   ("b4", L2_gnn_b2)]
        for name, v in vectors:
            bias[name] = sb("v_" + name, [P, v.shape[0]])
        b1c = sb("b1c", [P, KC])
        bff1c = sb("bff1c", [P, FF // P])
        scal = sb("scal", [P, 3])

        PS = [ctx.enter_context(nc.psum_tensor(f"PS{i}", [P, 512], F32)) for i in range(8)]

        def by_chunk(w):
            return w.rearrange("(k p) n -> p k n", p=P)

        weight_loads = [(w1[:], by_chunk(L0_gnn_w1)), (w2[:], by_chunk(L0_gnn_w2)),
                        (b1c[:], L0_gnn_b1.rearrange("(k p) -> p k", p=P)),
                        (bff1c[:], L3_gnn_b_ff1.rearrange("(k p) -> p k", p=P))]
        weight_loads += [(scal[:, c:c + 1], v.partition_broadcast(P))
                         for c, v in enumerate((L0_gnn_eps, L3_gnn_we[0], L3_gnn_be))]
        for h in range(HEADS):
            head = slice(h * HID, (h + 1) * HID)
            weight_loads += [(wz1[:, :, head], by_chunk(L1_gnn_W[h])),
                             (att[:, 0, head], L1_gnn_att[h, 0:HID].partition_broadcast(P)),
                             (att[:, 1, head], L1_gnn_att[h, HID:2 * HID].partition_broadcast(P)),
                             (att[:, 2, head], L2_gnn_att_src1[h].partition_broadcast(P)),
                             (att[:, 3, head], L2_gnn_att_dst1[h].partition_broadcast(P))]
        weight_loads += [(wz2[:, :, 0:D], by_chunk(L2_gnn_W1)), (wz3[:, :, 0:HID], by_chunk(L2_gnn_W2)),
                         (att2[:, 0, :], L2_gnn_att_src2[0].partition_broadcast(P)),
                         (att2[:, 1, :], L2_gnn_att_dst2[0].partition_broadcast(P)), (wf[:], L2_gnn_Wf),
                         (wq[:], by_chunk(L3_gnn_wq)), (wk[:], by_chunk(L3_gnn_wk)),
                         (wv[:], by_chunk(L3_gnn_wv)), (ws[:], by_chunk(L3_gnn_ws)),
                         (wff1[:], by_chunk(L3_gnn_w_ff1)), (wff2[:], by_chunk(L3_gnn_w_ff2))]
        weight_loads += [(bias[name][:], v.partition_broadcast(P)) for name, v in vectors]

        HEADS_OF = {"L1": HEADS, "L2a": HEADS, "L2b": 1, "L3": 1}
        WIDTH = {"L0": D, "L1": D, "L2a": D, "L2b": HID, "L3": D + 1}
        EXTRAS = {"L1": HEADS, "L2a": 2 * HEADS + 1, "L2b": 3}
        SLOPE = {"L1": 0.01, "L2a": 0.2, "L2b": 0.2}
        STEP_GE_AT, EDGES_AT, SOURCES_AT, DSTM_AT, DT_AT, BREAK_AT, SPAN_AT, SETUP_V = 16, 22, 27, 33, 34, 39, 45, 73
        LOGITS_AT = {"L1": 5, "L2a": 3, "L2b": 3, "L3": 4}
        SHIFTED_AT = {s: LOGITS_AT[s] + 4 * h + 5 for s, h in HEADS_OF.items()}
        MAXIMA_AT = {s: SHIFTED_AT[s] + 1 for s in ("L2a", "L2b")}
        COMBINED = {"L1": 7, "L2a": 23, "L2b": 16, "L3": 4}
        VARIANCE_AT = 7
        BANK, BANK_AGE = [0, 1, 2, 3, 1], [5, 2, 5, 5, 3]

        def back_columns(stage):
            heads = HEADS_OF[stage]
            cols = [LT[:, h, :] for h in range(heads)]
            if stage in MAXIMA_AT:
                cols += [FT[:, h, :] for h in range(heads)] + [first[:]]
            return cols

        def at_block(buf, b):
            return buf[:, bass.ds(b, 1), :].rearrange("p o c -> p (o c)")

        def load_blocks(eng, it):
            k = U * it
            _, values = nc.values_load_multi_w_load_instructions(
                blockI[0:1, bass.ds(k, U)], engines=(eng.engine,), min_val=0, max_val=BLOCKS - 1,
                skip_runtime_bounds_check_because="the table was clamped to the blocks")
            return values

        def signal(name, totals):
            return Signal(ctx.enter_context(nc.semaphore(name)), totals)

        def each_of(stages, n):
            return {s: n for s in stages}

        SUMMING = ["L0", "L1", "L2a", "L2b", "L3"]
        SCALED = ["L1", "L2a", "L2b"]
        SOFTMAX = ["L1", "L2a", "L2b", "L3"]
        PRODUCTS = ["mlp", "z1", "z2", "z3", "wf", "qkv", "ws", "ffn"]
        NORMS = ["mlp", "gat", "wf", "ws", "ffn", "last"]

        edges_padded = signal("edges_padded", {"setup": 1})
        edges_in = signal("edges_in", {"setup": 16 * 8})
        features_in = signal("features_in", {"setup": 32})
        weights_in = signal("weights_in", {"setup": 0})
        consts_made = signal("consts_made", {"setup": 6})
        setup_v = signal("setup_v", {"setup": 0})
        setup_p = signal("setup_p", {"setup": 0})
        indices_put = signal("indices_put", {"all": 0})
        half_opened = signal("half_opened", {"all": 0})
        row_landed = [signal(f"row_landed{j}", {"all": 0}) for j in range(U)]
        sums_zeroed = signal("sums_zeroed", each_of(SUMMING, 1))
        onehot_made = signal("onehot_made", each_of(SUMMING, STEPS))
        row_scaled = signal("row_scaled", each_of(SCALED, STEPS))
        extras_put = signal("extras_put", each_of(SCALED, STEPS))
        step_summed = signal("step_summed", each_of(SUMMING, STEPS))
        sum_added = signal("sum_added", each_of(SUMMING, STEPS))
        mask_made = signal("mask_made", each_of(SOFTMAX, STEPS))
        mask_turned = signal("mask_turned", each_of(SOFTMAX, STEPS))
        mask_copied = signal("mask_copied", each_of(SOFTMAX, STEPS))
        dst_spread = signal("dst_spread", each_of(SOFTMAX, STEPS))
        logit_made = signal("logit_made", each_of(SOFTMAX, STEPS))
        softmax_v = signal("softmax_v", {s: MAXIMA_AT.get(s, SHIFTED_AT[s]) for s in SOFTMAX})
        softmax_p = signal("softmax_p", {s: 5 + len(back_columns(s)) for s in SOFTMAX})
        softmax_a = signal("softmax_a", {s: 2 + len(back_columns(s)) for s in SOFTMAX})
        input_staged = signal("input_staged", each_of(PRODUCTS, BLOCKS))
        in_turned = signal("in_turned", each_of(PRODUCTS, BLOCKS))
        in_copied = signal("in_copied", each_of(PRODUCTS, BLOCKS))
        hidden_made = signal("hidden_made", each_of(("mlp", "ffn"), BLOCKS))
        hidden_acted = signal("hidden_acted", each_of(("mlp", "ffn"), BLOCKS))
        product_made = signal("product_made", each_of(PRODUCTS, BLOCKS) | {"qkv": 3 * BLOCKS})
        product_copied = signal("product_copied", {"z1": BLOCKS, "z2": 2 * BLOCKS, "z3": 2 * BLOCKS, "qkv": 3 * BLOCKS})
        input_made = signal("input_made", {"mlp": BLOCKS})
        combined_v = signal("combined_v", COMBINED)
        combined_a = signal("combined_a", each_of(("L2a", "L2b"), 2))
        product_added = signal("product_added", each_of(("mlp", "wf", "ws", "ffn"), 2 * BLOCKS))
        stats_made = signal("stats_made", each_of(NORMS, BLOCKS))
        norm_step = signal("norm_step", each_of(NORMS, VARIANCE_AT + 1))
        norm_root = signal("norm_root", each_of(NORMS, 1))
        normed = signal("normed", {"mlp": BLOCKS, "gat": BLOCKS, "wf": BLOCKS, "ws": 3 * BLOCKS,
                                   "ffn": 3 * BLOCKS, "last": BLOCKS})
        residual_added = signal("residual_added", {"last": 1})
        TABLE_LOOPS = {"z1": 32 * VITERS, "z2": 32 * VITERS, "z3": 32 * VITERS, "qkv": 32 * VITERS}
        table_stored = [signal(f"table_stored{v}", TABLE_LOOPS) for v in range(V)]
        out_stored = signal("out_stored", {"out": 32})

        PASSES = [(x, D, None, step_summed, "L0"),
                  (t_s1, HEADS, "z1", logit_made, "L1"), (t_z1, D, "z1", row_scaled, "L1"),
                  (t_s2, HEADS, "z2", logit_made, "L2a"), (t_z2, D, "z2", row_scaled, "L2a"),
                  (t_s3, 1, "z3", logit_made, "L2b"), (t_z3, HID, "z3", row_scaled, "L2b"),
                  (t_k, D, "qkv", logit_made, "L3"), (t_v, D, "qkv", step_summed, "L3")]
        SUM_PASS = {"L0": 0, "L1": 2, "L2a": 4, "L2b": 6, "L3": 8}
        LOGIT_PASS = {"L1": 1, "L2a": 3, "L2b": 5, "L3": 7}
        def landed(eng, g, it, j):
            eng.wait_ge(row_landed[j].sem, 16 * (ITERS * g + 1) + 16 * it)

        block = ctx.enter_context(nc.Block())

        @block.gpsimd
        def _(pool):
            for t, pattern, base, mult in (
                    (iota[:], [[1, P]], 0, 0), (stepno, [[1, STEPS]], 0, 0), (tileno[:], [[1, G + 1]], 0, G),
                    (part[:, 0:1], [[0, 1]], 0, 1), (part[:, 1:2], [[0, 1]], 1, 1), (part[:, 2:3], [[0, 1]], -1, 1)):
                nc.gpsimd.iota(t, pattern, base=base, channel_multiplier=mult,
                               allow_small_or_imprecise_dtypes=True).then_inc(consts_made.sem, 1)
            def stage_input(loop, buf, ready, cols=D):
                def body(it):
                    for v in range(V):
                        b = V * it + v
                        ready(b)
                        if due(b - V + 1):
                            pool.wait_ge(in_turned.sem, in_turned.at(loop, b - V + 1))
                        nc.gpsimd.tensor_copy(rows[:, v, 0:cols], at_block(buf, b)[:, 0:cols])\
                            .then_inc(input_staged.sem, 1)
                each(pool, VITERS, body)

            def gather(g):
                table, width, writer, used, stage = PASSES[g]
                if writer:
                    for v in range(V):
                        pool.wait_ge(table_stored[v].sem, table_stored[v].at(writer, 32 * VITERS))

                def body(it):
                    for j in range(U):
                        if j % HALF == 0:
                            if not is_first(it):
                                pool.wait_ge(used.sem, used.at(stage, U * it - U + j + HALF))
                            elif g:
                                _, _, _, before, before_stage = PASSES[g - 1]
                                pool.wait_ge(before.sem, before.at(before_stage, STEPS - U + j + HALF))
                            pool.wait_ge(indices_put.sem, 2 * ITERS * g + j // HALF + 1 + 2 * it)
                            pool.sem_inc(half_opened.sem, 1)
                        pool.indirect_dma_start(
                            out=rows[:, j, 0:width], out_offset=None, in_=table[:, :],
                            in_offset=bass.IndirectOffsetOnAxis(
                                ap=idx[:, j // HALF, j % HALF:j % HALF + 1], axis=0)).then_inc(row_landed[j].sem, 16)
                each(pool, ITERS, body)

            gather(0)
            stage_input("mlp", ACC, lambda b: pool.wait_ge(input_made.sem, input_made.at("mlp", b + 1)))
            stage_input("z1", X, lambda b: pool.wait_ge(normed.sem, normed.at("mlp", b + 1)))
            gather(1)
            gather(2)
            stage_input("z2", X, lambda b: pool.wait_ge(normed.sem, normed.at("gat", b + 1)))
            gather(3)
            gather(4)
            stage_input("z3", Y, lambda b: pool.wait_ge(combined_v.sem, combined_v.at("L2a", COMBINED["L2a"])))
            gather(5)
            gather(6)
            stage_input("wf", Y, lambda b: pool.wait_ge(combined_v.sem, combined_v.at("L2b", COMBINED["L2b"])), P)
            stage_input("qkv", X, lambda b: pool.wait_ge(normed.sem, normed.at("wf", b + 1)))
            gather(7)
            gather(8)
            stage_input("ws", X, lambda b: pool.wait_ge(combined_v.sem, combined_v.at("L3", COMBINED["L3"])))
            stage_input("ffn", ACC, lambda b: pool.wait_ge(normed.sem, normed.at("ws", 2 * BLOCKS + b + 1)))

        @block.sync
        def _(sp):
            sp.wait_ge(edges_padded.sem, edges_padded.at("setup", 1))
            for tile, vec in ((dstI, dst), (srcI, src), (wT, edge_weight)):
                sp.dma_start(tile[0:EFULL, :], vec[0:EFULL * ROW].rearrange("(p j) -> p j", j=ROW))\
                    .then_inc(edges_in.sem, 16)
                sp.dma_start(tile[EFULL:EFULL + 1, 0:EREST],
                             vec[EFULL * ROW:E].rearrange("(o j) -> o j", o=1)).then_inc(edges_in.sem, 16)
            sp.dma_start(nextI[0:EFULL - 1, :], dst[ROW:EFULL * ROW].rearrange("(p j) -> p j", j=ROW)[:, 0:1],
                         allow_slow_non_contiguous=True).then_inc(edges_in.sem, 16)
            sp.dma_start(nextI[EFULL - 1:EFULL, :], dst[EFULL * ROW:EFULL * ROW + 1].rearrange("(o j) -> o j", o=1))\
                .then_inc(edges_in.sem, 16)
            sp.dma_start(X[:, 0:FULL, :], x[0:FULL * P, :].rearrange("(b p) d -> p b d", p=P))\
                .then_inc(features_in.sem, 16)
            sp.dma_start(X[0:REST, FULL, :], x[FULL * P:N, :]).then_inc(features_in.sem, 16)

            for tile, source in weight_loads:
                sp.dma_start(tile, source, allow_slow_non_contiguous=True).then_inc(weights_in.sem, 16)

            def store(loop, parts, copies):
                def body(it):
                    for v in range(V):
                        sp.wait_ge(product_copied.sem, product_copied.at(loop, copies * (V * it + v + 1)))
                        for table, slot in parts:
                            sp.dma_start(table[bass.ds((V * it + v) * P, P), :], slot(v))\
                                .then_inc(table_stored[v].sem, 16)
                each(sp, VITERS, body)

            store("z1", [(t_z1, lambda v: zrow[:, v, 0:D]), (t_s1, lambda v: zrow[:, v, D:D + HEADS])], 1)
            store("z2", [(t_z2, lambda v: zrow[:, v, 0:D]), (t_s2, lambda v: zrow[:, v, D:D + HEADS])], 2)
            store("z3", [(t_z3, lambda v: zrow[:, v, 0:HID]), (t_s3, lambda v: zrow[:, v, HID:HID + 1])], 2)
            store("qkv", [(t_k, lambda v: zrow[:, v, 0:D]), (t_v, lambda v: hidT[:, v, 0:KC, :].rearrange("p m n -> p (m n)"))], 3)

            sp.wait_ge(normed.sem, normed.at("last", BLOCKS))
            sp.dma_start(out[0:FULL * P, :].rearrange("(b p) d -> p b d", p=P), X[:, 0:FULL, :])\
                .then_inc(out_stored.sem, 16)
            sp.dma_start(out[FULL * P:N, :], X[0:REST, FULL, :]).then_inc(out_stored.sem, 16)
            sp.wait_ge(out_stored.sem, 32)

        @block.vector
        def _(dve):
            vec = nc.vector
            done = [0]

            def step(instruction):
                done[0] += 1
                instruction.then_inc(setup_v.sem, 1)
                return done[0]

            def settled():
                dve.wait_ge(setup_v.sem, done[0])

            vec.memset(dstI, int(NODST))
            vec.memset(srcI, 0)
            vec.memset(wT, 0.0)
            vec.memset(X[:, FULL, :], 0.0)
            vec.memset(nextI[:], int(NODST)).then_inc(edges_padded.sem, 1)
            step(vec.memset(rows[:, :, D:D + 1], 1.0))
            step(vec.memset(ones[:], 1.0))
            step(vec.memset(carryF[:], -BIG))
            step(vec.memset(carryB[:], -BIG))
            dve.wait_ge(consts_made.sem, consts_made.at("setup", 6))
            step(vec.tensor_scalar(ident[:], iota[:], part[:, 0:1], None, ALU.is_equal))
            step(vec.tensor_scalar(up[:], iota[:], part[:, 1:2], None, ALU.is_equal))
            step(vec.tensor_scalar(down[:], iota[:], part[:, 2:3], None, ALU.is_equal))

            dve.wait_ge(edges_in.sem, 16 * 8)
            step(vec.tensor_scalar(tileI[:, 0:G], dstI[:, ::P], BLOCK_SHIFT, None, ALU.arith_shift_right))
            step(vec.tensor_scalar(tileI[:, G:G + 1], nextI[:], BLOCK_SHIFT, None, ALU.arith_shift_right))
            settled()
            step(vec.tensor_tensor(tileC[:], tileI[:], tileno[:], ALU.add))
            settled()
            step(vec.memset(tileC[0:1, 0:1], 0.0))
            settled()
            for g in range(G + 1):
                step(vec.tensor_scalar(step_ge[:, g, :], stepno[0:EP, :], tileC[:, g:g + 1], None, ALU.is_ge))
            settled()
            assert done[0] == STEP_GE_AT
            for g in range(G):
                step(vec.tensor_tensor(pick[:, g, :], step_ge[:, g, :], step_ge[:, g + 1, :], ALU.subtract))
            step(vec.tensor_copy(dstT, dstI))
            step(vec.tensor_copy(srcT, srcI))
            assert done[0] == EDGES_AT
            dve.wait_ge(setup_p.sem, 1)
            step(vec.scalar_tensor_tensor(stepB, PS[0][:, 0:STEPS], -1.0, stepno, ALU.mult, ALU.add))
            settled()
            step(vec.tensor_scalar(stepB, stepB, 1.0, None, ALU.add))
            settled()
            step(vec.tensor_scalar(blockI[:], stepB[0:1, :], float(BLOCKS - 1), None, ALU.min))
            dve.wait_ge(setup_p.sem, 2)
            step(vec.tensor_copy(srcK[:, 0:STEPS], PS[1][:, 0:STEPS]))
            step(vec.tensor_copy(srcK[:, STEPS:STEPS + U], PS[1][:, 0:U]))
            assert done[0] == SOURCES_AT
            step(vec.scalar_tensor_tensor(dloc[:], stepB, -float(P), PS[2][:, 0:STEPS], ALU.mult, ALU.add))
            settled()
            step(vec.tensor_copy(wK[:], PS[3][:, 0:STEPS]))
            step(vec.tensor_scalar(vtmp, dloc[:], 0.0, None, ALU.is_ge))
            settled()
            step(vec.scalar_tensor_tensor(valid[:], dloc[:], float(P), vtmp, ALU.is_lt, ALU.mult))
            settled()
            step(vec.tensor_tensor(vtmp, PS[2][:, 0:STEPS], valid[:], ALU.mult))
            settled()
            step(vec.scalar_tensor_tensor(dstM, valid[:], -1.0, vtmp, ALU.add, ALU.add))
            assert done[0] == DSTM_AT
            dve.wait_ge(setup_p.sem, 3)
            step(vec.tensor_copy(DT, PS[4][0:SPARTS, :]))
            assert done[0] == DT_AT
            settled()
            same = FT[:, 0, :]
            step(vec.tensor_tensor(same[:, 1:ROW], DT[:, 1:ROW], DT[:, 0:ROW - 1], ALU.is_equal))
            dve.wait_ge(setup_p.sem, 4)
            step(vec.tensor_tensor(same[:, 0:1], DT[:, 0:1], PS[5][0:SPARTS, 0:1], ALU.is_equal))
            settled()
            step(vec.memset(same[0:1, 0:1], 0.0))
            settled()
            step(vec.tensor_scalar(breakF[:], same, -1.0, BIG, ALU.add, ALU.mult))
            step(vec.tensor_scalar(first[:], same, -1.0, 1.0, ALU.mult, ALU.add))
            settled()
            assert done[0] == BREAK_AT
            step(vec.tensor_copy(breakB[:, 0:ROW - 1], breakF[:, 1:ROW]))
            dve.wait_ge(setup_p.sem, 5)
            step(vec.tensor_copy(breakB[:, ROW - 1:ROW], PS[5][0:SPARTS, 1:2]))
            settled()
            step(vec.tensor_reduce(brk1[:, 0:1], breakF[:], AX, ALU.add))
            step(vec.tensor_reduce(brk1[:, 1:2], breakB[:], AX, ALU.add))
            settled()
            for i in range(2):
                step(vec.tensor_copy(brk[:, i, :], brk1[:, i:i + 1].to_broadcast([SPARTS, HEADS])))
            assert done[0] == SPAN_AT
            dve.wait_ge(setup_p.sem, 6)
            step(vec.tensor_copy(spanF[:], PS[6][0:HEADS, 0:SPARTS]))
            step(vec.tensor_copy(spanB[:], PS[6][0:HEADS, SPARTS:2 * SPARTS]))
            dve.wait_ge(weights_in.sem, 16 * len(weight_loads))
            for wz, a0 in ((wz1, 0), (wz2, 2)):
                for which in range(2):
                    settled()
                    for k in range(KC):
                        step(vec.tensor_tensor(junk[:, k, :], wz[:, k, 0:D], att[:, a0 + which, :], ALU.mult))
                    settled()
                    for k in range(KC):
                        step(vec.tensor_reduce(wz[:, k, D + which * HEADS:D + (which + 1) * HEADS],
                                               junk[:, k, :].rearrange("p (h f) -> p h f", h=HEADS), AX, ALU.add))
            for which in range(2):
                settled()
                for k in range(KC):
                    step(vec.tensor_tensor(junk[:, k, 0:HID], wz3[:, k, 0:HID], att2[:, which, :], ALU.mult))
                settled()
                for k in range(KC):
                    step(vec.tensor_reduce(wz3[:, k, HID + which:HID + which + 1], junk[:, k, 0:HID], AX, ALU.add))
            step(vec.tensor_scalar(maskneg[:], valid[:], -1.0, BIG, ALU.add, ALU.mult))
            step(vec.tensor_scalar(onePeps[:], scal[:, 0:1], 1.0, None, ALU.add))
            settled()
            assert done[0] == SETUP_V

            def sum_edges(stage):
                width = WIDTH[stage]
                scaled = stage in SCALED
                heads = HEADS_OF.get(stage, 1)
                cols = width + EXTRAS.get(stage, 0)
                g = SUM_PASS[stage]
                vec.memset(ACC[:], 0.0).then_inc(sums_zeroed.sem, 1)

                def prepare(it, j):
                    k = U * it + j
                    col = bass.ds(k, 1)
                    if due(k - 3):
                        dve.wait_ge(step_summed.sem, step_summed.at(stage, k - 3))
                    if scaled:
                        vec.tensor_scalar(M[:, j % 4, :], iota[:], dloc[:, col], None, ALU.is_equal)\
                            .then_inc(onehot_made.sem, 1)
                        landed(dve, g, it, j)
                        vec.tensor_tensor(
                            R[:, j % 4, 0:width].rearrange("p (h f) -> p h f", h=heads),
                            rows[:, j, 0:width].rearrange("p (h f) -> p h f", h=heads),
                            PX[:, col, 0:heads].rearrange("p o h -> p (o h)").unsqueeze(2).to_broadcast([P, heads, width // heads]),
                            ALU.mult).then_inc(row_scaled.sem, 1)
                    else:
                        w = wK[:, col] if stage == "L0" else PX[:, col, 0]
                        vec.tensor_scalar(M[:, j % 4, :], iota[:], dloc[:, col], w, ALU.is_equal, ALU.mult)\
                            .then_inc(onehot_made.sem, 1)

                def add(k, j, b):
                    dve.wait_ge(step_summed.sem, step_summed.at(stage, k + 1))
                    if due(k):
                        dve.wait_ge(sum_added.sem, sum_added.at(stage, k))
                    a = ACC[:, bass.ds(b, 1), 0:cols].rearrange("p o c -> p (o c)")
                    vec.tensor_tensor(a, a, PS[j % 4][:, 0:cols], ALU.add).then_inc(sum_added.sem, 1)

                prepare(0, 0)
                dve.wait_ge(sums_zeroed.sem, sums_zeroed.at(stage, 1))

                def body(it):
                    blocks = load_blocks(dve, it)
                    for j in range(U):
                        if j < U - 1:
                            prepare(it, j + 1)
                        elif not is_last(it, ITERS):
                            prepare(it + 1, 0)
                        add(U * it + j, j, blocks[j])
                each(dve, ITERS, body)

            def logits(stage):
                g = LOGIT_PASS[stage]
                heads = HEADS_OF[stage]

                def mask(it, j):
                    k = U * it + j
                    col = bass.ds(k, 1)
                    if due(k - 3):
                        dve.wait_ge(mask_turned.sem, mask_turned.at(stage, k - 3))
                    vec.tensor_scalar(M[:, j % 4, :], iota[:], dloc[:, col], None, ALU.is_equal)\
                        .then_inc(mask_made.sem, 1)

                def body(it):
                    for j in range(U):
                        k = U * it + j
                        col = bass.ds(k, 1)
                        if j < U - 2:
                            mask(it, j + 2)
                        elif not is_last(it, ITERS):
                            mask(it + 1, j + 2 - U)
                        dve.wait_ge(dst_spread.sem, dst_spread.at(stage, k + 1))
                        landed(dve, g, it, j)
                        spread = PS[4 + j % 4]
                        if stage == "L3":
                            if due(k - 1):
                                dve.wait_ge(logit_made.sem, logit_made.at(stage, k - 1))
                            vec.scalar_tensor_tensor(junk[:, j % 2, :], spread[:, 0:D], float(D) ** -0.5,
                                                     rows[:, j, 0:D], ALU.mult, ALU.mult,
                                                     accum_out=LG[:, col, 0]).then_inc(logit_made.sem, 1)
                        else:
                            vec.tensor_tensor(LG[:, col, 0:heads].rearrange("p o h -> p (o h)"),
                                              spread[:, 0:heads], rows[:, j, 0:heads], ALU.add)\
                                .then_inc(logit_made.sem, 1)
                mask(0, 0)
                mask(0, 1)
                each(dve, ITERS, body)

            def softmax(stage):
                heads = HEADS_OF[stage]
                n = [0]

                def step(instruction):
                    n[0] += 1
                    instruction.then_inc(softmax_v.sem, 1)

                def settled():
                    dve.wait_ge(softmax_v.sem, softmax_v.at(stage, n[0]))

                L = LG[:, :, 0:heads]
                vb = valid[:].unsqueeze(2).to_broadcast([P, STEPS, heads])
                dve.wait_ge(logit_made.sem, logit_made.at(stage, STEPS))
                if stage == "L3":
                    step(vec.scalar_tensor_tensor(LG[:, :, 0], wK[:], scal[:, 1:2], LG[:, :, 0], ALU.mult, ALU.add))
                    settled()
                    step(vec.tensor_scalar(LG[:, :, 0], LG[:, :, 0], scal[:, 2:3], None, ALU.add))
                    settled()
                else:
                    step(vec.scalar_tensor_tensor(L, L, SLOPE[stage], L, ALU.mult, ALU.max))
                    settled()
                if stage == "L1":
                    z = PX[:, :, 0:heads]
                    step(vec.tensor_scalar(z, L, 0.0, -1000.0, ALU.is_equal, ALU.mult))
                    settled()
                    step(vec.tensor_tensor(L, L, z, ALU.add))
                    settled()
                step(vec.tensor_tensor(L, L, vb, ALU.mult))
                settled()
                step(vec.tensor_tensor(L, L, maskneg[:].unsqueeze(2).to_broadcast([P, STEPS, heads]), ALU.add))
                assert n[0] == LOGITS_AT[stage]
                dve.wait_ge(softmax_a.sem, softmax_a.at(stage, 1))
                for h in range(heads):
                    step(vec.tensor_tensor_scan(FT[:, h, :], breakF[:], LT[:, h, :], -BIG, ALU.add, ALU.max))
                assert n[0] == LOGITS_AT[stage] + heads
                dve.wait_ge(softmax_p.sem, softmax_p.at(stage, 2))
                settled()
                step(vec.tensor_tensor_scan(carryF[0:heads, 1:SPARTS + 1], spanF[0:heads, :], PS[4][0:heads, 0:SPARTS],
                                            -BIG, ALU.add, ALU.max))
                dve.wait_ge(softmax_p.sem, softmax_p.at(stage, 3))
                step(vec.tensor_copy(startF[:, 0:heads], PS[5][0:SPARTS, 0:heads]))
                settled()
                for h in range(heads):
                    step(vec.tensor_tensor_scan(FT[:, h, :], breakF[:], LT[:, h, :], startF[:, h:h + 1],
                                                ALU.add, ALU.max))
                settled()
                for h in range(heads):
                    step(vec.tensor_tensor_scan(BT[:, h, ::-1], breakB[:, ::-1], FT[:, h, ::-1], -BIG,
                                                ALU.add, ALU.max))
                dve.wait_ge(softmax_p.sem, softmax_p.at(stage, 4))
                settled()
                step(vec.tensor_tensor_scan(carryB[0:heads, SPARTS - 1::-1], spanB[0:heads, ::-1],
                                            PS[6][0:heads, SPARTS - 1::-1], -BIG, ALU.add, ALU.max))
                dve.wait_ge(softmax_p.sem, softmax_p.at(stage, 5))
                step(vec.tensor_copy(startB[:, 0:heads], PS[7][0:SPARTS, 0:heads]))
                settled()
                for h in range(heads):
                    step(vec.tensor_tensor_scan(BT[:, h, ::-1], breakB[:, ::-1], FT[:, h, ::-1],
                                                startB[:, h:h + 1], ALU.add, ALU.max))
                settled()
                step(vec.tensor_tensor(LT[:, 0:heads, :], LT[:, 0:heads, :], BT[:, 0:heads, :], ALU.subtract))
                assert n[0] == SHIFTED_AT[stage]
                if stage in ("L2a", "L2b"):
                    step(vec.tensor_tensor(FT[:, 0:heads, :], BT[:, 0:heads, :],
                                           first[:].unsqueeze(1).to_broadcast([SPARTS, heads, ROW]), ALU.mult))
                    assert n[0] == MAXIMA_AT[stage]
                dve.wait_ge(softmax_a.sem, softmax_a.at(stage, 2 + len(back_columns(stage))))

            def combine(stage):
                heads = HEADS_OF[stage]
                width = WIDTH[stage] - (stage == "L3")
                n = [0]

                def step(instruction):
                    n[0] += 1
                    instruction.then_inc(combined_v.sem, 1)

                def settled():
                    dve.wait_ge(combined_v.sem, combined_v.at(stage, n[0]))

                dve.wait_ge(sum_added.sem, sum_added.at(stage, STEPS))
                if stage in ("L1", "L3"):
                    den = ACC[:, :, D:D + heads]
                    step(vec.tensor_scalar(nodeA[:, :, 0:heads], den, 1e-12, None, ALU.max))
                    settled()
                    step(vec.reciprocal(nodeA[:, :, 0:heads], nodeA[:, :, 0:heads]))
                    settled()
                    for h in range(heads):
                        f = D // heads
                        a = ACC[:, :, h * f:(h + 1) * f]
                        step(vec.tensor_tensor(a, a, nodeA[:, :, h:h + 1].to_broadcast([P, BLOCKS, f]), ALU.mult))
                    settled()
                    if stage == "L1":
                        step(vec.tensor_tensor(X[:], X[:], ACC[:, :, 0:D], ALU.add))
                    else:
                        step(vec.tensor_tensor(ACC[:, :, 0:D], X[:], ACC[:, :, 0:D], ALU.add))
                    settled()
                    assert n[0] == COMBINED[stage]
                    return
                den = ACC[:, :, width:width + heads]
                top = ACC[:, :, width + heads:width + 2 * heads]
                has = ACC[:, :, width + 2 * heads:width + 2 * heads + 1].to_broadcast([P, BLOCKS, heads])
                A, B, C = (t[:, :, 0:heads] for t in (nodeA, nodeB, nodeC))
                step(vec.tensor_scalar(A, has, -1.0, BIG, ALU.add, ALU.mult))
                step(vec.tensor_tensor(B, tab[:, :, 0:heads], tab[:, :, heads:2 * heads], ALU.add))
                settled()
                step(vec.tensor_tensor(A, A, top, ALU.add))
                step(vec.scalar_tensor_tensor(B, B, SLOPE[stage], B, ALU.mult, ALU.max))
                settled()
                step(vec.tensor_tensor(C, A, B, ALU.max))
                settled()
                step(vec.tensor_tensor(A, A, C, ALU.subtract))
                step(vec.tensor_tensor(B, B, C, ALU.subtract))
                assert n[0] == 7
                dve.wait_ge(combined_a.sem, combined_a.at(stage, 2))
                step(vec.tensor_tensor(C, den, A, ALU.mult))
                settled()
                step(vec.tensor_tensor(C, C, B, ALU.add))
                settled()
                step(vec.reciprocal(C, C))
                settled()
                step(vec.tensor_tensor(A, A, C, ALU.mult))
                step(vec.tensor_tensor(B, B, C, ALU.mult))
                settled()
                f = width // heads
                for h in range(heads):
                    a, y = ACC[:, :, h * f:(h + 1) * f], Y[:, :, h * f:(h + 1) * f]
                    step(vec.tensor_tensor(a, a, A[:, :, h:h + 1].to_broadcast([P, BLOCKS, f]), ALU.mult))
                    step(vec.tensor_tensor(y, y, B[:, :, h:h + 1].to_broadcast([P, BLOCKS, f]), ALU.mult))
                settled()
                y, a = Y[:, :, 0:width], ACC[:, :, 0:width]
                step(vec.tensor_tensor(y, y, a, ALU.add))
                settled()
                bv = bias["b3" if stage == "L2a" else "b4"][:].unsqueeze(1).to_broadcast([P, BLOCKS, width])
                step(vec.tensor_tensor(y, y, bv, ALU.add))
                settled()
                if stage == "L2a":
                    step(vec.tensor_scalar(y, y, 0.0, None, ALU.max))
                    settled()
                assert n[0] == COMBINED[stage]

            def norm(stage, buf, gain=None, shift=None):
                def stats(it):
                    for v in range(V):
                        b = V * it + v
                        vec.bn_stats(at_block(stat, b), at_block(buf, b)).then_inc(stats_made.sem, 1)
                each(dve, VITERS, stats)
                dve.wait_ge(stats_made.sem, stats_made.at(stage, BLOCKS))
                n = [0]

                def step(instruction):
                    n[0] += 1
                    instruction.then_inc(norm_step.sem, 1)

                def settled():
                    dve.wait_ge(norm_step.sem, norm_step.at(stage, n[0]))
                mean_e, sq_e, mean_o, sq_o = (stat[:, :, c] for c in (1, 2, 4, 5))
                step(vec.tensor_tensor(mean[:], mean_e, mean_o, ALU.add))
                step(vec.tensor_tensor(root[:], mean_e, mean_o, ALU.subtract))
                step(vec.tensor_tensor(rstd[:], sq_e, sq_o, ALU.add))
                settled()
                step(vec.tensor_scalar(mean[:], mean[:], 0.5, None, ALU.mult))
                step(vec.scalar_tensor_tensor(root[:], root[:], 0.25, root[:], ALU.mult, ALU.mult))
                step(vec.tensor_scalar(rstd[:], rstd[:], 1.0 / D, EPS, ALU.mult, ALU.add))
                settled()
                step(vec.tensor_tensor(rstd[:], rstd[:], root[:], ALU.add))
                assert n[0] == VARIANCE_AT
                dve.wait_ge(norm_root.sem, norm_root.at(stage, 1))
                step(vec.reciprocal(rstd[:], root[:]))
                settled()

                def apply(it):
                    for v in range(V):
                        b = V * it + v
                        vec.tensor_scalar(at_block(buf, b), at_block(buf, b), mean[:, bass.ds(b, 1)],
                                          rstd[:, bass.ds(b, 1)], ALU.subtract, ALU.mult).then_inc(normed.sem, 1)
                each(dve, VITERS, apply)
                if gain is not None:
                    for i, (op, w) in enumerate(((ALU.mult, gain), (ALU.add, shift))):
                        def apply(it):
                            for v in range(V):
                                b = V * it + v
                                dve.wait_ge(normed.sem, normed.at(stage, BLOCKS * i + b + 1))
                                vec.tensor_tensor(at_block(buf, b), at_block(buf, b), w[:], op)\
                                    .then_inc(normed.sem, 1)
                        each(dve, VITERS, apply)

            def residual(loop, terms, buf):
                nt = len(terms)

                def body(it):
                    for v in range(V):
                        b = V * it + v
                        dve.wait_ge(product_made.sem, product_made.at(loop, b + 1))
                        for i, t in enumerate(terms):
                            if i:
                                dve.wait_ge(product_added.sem, product_added.at(loop, nt * b + i))
                            other = t(b)
                            first_in = PS[4 + BANK[v]][:, 0:D] if i == 0 else at_block(buf, b)
                            ins = vec.tensor_tensor(at_block(buf, b), first_in, other, ALU.add)
                            ins.then_inc(product_added.sem, 1)
                each(dve, VITERS, body)
                dve.wait_ge(product_added.sem, product_added.at(loop, nt * BLOCKS))

            sum_edges("L0")
            dve.wait_ge(sum_added.sem, sum_added.at("L0", STEPS))
            dve.wait_ge(features_in.sem, 32)

            def scale_input(it):
                for v in range(V):
                    b = V * it + v
                    vec.scalar_tensor_tensor(at_block(ACC, b)[:, 0:D], at_block(X, b), onePeps[:],
                                             at_block(ACC, b)[:, 0:D], ALU.mult, ALU.add)\
                        .then_inc(input_made.sem, 1)
            each(dve, VITERS, scale_input)
            residual("mlp", [lambda b: at_block(X, b), lambda b: bias["b2"][:]], X)
            norm("mlp", X)
            logits("L1")
            softmax("L1")
            sum_edges("L1")
            combine("L1")
            norm("gat", X)
            logits("L2a")
            softmax("L2a")
            sum_edges("L2a")
            combine("L2a")
            logits("L2b")
            softmax("L2b")
            sum_edges("L2b")
            combine("L2b")
            residual("wf", [lambda b: at_block(X, b), lambda b: bias["bf"][:]], X)
            norm("wf", X)

            def project(it):
                for v in range(V):
                    b = V * it + v
                    for i, (w, o) in enumerate((("bq", at_block(Y, b)), ("bk", zrow[:, v, 0:D]),
                                                ("bv", hidT[:, v, 0:KC, :].rearrange("p m n -> p (m n)")))):
                        dve.wait_ge(product_made.sem, product_made.at("qkv", 3 * b + i + 1))
                        if not is_first(it) and i:
                            dve.wait_ge(table_stored[v].sem, table_stored[v].at("qkv", 32 * it))
                        vec.tensor_tensor(o, PS[4 + i][:, 0:D], bias[w][:], ALU.add)\
                            .then_inc(product_copied.sem, 1)
            each(dve, VITERS, project)
            logits("L3")
            softmax("L3")
            sum_edges("L3")
            combine("L3")
            residual("ws", [lambda b: at_block(ACC, b)[:, 0:D], lambda b: bias["bs"][:]], ACC3)
            norm("ws", ACC3, bias["g1"], bias["h1"])
            residual("ffn", [lambda b: at_block(ACC3, b), lambda b: bias["bff2"][:]], ACC3)
            norm("ffn", ACC3, bias["g2"], bias["h2"])
            dve.wait_ge(normed.sem, normed.at("ffn", 3 * BLOCKS))
            vec.tensor_tensor(X[:], X[:], ACC3, ALU.add).then_inc(residual_added.sem, 1)
            dve.wait_ge(residual_added.sem, residual_added.at("last", 1))
            norm("last", X)

        @block.tensor
        def _(pe):
            mm = nc.tensor.matmul
            pe.wait_ge(setup_v.sem, STEP_GE_AT)
            for g in range(G):
                last = mm(PS[0][:, 0:STEPS], ones[0:EP, :], step_ge[:, g, :], start=g == 0, stop=g == G - 1)
            last.then_inc(setup_p.sem, 1)
            pe.wait_ge(setup_v.sem, EDGES_AT)
            for i, t in enumerate((srcT, dstT, wT)):
                for g in range(G):
                    last = mm(PS[1 + i][:, 0:STEPS], t[:, g * P:(g + 1) * P], pick[:, g, :],
                              start=g == 0, stop=g == G - 1)
            last.then_inc(setup_p.sem, 1)
            pe.wait_ge(setup_v.sem, DSTM_AT)
            for g in range(G):
                last = nc.tensor.transpose(PS[4][0:SPARTS, g * P:(g + 1) * P], dstM[:, g::G], ident[:])
            last.then_inc(setup_p.sem, 1)
            pe.wait_ge(setup_v.sem, DT_AT)
            mm(PS[5][0:SPARTS, 0:1], up[0:SPARTS, 0:SPARTS], DT[:, ROW - 1:ROW], start=True, stop=True)\
                .then_inc(setup_p.sem, 1)
            pe.wait_ge(setup_v.sem, BREAK_AT)
            mm(PS[5][0:SPARTS, 1:2], down[0:SPARTS, 0:SPARTS], breakF[:, 0:1], start=True, stop=True)\
                .then_inc(setup_p.sem, 1)
            pe.wait_ge(setup_v.sem, SPAN_AT)
            for i in range(2):
                last = mm(PS[6][0:HEADS, i * SPARTS:(i + 1) * SPARTS], brk[:, i, :], ident[0:SPARTS, 0:SPARTS],
                          start=True, stop=True)
            last.then_inc(setup_p.sem, 1)
            pe.wait_ge(setup_v.sem, SETUP_V)

            def sum_edges(stage):
                g = SUM_PASS[stage]
                cols = WIDTH[stage] + EXTRAS.get(stage, 0)

                def body(it):
                    for j in range(U):
                        k = U * it + j
                        pe.wait_ge(onehot_made.sem, onehot_made.at(stage, k + 1))
                        if stage in SCALED:
                            pe.wait_ge(row_scaled.sem, row_scaled.at(stage, k + 1))
                            pe.wait_ge(extras_put.sem, extras_put.at(stage, k + 1))
                            moving = R[:, j % 4, 0:cols]
                        else:
                            landed(pe, g, it, j)
                            moving = rows[:, j, 0:cols]
                        if due(k - 3):
                            pe.wait_ge(sum_added.sem, sum_added.at(stage, k - 3))
                        mm(PS[j % 4][:, 0:cols], M[:, j % 4, :], moving, start=True, stop=True)\
                            .then_inc(step_summed.sem, 1)
                each(pe, ITERS, body)

            def logits(stage):
                heads = HEADS_OF[stage]

                def turn(k, j):
                    pe.wait_ge(mask_made.sem, mask_made.at(stage, k + 1))
                    if due(k - 1):
                        pe.wait_ge(mask_copied.sem, mask_copied.at(stage, k - 1))
                    nc.tensor.transpose(PS[j % 2][:, 0:P], M[:, j % 4, :], ident[:]).then_inc(mask_turned.sem, 1)

                def body(it):
                    blocks = load_blocks(pe, it)
                    for j in range(U):
                        k = U * it + j
                        if j < U - 1:
                            turn(k + 1, j + 1)
                        elif not is_last(it, ITERS):
                            turn(k + 1, 0)
                        pe.wait_ge(mask_copied.sem, mask_copied.at(stage, k + 1))
                        if due(k - 3):
                            pe.wait_ge(logit_made.sem, logit_made.at(stage, k - 3))
                        if stage == "L3":
                            values, n = Y[:, bass.ds(blocks[j], 1), :], D
                        else:
                            values, n = tab[:, bass.ds(blocks[j], 1), heads:2 * heads], heads
                        mm(PS[4 + j % 4][:, 0:n], MT[:, j % 2, :], values.rearrange("p o c -> p (o c)"),
                           start=True, stop=True).then_inc(dst_spread.sem, 1)
                turn(0, 0)
                each(pe, ITERS, body)

            def softmax(stage):
                heads = HEADS_OF[stage]
                pe.wait_ge(softmax_v.sem, softmax_v.at(stage, LOGITS_AT[stage]))
                for h in range(heads):
                    for g in range(G):
                        last = nc.tensor.transpose(PS[h][0:SPARTS, g * P:(g + 1) * P], LG[:, g::G, h], ident[:])
                last.then_inc(softmax_p.sem, 1)
                pe.wait_ge(softmax_v.sem, softmax_v.at(stage, LOGITS_AT[stage] + heads))
                nc.tensor.transpose(PS[4][0:heads, 0:SPARTS], FT[:, 0:heads, ROW - 1], ident[0:SPARTS, 0:SPARTS])\
                    .then_inc(softmax_p.sem, 1)
                pe.wait_ge(softmax_v.sem, softmax_v.at(stage, LOGITS_AT[stage] + heads + 1))
                nc.tensor.transpose(PS[5][0:SPARTS, 0:heads], carryF[0:heads, 0:SPARTS], ident[0:heads, 0:heads])\
                    .then_inc(softmax_p.sem, 1)
                pe.wait_ge(softmax_v.sem, softmax_v.at(stage, LOGITS_AT[stage] + 3 * heads + 2))
                nc.tensor.transpose(PS[6][0:heads, 0:SPARTS], BT[:, 0:heads, 0], ident[0:SPARTS, 0:SPARTS])\
                    .then_inc(softmax_p.sem, 1)
                pe.wait_ge(softmax_v.sem, softmax_v.at(stage, LOGITS_AT[stage] + 3 * heads + 3))
                nc.tensor.transpose(PS[7][0:SPARTS, 0:heads], carryB[0:heads, 1:SPARTS + 1], ident[0:heads, 0:heads])\
                    .then_inc(softmax_p.sem, 1)
                pe.wait_ge(softmax_a.sem, softmax_a.at(stage, 2))
                for c, source in enumerate(back_columns(stage)):
                    if c >= 4:
                        if due(3 + c - 4):
                            pe.wait_ge(softmax_a.sem, softmax_a.at(stage, 3 + c - 4))
                    if stage in MAXIMA_AT and c == heads:
                        pe.wait_ge(softmax_v.sem, softmax_v.at(stage, MAXIMA_AT[stage]))
                    for g in range(G):
                        last = nc.tensor.transpose(PS[c % 4][:, g * SPARTS:(g + 1) * SPARTS],
                                                   source[:, g * P:(g + 1) * P], ident[0:SPARTS, 0:SPARTS])
                    last.then_inc(softmax_p.sem, 1)

            def turn_in(loop, chunks=KC):
                def turn(b, v):
                    pe.wait_ge(input_staged.sem, input_staged.at(loop, b + 1))
                    if due(b - 1 if v else b):
                        pe.wait_ge(in_copied.sem, in_copied.at(loop, b - 1 if v else b))
                    for k in range(chunks):
                        last = nc.tensor.transpose(PS[v % 2][:, k * P:(k + 1) * P], rows[:, v, k * P:(k + 1) * P], ident[:])
                    last.then_inc(in_turned.sem, 1)
                return turn

            def product(loop, turn, use):
                def body(it):
                    for v in range(V):
                        b = V * it + v
                        if v < V - 1:
                            turn(b + 1, v + 1)
                        elif not is_last(it, VITERS):
                            turn(b + 1, 0)
                        pe.wait_ge(in_copied.sem, in_copied.at(loop, b + 1))
                        use(b, v)
                turn(0, 0)
                each(pe, VITERS, body)

            def linear(loop, weights, cols, chunks, taken, width=P):
                nw = len(weights)

                def use(b, v):
                    for i, w in enumerate(weights):
                        slot = BANK[v] if nw == 1 else i
                        taken(b, v, i)
                        for k in range(chunks):
                            last = mm(PS[4 + slot][:, 0:cols], inT[0:width, v, k, :], w[:, k, 0:cols] if width == P else w,
                                      start=k == 0, stop=k == chunks - 1)
                        last.then_inc(product_made.sem, 1)
                return use

            def hidden(loop, first_w, second_w, mids, taken):
                def use(b, v):
                    if due(b):
                        pe.wait_ge(hidden_acted.sem, hidden_acted.at(loop, b))
                    for m in range(mids):
                        for k in range(KC):
                            last = mm(PS[2][:, m * P:(m + 1) * P], first_w[:, k, m * P:(m + 1) * P],
                                      inT[:, v, k, :], start=k == 0, stop=k == KC - 1)
                    last.then_inc(hidden_made.sem, 1)
                    pe.wait_ge(hidden_acted.sem, hidden_acted.at(loop, b + 1))
                    taken(b, v, 0)
                    for m in range(mids):
                        last = mm(PS[4 + BANK[v]][:, 0:D], hidT[:, v, m, :], second_w[:, m, :],
                                  start=m == 0, stop=m == mids - 1)
                    last.then_inc(product_made.sem, 1)
                return use

            def copied(loop, per):
                return lambda b, v, i: due(per * (b - BANK_AGE[v] + 1)) and pe.wait_ge(product_copied.sem, product_copied.at(loop, per * (b - BANK_AGE[v] + 1)))

            def added(loop):
                return lambda b, v, i: due(2 * (b - BANK_AGE[v] + 1)) and pe.wait_ge(product_added.sem, product_added.at(loop, 2 * (b - BANK_AGE[v] + 1)))

            sum_edges("L0")
            product("mlp", turn_in("mlp"), hidden("mlp", w1, w2, KC, added("mlp")))
            product("z1", turn_in("z1"), linear("z1", [wz1], ZW, KC, copied("z1", 1)))
            pe.wait_ge(product_copied.sem, product_copied.at("z1", BLOCKS))
            logits("L1")
            softmax("L1")
            sum_edges("L1")
            product("z2", turn_in("z2"), linear("z2", [wz2], ZW, KC, copied("z2", 2)))
            pe.wait_ge(product_copied.sem, product_copied.at("z2", 2 * BLOCKS))
            logits("L2a")
            softmax("L2a")
            sum_edges("L2a")
            product("z3", turn_in("z3"), linear("z3", [wz3], HID + 2, KC, copied("z3", 2)))
            pe.wait_ge(product_copied.sem, product_copied.at("z3", 2 * BLOCKS))
            logits("L2b")
            softmax("L2b")
            sum_edges("L2b")
            product("wf", turn_in("wf", 1), linear("wf", [wf[:]], D, 1, added("wf"), width=HID))
            product("qkv", turn_in("qkv"), linear("qkv", [wq, wk, wv], D, KC,
                                                  lambda b, v, i: due(3 * b + i - 2) and pe.wait_ge(product_copied.sem, product_copied.at("qkv", 3 * b + i - 2))))
            pe.wait_ge(product_copied.sem, product_copied.at("qkv", 3 * BLOCKS))
            logits("L3")
            softmax("L3")
            sum_edges("L3")
            product("ws", turn_in("ws"), linear("ws", [ws], D, KC, added("ws")))
            product("ffn", turn_in("ffn"), hidden("ffn", wff1, wff2, FF // P, added("ffn")))

        @block.scalar
        def _(act):
            sc = nc.scalar

            def put_indices(k, half):
                cols = bass.ds(k, HALF)
                sc.activation(idx[:, half, :], srcK[:, cols], ACT.Copy).then_inc(indices_put.sem, 1)

            act.wait_ge(setup_v.sem, SOURCES_AT)
            put_indices(0, 0)
            put_indices(HALF, 1)

            def edge_loop(g, per_step):
                def body(it):
                    for j in range(U):
                        if per_step:
                            per_step(it, j)
                        if j % HALF == HALF - 1:
                            for i in range(j + 1 - HALF, j + 1):
                                landed(act, g, it, i)
                            put_indices(U * it + U + j + 1 - HALF, j // HALF)
                each(act, ITERS, body)

            def sum_edges(stage):
                if stage not in SCALED:
                    edge_loop(SUM_PASS[stage], None)
                    return
                width, extra = WIDTH[stage], EXTRAS[stage]

                def per_step(it, j):
                    k = U * it + j
                    col = bass.ds(k, 1)
                    if due(k - 3):
                        act.wait_ge(step_summed.sem, step_summed.at(stage, k - 3))
                    sc.activation(R[:, j % 4, width:width + extra], PX[:, col, 0:extra].rearrange("p o c -> p (o c)"),
                                  ACT.Copy).then_inc(extras_put.sem, 1)
                edge_loop(SUM_PASS[stage], per_step)

            def logits(stage):
                def per_step(it, j):
                    k = U * it + j
                    act.wait_ge(mask_turned.sem, mask_turned.at(stage, k + 1))
                    if due(k - 1):
                        act.wait_ge(dst_spread.sem, dst_spread.at(stage, k - 1))
                    sc.activation(MT[:, j % 2, :], PS[j % 2][:, 0:P], ACT.Copy).then_inc(mask_copied.sem, 1)
                edge_loop(LOGIT_PASS[stage], per_step)

            def softmax(stage):
                heads = HEADS_OF[stage]
                n = [0]

                def step(instruction):
                    n[0] += 1
                    instruction.then_inc(softmax_a.sem, 1)
                act.wait_ge(softmax_p.sem, softmax_p.at(stage, 1))
                for h in range(heads):
                    last = sc.activation(LT[:, h, :], PS[h][0:SPARTS, :], ACT.Copy)
                step(last)
                act.wait_ge(softmax_v.sem, softmax_v.at(stage, SHIFTED_AT[stage]))
                step(sc.activation(LT[:, 0:heads, :], LT[:, 0:heads, :], ACT.Exp))
                for c, _ in enumerate(back_columns(stage)):
                    act.wait_ge(softmax_p.sem, softmax_p.at(stage, 6 + c))
                    step(sc.activation(PX[:, :, c].rearrange("p (q g) -> p g q", g=G),
                                       PS[c % 4][:, 0:STEPS].rearrange("p (g q) -> p g q", g=G), ACT.Copy))
                act.wait_ge(softmax_a.sem, softmax_a.at(stage, n[0]))

            def copy_in(loop, chunks=KC, width=P):
                def copy(b, v):
                    act.wait_ge(in_turned.sem, in_turned.at(loop, b + 1))
                    if due((3 if loop == "qkv" else 1) * (b - V + 1)):
                        act.wait_ge(product_made.sem, product_made.at(loop, (3 if loop == "qkv" else 1) * (b - V + 1)))
                    sc.activation(inT[0:width, v, 0:chunks, :], PS[v % 2][0:width, 0:chunks * P].rearrange("p (k n) -> p k n", k=chunks),
                                  ACT.Copy).then_inc(in_copied.sem, 1)
                return copy

            def node_loop(copy, then=None):
                def body(it):
                    for v in range(V):
                        b = V * it + v
                        if v < V - 1:
                            copy(b + 1, v + 1)
                        elif not is_last(it, VITERS):
                            copy(b + 1, 0)
                        if then:
                            then(b, v, it)
                copy(0, 0)
                each(act, VITERS, body)

            def activate(loop, mids, func, biases):
                def then(b, v, it):
                    act.wait_ge(hidden_made.sem, hidden_made.at(loop, b + 1))
                    if due(b - V + 1):
                        act.wait_ge(product_made.sem, product_made.at(loop, b - V + 1))
                    for m in range(mids):
                        last = sc.activation(hidT[:, v, m, :], PS[2][:, m * P:(m + 1) * P], func, bias=biases[:, m:m + 1])
                    last.then_inc(hidden_acted.sem, 1)
                return then

            def copy_out(loop, cols, tabs, keep):
                def then(b, v, it):
                    act.wait_ge(product_made.sem, product_made.at(loop, b + 1))
                    if not is_first(it):
                        act.wait_ge(table_stored[v].sem, table_stored[v].at(loop, 32 * it))
                    bank = PS[4 + BANK[v]]
                    sc.activation(at_block(tab, b)[:, 0:cols - tabs], bank[:, tabs:cols], ACT.Copy)
                    ins = sc.activation(zrow[:, v, 0:cols], bank[:, 0:cols], ACT.Copy)
                    ins.then_inc(product_copied.sem, 1)
                    if keep:
                        sc.activation(at_block(Y, b)[:, 0:tabs], bank[:, 0:tabs], ACT.Copy).then_inc(product_copied.sem, 1)
                return then

            def combine(stage):
                heads = HEADS_OF[stage]
                act.wait_ge(combined_v.sem, combined_v.at(stage, 7))
                for t in (nodeA, nodeB):
                    sc.activation(t[:, :, 0:heads], t[:, :, 0:heads], ACT.Exp).then_inc(combined_a.sem, 1)

            def root_of(stage):
                act.wait_ge(norm_step.sem, norm_step.at(stage, VARIANCE_AT))
                sc.activation(root[:], rstd[:], ACT.Sqrt).then_inc(norm_root.sem, 1)

            edge_loop(0, None)
            act.wait_ge(weights_in.sem, 16 * len(weight_loads))
            node_loop(copy_in("mlp"), activate("mlp", KC, ACT.Relu, b1c))
            root_of("mlp")
            node_loop(copy_in("z1"), copy_out("z1", ZW, D, False))
            logits("L1")
            softmax("L1")
            sum_edges("L1")
            root_of("gat")
            node_loop(copy_in("z2"), copy_out("z2", ZW, D, True))
            logits("L2a")
            softmax("L2a")
            sum_edges("L2a")
            combine("L2a")
            node_loop(copy_in("z3"), copy_out("z3", HID + 2, HID, True))
            logits("L2b")
            softmax("L2b")
            sum_edges("L2b")
            combine("L2b")
            node_loop(copy_in("wf", 1, HID))
            root_of("wf")
            node_loop(copy_in("qkv"))
            logits("L3")
            softmax("L3")
            sum_edges("L3")
            node_loop(copy_in("ws"))
            root_of("ws")
            node_loop(copy_in("ffn"), activate("ffn", FF // P, ACT.Gelu_apprx_tanh, bff1c))
            root_of("ffn")
            root_of("last")


INPUTS = ["x", "src", "dst", "edge_weight", "L0_gnn_eps", "L0_gnn_w1", "L0_gnn_b1", "L0_gnn_w2", "L0_gnn_b2",
          "L1_gnn_W", "L1_gnn_att", "L2_gnn_W1", "L2_gnn_att_src1", "L2_gnn_att_dst1", "L2_gnn_b1", "L2_gnn_W2",
          "L2_gnn_att_src2", "L2_gnn_att_dst2", "L2_gnn_b2", "L2_gnn_Wf", "L2_gnn_bf", "L3_gnn_wq", "L3_gnn_bq",
          "L3_gnn_wk", "L3_gnn_bk", "L3_gnn_wv", "L3_gnn_bv", "L3_gnn_ws", "L3_gnn_bs", "L3_gnn_we", "L3_gnn_be",
          "L3_gnn_g1", "L3_gnn_b1", "L3_gnn_g2", "L3_gnn_b2", "L3_gnn_w_ff1", "L3_gnn_b_ff1", "L3_gnn_w_ff2",
          "L3_gnn_b_ff2"]


def kernel(**inputs):
    import concourse.bacc as bacc
    from concourse.bass_utils import run_bass_kernel_spmd

    nc = bacc.Bacc("TRN2", target_bir_lowering=False, num_devices=1)
    arrays, args = {}, []
    for name in INPUTS:
        a = np.ascontiguousarray(inputs[name])
        arrays["in_" + name] = a
        args.append(nc.dram_tensor("in_" + name, a.shape, mybir.dt.from_np(a.dtype), kind="ExternalInput").ap())
    args.append(nc.dram_tensor("result", (N, D), F32, kind="ExternalOutput").ap())
    build(nc, *args)
    ran = run_bass_kernel_spmd(nc, [arrays], core_ids=[0])
    return ran.results[0]["result"]
```

```python
from contextlib import ExitStack

import numpy as np

import concourse.bass as bass
from concourse import mybir

F32 = mybir.dt.float32
I32 = mybir.dt.int32
U8 = mybir.dt.uint8
ALU = mybir.AluOpType
ACT = mybir.ActivationFunctionType
AX = mybir.AxisListType.X
DVE_ENGINE = (mybir.EngineType.DVE,)
PE_ENGINE = (mybir.EngineType.PE,)

P = 128
N, E, D = 3125, 50000, 256
KC = D // P
BLOCKS = -(-N // P)
FULL = N // P
REST = N - FULL * P
TILES = -(-E // P)
G = 4
EP = -(-TILES // G)
ROW = G * P
EFULL = E // ROW
EREST = E - EFULL * ROW
STEPS = EP * G + BLOCKS - 1
SPARTS = STEPS // G
U = 16
ITERS = STEPS // U
HALF = U // 2
V = 5
VITERS = BLOCKS // V
HEADS, HID = 4, 64
FF = 2 * D
BIG = 1e30
NOWHERE = 255.0
NODST = 4000.0
EPS = 1e-5
ACCW = D + 2 * HEADS + 1
assert STEPS % U == 0 and STEPS % G == 0 and BLOCKS % V == 0 and TILES + BLOCKS - 1 <= STEPS


class Signal:

    def __init__(self, sem, totals):
        self.sem, self.base, total = sem, {}, 0
        for stage, n in totals.items():
            self.base[stage], total = total, total + n

    def at(self, stage, n):
        return self.base[stage] + n


def due(n):
    return not isinstance(n, int) or n > 0


def each(eng, iters, body):
    body(0)
    with eng.Fori(1, iters - 1) as it:
        body(it)
    body(iters - 1)


def is_last(it, iters):
    return isinstance(it, int) and it == iters - 1


def is_first(it):
    return isinstance(it, int) and it == 0


def build(nc, x, src, dst, edge_weight, L0_gnn_eps, L0_gnn_w1, L0_gnn_b1, L0_gnn_w2, L0_gnn_b2,
          L1_gnn_W, L1_gnn_att, L2_gnn_W1, L2_gnn_att_src1, L2_gnn_att_dst1, L2_gnn_b1, L2_gnn_W2,
          L2_gnn_att_src2, L2_gnn_att_dst2, L2_gnn_b2, L2_gnn_Wf, L2_gnn_bf, L3_gnn_wq, L3_gnn_bq,
          L3_gnn_wk, L3_gnn_bk, L3_gnn_wv, L3_gnn_bv, L3_gnn_ws, L3_gnn_bs, L3_gnn_we, L3_gnn_be,
          L3_gnn_g1, L3_gnn_b1, L3_gnn_g2, L3_gnn_b2, L3_gnn_w_ff1, L3_gnn_b_ff1, L3_gnn_w_ff2,
          L3_gnn_b_ff2, out):
    ctx = ExitStack()
    with ctx:
        def sb(name, shape, dt=F32):
            return ctx.enter_context(nc.sbuf_tensor(name, shape, dt))

        def sem(name):
            return ctx.enter_context(nc.semaphore(name))

        def dram(name, shape):
            return nc.dram_tensor(name, shape, F32, kind="Internal").ap()

        rows_total = BLOCKS * P
        t_z1, t_z2, t_z3 = dram("t_z1", [rows_total, D]), dram("t_z2", [rows_total, D]), dram("t_z3", [rows_total, HID])
        t_k, t_v = dram("t_k", [rows_total, D]), dram("t_v", [rows_total, D])

        X = sb("X", [P, BLOCKS, D])
        ACC = sb("ACC", [P, BLOCKS, ACCW])
        Y = sb("Y", [P, BLOCKS, D])
        Yf = Y[:].rearrange("p b d -> p (b d)")
        srcblock = sb("srcblock", [P, STEPS])
        tabS = sb("tabS", [P, BLOCKS * HEADS])
        tabD = sb("tabD", [P, BLOCKS * HEADS])
        mean = sb("mean", [P, BLOCKS])
        rstd = sb("rstd", [P, BLOCKS])
        nodeA = sb("nodeA", [P, BLOCKS, HEADS])
        nodeB = sb("nodeB", [P, BLOCKS, HEADS])
        nodeC = sb("nodeC", [P, BLOCKS, HEADS])

        rows = sb("rows", [P, U, D + 1])
        idx = sb("idx", [P, 2, HALF], I32)
        srcK = sb("srcK", [P, STEPS + U], I32)
        dloc = sb("dloc", [P, STEPS])
        wK = sb("wK", [P, STEPS])
        valid = sb("valid", [P, STEPS])
        blockI = sb("blockI", [1, STEPS], I32)
        LG = sb("LG", [P, STEPS, HEADS])
        PX = sb("PX", [P, STEPS, 2 * HEADS + 1])
        M = sb("M", [P, 4, P])
        R = sb("R", [P, 4, ACCW])
        junk = sb("junk", [P, 2, D])

        rowbuf = sb("rowbuf", [P, 3, HEADS * ROW])
        LT, FT, BT = (rowbuf[0:SPARTS, i, :].rearrange("p (h j) -> p h j", h=HEADS) for i in range(3))
        breakF = sb("breakF", [SPARTS, ROW])
        breakB = sb("breakB", [SPARTS, ROW])
        first = sb("first", [SPARTS, ROW])
        brk = sb("brk", [SPARTS, 2, HEADS])
        spanF = sb("spanF", [HEADS, SPARTS])
        spanB = sb("spanB", [HEADS, SPARTS])
        carryF = sb("carryF", [HEADS, SPARTS + 1])
        carryB = sb("carryB", [HEADS, SPARTS + 1])
        startF = sb("startF", [SPARTS, HEADS])
        startB = sb("startB", [SPARTS, HEADS])
        flat = rowbuf[:].rearrange("p a b -> p (a b)")
        inT = flat[:, 0:V * D].rearrange("p (v k n) -> p v k n", v=V, k=KC)
        hidT = flat[:, V * D:V * (D + FF)].rearrange("p (v m n) -> p v m n", v=V, m=FF // P)
        ZW = D + 2 * HEADS
        zrow = flat[:, V * (D + FF):V * (D + FF + ZW)].rearrange("p (v c) -> p v c", v=V)
        assert V * (D + FF + ZW) <= 3 * HEADS * ROW

        BF = mybir.dt.bfloat16
        PARTS = 3
        PICK = BLOCKS + PARTS
        place = [0]

        def lay(shape, dt=F32):
            words = int(np.prod(shape)) // (4 // mybir.dt.size(dt))
            v = flat[:, place[0]:place[0] + words]
            place[0] += words
            return v.bitcast(dt) if dt != F32 else v

        spread8 = lay([4, 2, ROW], U8).rearrange("p (s t j) -> p s t j", s=4, t=2)
        lowhot = lay([2, ROW], BF).rearrange("p (s j) -> p s j", s=2)
        apart = lay([2, ROW], BF).rearrange("p (s j) -> p s j", s=2)
        dsthot = lay([2, ROW], BF).rearrange("p (s j) -> p s j", s=2)
        blockhot = lay([2, G, PICK]).rearrange("p (s g b) -> p s g b", s=2, g=G)
        masked = lay([2, G, PICK * HEADS]).rearrange("p (s c) -> p s c", s=2)
        dsthotF = lay([2, ROW]).rearrange("p (s j) -> p s j", s=2)
        partsS = lay([PARTS * BLOCKS * HEADS], BF)
        partsD = lay([PARTS * BLOCKS * HEADS], BF)
        assert place[0] <= 3 * HEADS * ROW
        PW = 2 * ROW // 4

        at = [0]

        def temp(parts, words, dt=F32):
            v = Yf[0:parts, at[0]:at[0] + words]
            at[0] += words
            return v.bitcast(dt) if dt != F32 else v

        step_ge = temp(EP, (G + 1) * STEPS).rearrange("p (g k) -> p g k", g=G + 1)
        pick = temp(EP, G * STEPS).rearrange("p (g k) -> p g k", g=G)
        dstT, srcT, wT = temp(EP, ROW), temp(EP, ROW), temp(EP, ROW)
        dstI, srcI = temp(EP, ROW, I32), temp(EP, ROW, I32)
        assert at[0] <= BLOCKS * D
        dstM = LG[:, :, 0]
        stepB = LG[:, :, 1]
        vtmp = LG[:, :, 2]
        FT0 = rowbuf[:, 1, ROW:2 * ROW]
        srcF = LG[:, :, 2]
        dlocF = LG[:, :, 3]
        rowI, partsI = (BT[:, i, :].bitcast(I32) for i in range(2))
        srcblockI = FT0[:, 0:STEPS].bitcast(I32)
        edge8 = BT[:, 2, 0:PW].bitcast(U8).rearrange("p (t j) -> p t j", t=2)
        t_edge8 = nc.dram_tensor("t_edge8", [SPARTS, 2 * ROW], U8, kind="Internal").ap()
        DT = LT[:, 0, :]
        nextI = sb("nextI", [EP, 1], I32)
        brk1 = sb("brk1", [SPARTS, 2])
        maskneg = sb("maskneg", [P, STEPS])
        onePeps = sb("onePeps", [P, 1])
        stat = sb("stat", [P, BLOCKS, 6])
        root = sb("root", [P, BLOCKS])
        ACC3 = ACC[:, :, 0:D]
        BLOCK_SHIFT = P.bit_length() - 1
        tileI = sb("tileI", [EP, G + 1], I32)
        tileC = sb("tileC", [EP, G + 1])

        iota = sb("iota", [P, P])
        stepno = junk[:].rearrange("p a d -> p (a d)")[:, 0:STEPS]
        tileno = sb("tileno", [EP, G + 1])
        minus = sb("minus", [P, 1])
        part = sb("part", [P, 3])
        ident = sb("ident", [P, P])
        up = rowbuf[:, 1, 2 * ROW:2 * ROW + P]
        down = rowbuf[:, 1, 2 * ROW + P:2 * ROW + 2 * P]
        ones = sb("ones", [P, P])

        w1, w2 = sb("w1", [P, KC, D]), sb("w2", [P, KC, D])
        wz1, wz2 = sb("wz1", [P, KC, ZW]), sb("wz2", [P, KC, ZW])
        wz3 = sb("wz3", [P, KC, HID + 2])
        wf = sb("wf", [HID, D])
        wq, wk = sb("wq", [P, KC, D]), sb("wk", [P, KC, D])
        wv, ws = sb("wv", [P, KC, D]), sb("ws", [P, KC, D])
        wff1, wff2 = sb("wff1", [P, KC, FF]), sb("wff2", [P, FF // P, D])
        ACCf = ACC[:].rearrange("p b c -> p (b c)")
        att = ACCf[:, 0:4 * D].rearrange("p (a d) -> p a d", a=4)
        att2 = ACCf[:, 4 * D:4 * D + 2 * HID].rearrange("p (a d) -> p a d", a=2)
        bias = {}
        vectors = [("b2", L0_gnn_b2), ("b3", L2_gnn_b1), ("bf", L2_gnn_bf), ("bq", L3_gnn_bq),
                   ("bk", L3_gnn_bk), ("bv", L3_gnn_bv), ("bs", L3_gnn_bs), ("g1", L3_gnn_g1),
                   ("h1", L3_gnn_b1), ("g2", L3_gnn_g2), ("h2", L3_gnn_b2), ("bff2", L3_gnn_b_ff2),
                   ("b4", L2_gnn_b2)]
        for name, v in vectors:
            bias[name] = sb("v_" + name, [P, v.shape[0]])
        b1c = sb("b1c", [P, KC])
        bff1c = sb("bff1c", [P, FF // P])
        scal = sb("scal", [P, 3])

        PS = [ctx.enter_context(nc.psum_tensor(f"PS{i}", [P, 512], F32)) for i in range(8)]

        def by_chunk(w):
            return w.rearrange("(k p) n -> p k n", p=P)

        weight_loads = [(w1[:], by_chunk(L0_gnn_w1)), (w2[:], by_chunk(L0_gnn_w2)),
                        (b1c[:], L0_gnn_b1.rearrange("(k p) -> p k", p=P)),
                        (bff1c[:], L3_gnn_b_ff1.rearrange("(k p) -> p k", p=P))]
        weight_loads += [(scal[:, c:c + 1], v.partition_broadcast(P))
                         for c, v in enumerate((L0_gnn_eps, L3_gnn_we[0], L3_gnn_be))]
        for h in range(HEADS):
            head = slice(h * HID, (h + 1) * HID)
            weight_loads += [(wz1[:, :, head], by_chunk(L1_gnn_W[h])),
                             (att[:, 0, head], L1_gnn_att[h, 0:HID].partition_broadcast(P)),
                             (att[:, 1, head], L1_gnn_att[h, HID:2 * HID].partition_broadcast(P)),
                             (att[:, 2, head], L2_gnn_att_src1[h].partition_broadcast(P)),
                             (att[:, 3, head], L2_gnn_att_dst1[h].partition_broadcast(P))]
        weight_loads += [(wz2[:, :, 0:D], by_chunk(L2_gnn_W1)), (wz3[:, :, 0:HID], by_chunk(L2_gnn_W2)),
                         (att2[:, 0, :], L2_gnn_att_src2[0].partition_broadcast(P)),
                         (att2[:, 1, :], L2_gnn_att_dst2[0].partition_broadcast(P)), (wf[:], L2_gnn_Wf),
                         (wq[:], by_chunk(L3_gnn_wq)), (wk[:], by_chunk(L3_gnn_wk)),
                         (wv[:], by_chunk(L3_gnn_wv)), (ws[:], by_chunk(L3_gnn_ws)),
                         (wff1[:], by_chunk(L3_gnn_w_ff1)), (wff2[:], by_chunk(L3_gnn_w_ff2))]
        weight_loads += [(bias[name][:], v.partition_broadcast(P)) for name, v in vectors]

        HEADS_OF = {"L1": HEADS, "L2a": HEADS, "L2b": 1, "L3": 1}
        WIDTH = {"L0": D, "L1": D, "L2a": D, "L2b": HID, "L3": D + 1}
        EXTRAS = {"L1": HEADS, "L2a": 2 * HEADS + 1, "L2b": 3}
        SLOPE = {"L1": 0.01, "L2a": 0.2, "L2b": 0.2}
        STEP_GE_AT, EDGES_AT, SOURCES_AT, DSTM_AT, PLACES_AT, DT_AT, BREAK_AT, SPAN_AT, BYTES_AT, SETUP_V = (
            16, 22, 27, 33, 37, 38, 43, 49, 55, 83)
        LOGITS_AT = {"L1": 5, "L2a": 3, "L2b": 3, "L3": 4}
        SHIFTED_AT = {s: LOGITS_AT[s] + 4 * h + 5 for s, h in HEADS_OF.items()}
        MAXIMA_AT = {s: SHIFTED_AT[s] + 1 for s in ("L2a", "L2b")}
        COMBINED = {"L1": 7, "L2a": 23, "L2b": 16, "L3": 4}
        VARIANCE_AT = 7
        PARTS_AT = 2 * (2 * PARTS - 1)
        BANK, BANK_AGE = [0, 1, 2, 3, 1], [5, 2, 5, 5, 3]

        def back_columns(stage):
            heads = HEADS_OF[stage]
            cols = [LT[:, h, :] for h in range(heads)]
            if stage in MAXIMA_AT:
                cols += [FT[:, h, :] for h in range(heads)] + [first[:]]
            return cols

        def at_block(buf, b):
            return buf[:, bass.ds(b, 1), :].rearrange("p o c -> p (o c)")

        def by_head(table, heads):
            return table[:, 0:BLOCKS * heads].rearrange("p (b h) -> p b h", h=heads)

        def load_blocks(eng, it):
            k = U * it
            _, values = nc.values_load_multi_w_load_instructions(
                blockI[0:1, bass.ds(k, U)], engines=(eng.engine,), min_val=0, max_val=BLOCKS - 1,
                skip_runtime_bounds_check_because="the table was clamped to the blocks")
            return values

        def signal(name, totals):
            return Signal(ctx.enter_context(nc.semaphore(name)), totals)

        def each_of(stages, n):
            return {s: n for s in stages}

        SUMMING = ["L0", "L1", "L2a", "L2b", "L3"]
        SCALED = ["L1", "L2a", "L2b"]
        SOFTMAX = ["L1", "L2a", "L2b", "L3"]
        GAT = ["L1", "L2a", "L2b"]
        CHUNKS = SPARTS
        PRODUCTS = ["mlp", "z1", "z2", "z3", "wf", "qkv", "ws", "ffn"]
        NORMS = ["mlp", "gat", "wf", "ws", "ffn", "last"]

        edges_padded = signal("edges_padded", {"setup": 1})
        edges_in = signal("edges_in", {"setup": 16 * 8})
        features_in = signal("features_in", {"setup": 32})
        weights_in = signal("weights_in", {"setup": 0})
        consts_made = signal("consts_made", {"setup": 7})
        setup_v = signal("setup_v", {"setup": 0})
        setup_p = signal("setup_p", {"setup": 0})
        indices_put = signal("indices_put", {"all": 0})
        slot_opened = signal("slot_opened", {"all": 0})
        half_opened = signal("half_opened", {"all": 0})
        row_landed = [signal(f"row_landed{j}", {"all": 0}) for j in range(U)]
        sums_zeroed = signal("sums_zeroed", each_of(SUMMING, 1))
        onehot_made = signal("onehot_made", each_of(SUMMING, STEPS))
        row_scaled = signal("row_scaled", each_of(SCALED, STEPS))
        extras_put = signal("extras_put", each_of(SCALED, STEPS))
        step_summed = signal("step_summed", each_of(SUMMING, STEPS))
        sum_added = signal("sum_added", each_of(SUMMING, STEPS))
        spread_landed = [signal(f"spread_landed{i}", each_of(SOFTMAX, 16 * ITERS)) for i in range(4)]
        lowhot_made = signal("lowhot_made", each_of(GAT, CHUNKS))
        dst_apart = signal("dst_apart", each_of(GAT, CHUNKS))
        dsthot_made = signal("dsthot_made", each_of(SOFTMAX, CHUNKS))
        values_picked = signal("values_picked", each_of(GAT, CHUNKS))
        blockhot_made = signal("blockhot_made", each_of(GAT, CHUNKS + 1))
        values_masked = signal("values_masked", each_of(GAT, CHUNKS))
        parts_made = signal("parts_made", each_of(GAT, PARTS_AT))
        query_spread = signal("query_spread", {"L3": STEPS})
        logit_made = signal("logit_made", each_of(GAT, CHUNKS) | {"L3": STEPS})
        edges_stored = signal("edges_stored", {"setup": 16})
        softmax_v = signal("softmax_v", {s: MAXIMA_AT.get(s, SHIFTED_AT[s]) for s in SOFTMAX})
        softmax_p = signal("softmax_p", {s: 5 + len(back_columns(s)) for s in SOFTMAX})
        softmax_a = signal("softmax_a", {s: 2 + len(back_columns(s)) for s in SOFTMAX})
        input_staged = signal("input_staged", each_of(PRODUCTS, BLOCKS))
        in_turned = signal("in_turned", each_of(PRODUCTS, BLOCKS))
        in_copied = signal("in_copied", each_of(PRODUCTS, BLOCKS))
        hidden_made = signal("hidden_made", each_of(("mlp", "ffn"), BLOCKS))
        hidden_acted = signal("hidden_acted", each_of(("mlp", "ffn"), BLOCKS))
        product_made = signal("product_made", each_of(PRODUCTS, BLOCKS) | {"qkv": 3 * BLOCKS})
        product_copied = signal("product_copied", {"z1": BLOCKS, "z2": 2 * BLOCKS, "z3": 2 * BLOCKS, "qkv": 3 * BLOCKS})
        input_made = signal("input_made", {"mlp": BLOCKS})
        combined_v = signal("combined_v", COMBINED)
        combined_a = signal("combined_a", each_of(("L2a", "L2b"), 2))
        product_added = signal("product_added", each_of(("mlp", "wf", "ws", "ffn"), 2 * BLOCKS))
        stats_made = signal("stats_made", each_of(NORMS, BLOCKS))
        norm_step = signal("norm_step", each_of(NORMS, VARIANCE_AT + 1))
        norm_root = signal("norm_root", each_of(NORMS, 1))
        normed = signal("normed", {"mlp": BLOCKS, "gat": BLOCKS, "wf": BLOCKS, "ws": 3 * BLOCKS,
                                   "ffn": 3 * BLOCKS, "last": BLOCKS})
        residual_added = signal("residual_added", {"last": 1})
        TABLES = {"z1": 1, "z2": 1, "z3": 1, "qkv": 2}
        TABLE_LOOPS = {s: 16 * n * VITERS for s, n in TABLES.items()}
        table_stored = [signal(f"table_stored{v}", TABLE_LOOPS) for v in range(V)]
        out_stored = signal("out_stored", {"out": 32})

        PASSES = [(x, D, None, step_summed, "L0"), (t_z1, D, "z1", row_scaled, "L1"),
                  (t_z2, D, "z2", row_scaled, "L2a"), (t_z3, HID, "z3", row_scaled, "L2b"),
                  (t_k, D, "qkv", logit_made, "L3"), (t_v, D, "qkv", step_summed, "L3")]
        SUM_PASS = {"L0": 0, "L1": 1, "L2a": 2, "L2b": 3, "L3": 5}
        LOGIT_PASS = {"L3": 4}

        def landed(eng, g, it, j):
            eng.wait_ge(row_landed[j].sem, 16 * (ITERS * g + 1) + 16 * it)

        block = ctx.enter_context(nc.Block())

        @block.gpsimd
        def _(pool):
            for t, pattern, base, mult in (
                    (iota[:], [[1, P]], 0, 0), (stepno, [[1, STEPS]], 0, 0), (tileno[:], [[1, G + 1]], 0, G),
                    (part[:, 0:1], [[0, 1]], 0, 1), (part[:, 1:2], [[0, 1]], 1, 1), (part[:, 2:3], [[0, 1]], -1, 1),
                    (minus[:], [[0, 1]], 0, -1)):
                nc.gpsimd.iota(t, pattern, base=base, channel_multiplier=mult,
                               allow_small_or_imprecise_dtypes=True).then_inc(consts_made.sem, 1)
            def stage_input(loop, buf, ready, cols=D):
                def body(it):
                    for v in range(V):
                        b = V * it + v
                        ready(b)
                        if due(b - V + 1):
                            pool.wait_ge(in_turned.sem, in_turned.at(loop, b - V + 1))
                        nc.gpsimd.tensor_copy(rows[:, v, 0:cols], at_block(buf, b)[:, 0:cols])\
                            .then_inc(input_staged.sem, 1)
                each(pool, VITERS, body)

            def gather(g):
                table, width, writer, used, stage = PASSES[g]
                if writer:
                    for v in range(V):
                        pool.wait_ge(table_stored[v].sem, table_stored[v].at(writer, TABLE_LOOPS[writer]))

                def body(it):
                    for j in range(U):
                        if j % HALF == 0:
                            if not is_first(it):
                                pool.wait_ge(used.sem, used.at(stage, U * it - U + j + HALF))
                            elif g:
                                _, _, _, before, before_stage = PASSES[g - 1]
                                pool.wait_ge(before.sem, before.at(before_stage, STEPS - U + j + HALF))
                            pool.wait_ge(indices_put.sem, 2 * ITERS * g + j // HALF + 1 + 2 * it)
                            pool.sem_inc(half_opened.sem, 1)
                        pool.indirect_dma_start(
                            out=rows[:, j, 0:width], out_offset=None, in_=table[:, :],
                            in_offset=bass.IndirectOffsetOnAxis(
                                ap=idx[:, j // HALF, j % HALF:j % HALF + 1], axis=0)).then_inc(row_landed[j].sem, 16)
                each(pool, ITERS, body)

            gather(0)
            stage_input("mlp", ACC, lambda b: pool.wait_ge(input_made.sem, input_made.at("mlp", b + 1)))
            stage_input("z1", X, lambda b: pool.wait_ge(normed.sem, normed.at("mlp", b + 1)))
            gather(1)
            stage_input("z2", X, lambda b: pool.wait_ge(normed.sem, normed.at("gat", b + 1)))
            gather(2)
            stage_input("z3", Y, lambda b: pool.wait_ge(combined_v.sem, combined_v.at("L2a", COMBINED["L2a"])))
            gather(3)
            stage_input("wf", Y, lambda b: pool.wait_ge(combined_v.sem, combined_v.at("L2b", COMBINED["L2b"])), P)
            stage_input("qkv", X, lambda b: pool.wait_ge(normed.sem, normed.at("wf", b + 1)))
            gather(4)
            gather(5)
            stage_input("ws", X, lambda b: pool.wait_ge(combined_v.sem, combined_v.at("L3", COMBINED["L3"])))
            stage_input("ffn", ACC, lambda b: pool.wait_ge(normed.sem, normed.at("ws", 2 * BLOCKS + b + 1)))

        @block.sync
        def _(sp):
            sp.wait_ge(edges_padded.sem, edges_padded.at("setup", 1))
            for tile, vec in ((dstI, dst), (srcI, src), (wT, edge_weight)):
                sp.dma_start(tile[0:EFULL, :], vec[0:EFULL * ROW].rearrange("(p j) -> p j", j=ROW))\
                    .then_inc(edges_in.sem, 16)
                sp.dma_start(tile[EFULL:EFULL + 1, 0:EREST],
                             vec[EFULL * ROW:E].rearrange("(o j) -> o j", o=1)).then_inc(edges_in.sem, 16)
            sp.dma_start(nextI[0:EFULL - 1, :], dst[ROW:EFULL * ROW].rearrange("(p j) -> p j", j=ROW)[:, 0:1],
                         allow_slow_non_contiguous=True).then_inc(edges_in.sem, 16)
            sp.dma_start(nextI[EFULL - 1:EFULL, :], dst[EFULL * ROW:EFULL * ROW + 1].rearrange("(o j) -> o j", o=1))\
                .then_inc(edges_in.sem, 16)
            sp.dma_start(X[:, 0:FULL, :], x[0:FULL * P, :].rearrange("(b p) d -> p b d", p=P))\
                .then_inc(features_in.sem, 16)
            sp.dma_start(X[0:REST, FULL, :], x[FULL * P:N, :]).then_inc(features_in.sem, 16)

            for tile, source in weight_loads:
                sp.dma_start(tile, source, allow_slow_non_contiguous=True).then_inc(weights_in.sem, 16)

            def store(loop, parts, copies):
                def body(it):
                    for v in range(V):
                        sp.wait_ge(product_copied.sem, product_copied.at(loop, copies * (V * it + v + 1)))
                        for table, slot in parts:
                            sp.dma_start(table[bass.ds((V * it + v) * P, P), :], slot(v))\
                                .then_inc(table_stored[v].sem, 16)
                each(sp, VITERS, body)

            def spread_edges(stage):
                def body(it):
                    for s in range(4):
                        c = 4 * it + s
                        if due(c - 3):
                            if stage in GAT:
                                sp.wait_ge(lowhot_made.sem, lowhot_made.at(stage, c - 3))
                            sp.wait_ge(dsthot_made.sem, dsthot_made.at(stage, c - 3))
                            sp.sem_inc(slot_opened.sem, 1)
                        sp.dma_start(spread8[:, s, :, :].rearrange("p t j -> p (t j)"),
                                     t_edge8[bass.ds(c, 1), :].rearrange("o j -> (o j)").partition_broadcast(P))\
                            .then_inc(spread_landed[s].sem, 16)
                each(sp, ITERS, body)

            def tables_done(loop):
                for v in range(V):
                    sp.wait_ge(table_stored[v].sem, table_stored[v].at(loop, TABLE_LOOPS[loop]))

            sp.wait_ge(setup_v.sem, BYTES_AT)
            sp.dma_start(t_edge8[:, :], edge8.rearrange("p t j -> p (t j)")).then_inc(edges_stored.sem, 16)
            sp.wait_ge(edges_stored.sem, 16)
            store("z1", [(t_z1, lambda v: zrow[:, v, 0:D])], 1)
            tables_done("z1")
            spread_edges("L1")
            store("z2", [(t_z2, lambda v: zrow[:, v, 0:D])], 2)
            tables_done("z2")
            spread_edges("L2a")
            store("z3", [(t_z3, lambda v: zrow[:, v, 0:HID])], 2)
            tables_done("z3")
            spread_edges("L2b")
            store("qkv", [(t_k, lambda v: zrow[:, v, 0:D]),
                          (t_v, lambda v: hidT[:, v, 0:KC, :].rearrange("p m n -> p (m n)"))], 3)
            tables_done("qkv")
            spread_edges("L3")

            sp.wait_ge(normed.sem, normed.at("last", BLOCKS))
            sp.dma_start(out[0:FULL * P, :].rearrange("(b p) d -> p b d", p=P), X[:, 0:FULL, :])\
                .then_inc(out_stored.sem, 16)
            sp.dma_start(out[FULL * P:N, :], X[0:REST, FULL, :]).then_inc(out_stored.sem, 16)
            sp.wait_ge(out_stored.sem, 32)

        @block.vector
        def _(dve):
            vec = nc.vector
            done = [0]

            def step(instruction):
                done[0] += 1
                instruction.then_inc(setup_v.sem, 1)
                return done[0]

            def settled():
                dve.wait_ge(setup_v.sem, done[0])

            vec.memset(dstI, int(NODST))
            vec.memset(srcI, 0)
            vec.memset(wT, 0.0)
            vec.memset(X[:, FULL, :], 0.0)
            vec.memset(nextI[:], int(NODST)).then_inc(edges_padded.sem, 1)
            step(vec.memset(rows[:, :, D:D + 1], 1.0))
            step(vec.memset(ones[:], 1.0))
            step(vec.memset(carryF[:], -BIG))
            step(vec.memset(carryB[:], -BIG))
            dve.wait_ge(consts_made.sem, consts_made.at("setup", 7))
            step(vec.tensor_scalar(ident[:], iota[:], part[:, 0:1], None, ALU.is_equal))
            step(vec.tensor_scalar(up, iota[:], part[:, 1:2], None, ALU.is_equal))
            step(vec.tensor_scalar(down, iota[:], part[:, 2:3], None, ALU.is_equal))

            dve.wait_ge(edges_in.sem, 16 * 8)
            step(vec.tensor_scalar(tileI[:, 0:G], dstI[:, ::P], BLOCK_SHIFT, None, ALU.arith_shift_right))
            step(vec.tensor_scalar(tileI[:, G:G + 1], nextI[:], BLOCK_SHIFT, None, ALU.arith_shift_right))
            settled()
            step(vec.tensor_tensor(tileC[:], tileI[:], tileno[:], ALU.add))
            settled()
            step(vec.memset(tileC[0:1, 0:1], 0.0))
            settled()
            for g in range(G + 1):
                step(vec.tensor_scalar(step_ge[:, g, :], stepno[0:EP, :], tileC[:, g:g + 1], None, ALU.is_ge))
            settled()
            assert done[0] == STEP_GE_AT
            for g in range(G):
                step(vec.tensor_tensor(pick[:, g, :], step_ge[:, g, :], step_ge[:, g + 1, :], ALU.subtract))
            step(vec.tensor_copy(dstT, dstI))
            step(vec.tensor_copy(srcT, srcI))
            assert done[0] == EDGES_AT
            dve.wait_ge(setup_p.sem, 1)
            step(vec.scalar_tensor_tensor(stepB, PS[0][:, 0:STEPS], -1.0, stepno, ALU.mult, ALU.add))
            settled()
            step(vec.tensor_scalar(stepB, stepB, 1.0, None, ALU.add))
            settled()
            step(vec.tensor_scalar(blockI[:], stepB[0:1, :], float(BLOCKS - 1), None, ALU.min))
            dve.wait_ge(setup_p.sem, 2)
            step(vec.tensor_copy(srcK[:, 0:STEPS], PS[1][:, 0:STEPS]))
            step(vec.tensor_copy(srcK[:, STEPS:STEPS + U], PS[1][:, 0:U]))
            assert done[0] == SOURCES_AT
            step(vec.scalar_tensor_tensor(dloc[:], stepB, -float(P), PS[2][:, 0:STEPS], ALU.mult, ALU.add))
            settled()
            step(vec.tensor_copy(wK[:], PS[3][:, 0:STEPS]))
            step(vec.tensor_scalar(vtmp, dloc[:], 0.0, None, ALU.is_ge))
            settled()
            step(vec.scalar_tensor_tensor(valid[:], dloc[:], float(P), vtmp, ALU.is_lt, ALU.mult))
            settled()
            step(vec.tensor_tensor(vtmp, PS[2][:, 0:STEPS], valid[:], ALU.mult))
            settled()
            step(vec.scalar_tensor_tensor(dstM, valid[:], -1.0, vtmp, ALU.add, ALU.add))
            assert done[0] == DSTM_AT
            settled()
            step(vec.tensor_copy(srcF, PS[1][:, 0:STEPS]))
            step(vec.tensor_tensor(dlocF, dloc[:], valid[:], ALU.mult))
            settled()
            step(vec.scalar_tensor_tensor(dlocF, valid[:], -NOWHERE, dlocF, ALU.mult, ALU.add))
            settled()
            step(vec.tensor_scalar(dlocF, dlocF, NOWHERE, None, ALU.add))
            assert done[0] == PLACES_AT
            dve.wait_ge(setup_p.sem, 3)
            step(vec.tensor_copy(DT, PS[4][0:SPARTS, :]))
            assert done[0] == DT_AT
            settled()
            same = FT[:, 0, :]
            step(vec.tensor_tensor(same[:, 1:ROW], DT[:, 1:ROW], DT[:, 0:ROW - 1], ALU.is_equal))
            dve.wait_ge(setup_p.sem, 4)
            step(vec.tensor_tensor(same[:, 0:1], DT[:, 0:1], PS[5][0:SPARTS, 0:1], ALU.is_equal))
            settled()
            step(vec.memset(same[0:1, 0:1], 0.0))
            settled()
            step(vec.tensor_scalar(breakF[:], same, -1.0, BIG, ALU.add, ALU.mult))
            step(vec.tensor_scalar(first[:], same, -1.0, 1.0, ALU.mult, ALU.add))
            settled()
            assert done[0] == BREAK_AT
            step(vec.tensor_copy(breakB[:, 0:ROW - 1], breakF[:, 1:ROW]))
            dve.wait_ge(setup_p.sem, 5)
            step(vec.tensor_copy(breakB[:, ROW - 1:ROW], PS[5][0:SPARTS, 1:2]))
            settled()
            step(vec.tensor_reduce(brk1[:, 0:1], breakF[:], AX, ALU.add))
            step(vec.tensor_reduce(brk1[:, 1:2], breakB[:], AX, ALU.add))
            settled()
            for i in range(2):
                step(vec.tensor_copy(brk[:, i, :], brk1[:, i:i + 1].to_broadcast([SPARTS, HEADS])))
            assert done[0] == SPAN_AT
            dve.wait_ge(setup_p.sem, 6)
            step(vec.tensor_copy(spanF[:], PS[6][0:HEADS, 0:SPARTS]))
            step(vec.tensor_copy(spanB[:], PS[6][0:HEADS, SPARTS:2 * SPARTS]))
            dve.wait_ge(setup_p.sem, 7)
            step(vec.tensor_copy(rowI, PS[1][0:SPARTS, :]))
            step(vec.tensor_copy(edge8[:, 1, :], PS[3][0:SPARTS, :]))
            settled()
            step(vec.tensor_scalar(partsI, rowI, P - 1, None, ALU.bitwise_and))
            settled()
            step(vec.tensor_copy(edge8[:, 0, :], partsI))
            assert done[0] == BYTES_AT
            step(vec.tensor_scalar(srcblockI, srcK[:, 0:STEPS], BLOCK_SHIFT, None, ALU.arith_shift_right))
            settled()
            step(vec.tensor_copy(srcblock[:], srcblockI))
            dve.wait_ge(weights_in.sem, 16 * len(weight_loads))
            for wz, a0 in ((wz1, 0), (wz2, 2)):
                for which in range(2):
                    settled()
                    for k in range(KC):
                        step(vec.tensor_tensor(junk[:, k, :], wz[:, k, 0:D], att[:, a0 + which, :], ALU.mult))
                    settled()
                    for k in range(KC):
                        step(vec.tensor_reduce(wz[:, k, D + which * HEADS:D + (which + 1) * HEADS],
                                               junk[:, k, :].rearrange("p (h f) -> p h f", h=HEADS), AX, ALU.add))
            for which in range(2):
                settled()
                for k in range(KC):
                    step(vec.tensor_tensor(junk[:, k, 0:HID], wz3[:, k, 0:HID], att2[:, which, :], ALU.mult))
                settled()
                for k in range(KC):
                    step(vec.tensor_reduce(wz3[:, k, HID + which:HID + which + 1], junk[:, k, 0:HID], AX, ALU.add))
            step(vec.tensor_scalar(maskneg[:], valid[:], -1.0, BIG, ALU.add, ALU.mult))
            step(vec.tensor_scalar(onePeps[:], scal[:, 0:1], 1.0, None, ALU.add))
            settled()
            assert done[0] == SETUP_V

            def sum_edges(stage):
                width = WIDTH[stage]
                scaled = stage in SCALED
                heads = HEADS_OF.get(stage, 1)
                cols = width + EXTRAS.get(stage, 0)
                g = SUM_PASS[stage]
                vec.memset(ACC[:], 0.0).then_inc(sums_zeroed.sem, 1)

                def prepare(it, j):
                    k = U * it + j
                    col = bass.ds(k, 1)
                    if due(k - 3):
                        dve.wait_ge(step_summed.sem, step_summed.at(stage, k - 3))
                    if scaled:
                        vec.tensor_scalar(M[:, j % 4, :], iota[:], dloc[:, col], None, ALU.is_equal)\
                            .then_inc(onehot_made.sem, 1)
                        landed(dve, g, it, j)
                        vec.tensor_tensor(
                            R[:, j % 4, 0:width].rearrange("p (h f) -> p h f", h=heads),
                            rows[:, j, 0:width].rearrange("p (h f) -> p h f", h=heads),
                            PX[:, col, 0:heads].rearrange("p o h -> p (o h)").unsqueeze(2).to_broadcast([P, heads, width // heads]),
                            ALU.mult).then_inc(row_scaled.sem, 1)
                    else:
                        w = wK[:, col] if stage == "L0" else PX[:, col, 0]
                        vec.tensor_scalar(M[:, j % 4, :], iota[:], dloc[:, col], w, ALU.is_equal, ALU.mult)\
                            .then_inc(onehot_made.sem, 1)

                def add(k, j, b):
                    dve.wait_ge(step_summed.sem, step_summed.at(stage, k + 1))
                    if due(k):
                        dve.wait_ge(sum_added.sem, sum_added.at(stage, k))
                    a = ACC[:, bass.ds(b, 1), 0:cols].rearrange("p o c -> p (o c)")
                    vec.tensor_tensor(a, a, PS[j % 4][:, 0:cols], ALU.add).then_inc(sum_added.sem, 1)

                prepare(0, 0)
                dve.wait_ge(sums_zeroed.sem, sums_zeroed.at(stage, 1))

                def body(it):
                    blocks = load_blocks(dve, it)
                    for j in range(U):
                        if j < U - 1:
                            prepare(it, j + 1)
                        elif not is_last(it, ITERS):
                            prepare(it + 1, 0)
                        add(U * it + j, j, blocks[j])
                each(dve, ITERS, body)

            def rows_free(loop):
                for v in range(V):
                    dve.wait_ge(table_stored[v].sem, table_stored[v].at(loop, TABLE_LOOPS[loop]))
                dve.wait_ge(product_made.sem, product_made.at(loop, (3 if loop == "qkv" else 1) * BLOCKS))

            def logits_gat(stage):
                heads = HEADS_OF[stage]
                n = BLOCKS * heads
                vec.memset(blockhot[:, :, :, BLOCKS:PICK], 1.0).then_inc(blockhot_made.sem, 1)
                made = 0
                for tab, parts in ((tabS, lambda i: partsS[:, i * n:(i + 1) * n]),
                                   (tabD, lambda i: partsD[:, 0:PARTS * n].rearrange(
                                       "p (b c h) -> p c b h", c=PARTS, h=heads)[:, i, :, :])):
                    rest = nodeA[:].rearrange("p b h -> p (b h)")[:, 0:n]
                    left = tab[:, 0:n]
                    for i in range(PARTS):
                        shaped = left if tab is tabS else left.rearrange("p (b h) -> p b h", h=heads)
                        vec.tensor_copy(parts(i), shaped).then_inc(parts_made.sem, 1)
                        made += 1
                        dve.wait_ge(parts_made.sem, parts_made.at(stage, made))
                        if i < PARTS - 1:
                            o = rest if tab is tabS else rest.rearrange("p (b h) -> p b h", h=heads)
                            vec.tensor_tensor(o, shaped, parts(i), ALU.subtract).then_inc(parts_made.sem, 1)
                            made += 1
                            dve.wait_ge(parts_made.sem, parts_made.at(stage, made))
                            left = rest
                assert made == PARTS_AT
                hot = lambda s: blockhot[:, s % 2, :, 0:BLOCKS]

                def hots(it, s):
                    c = 4 * it + s
                    dve.wait_ge(spread_landed[s].sem, spread_landed[s].at(stage, 16 * (it + 1)))
                    if due(c - 1):
                        dve.wait_ge(values_picked.sem, values_picked.at(stage, c - 1))
                        dve.wait_ge(values_masked.sem, values_masked.at(stage, c - 1))
                    vec.tensor_scalar(lowhot[:, s % 2, :], spread8[:, s, 0, :], part[:, 0:1], None, ALU.is_equal)\
                        .then_inc(lowhot_made.sem, 1)
                    vec.tensor_tensor(hot(s), iota[:, 0:BLOCKS].unsqueeze(1).to_broadcast([P, G, BLOCKS]),
                                      srcblock[:, bass.ds(4 * c, G)].unsqueeze(2).to_broadcast([P, G, BLOCKS]),
                                      ALU.is_equal).then_inc(blockhot_made.sem, 1)

                def body(it):
                    for s in range(4):
                        c = 4 * it + s
                        if s < 3:
                            hots(it, s + 1)
                        elif not is_last(it, ITERS):
                            hots(it + 1, 0)
                        dve.wait_ge(values_picked.sem, values_picked.at(stage, c + 1))
                        dve.wait_ge(blockhot_made.sem, blockhot_made.at(stage, c + 2))
                        if due(c - 1):
                            dve.wait_ge(logit_made.sem, logit_made.at(stage, c - 1))
                        m = masked[:, s % 2, 0:G * PICK * heads]
                        vec.tensor_tensor(m.rearrange("p (r h) -> p r h", h=heads),
                                          PS[s % 4][:, 0:G * PICK * heads].rearrange("p (r h) -> p r h", h=heads),
                                          blockhot[:, s % 2, :, :].rearrange("p g b -> p (g b)").unsqueeze(2)
                                          .to_broadcast([P, G * PICK, heads]), ALU.mult).then_inc(values_masked.sem, 1)
                        dve.wait_ge(values_masked.sem, values_masked.at(stage, c + 1))
                        vec.tensor_reduce(LG[:, bass.ds(4 * c, G), 0:heads],
                                          m.rearrange("p (g b h) -> p g h b", g=G, h=heads), AX, ALU.add)\
                            .then_inc(logit_made.sem, 1)
                hots(0, 0)
                each(dve, ITERS, body)

            def logits_dot(stage):
                g = LOGIT_PASS[stage]

                def hots(it, s):
                    c = 4 * it + s
                    dve.wait_ge(spread_landed[s].sem, spread_landed[s].at(stage, 16 * (it + 1)))
                    if due(4 * (c - 1)):
                        dve.wait_ge(query_spread.sem, query_spread.at(stage, 4 * (c - 1)))
                    vec.tensor_scalar(dsthotF[:, s % 2, :], spread8[:, s, 1, :], part[:, 0:1], None, ALU.is_equal)\
                        .then_inc(dsthot_made.sem, 1)

                def body(it):
                    for s in range(4):
                        if s < 3:
                            hots(it, s + 1)
                        elif not is_last(it, ITERS):
                            hots(it + 1, 0)
                        for j in range(4 * s, 4 * s + 4):
                            k = U * it + j
                            dve.wait_ge(query_spread.sem, query_spread.at(stage, k + 1))
                            landed(dve, g, it, j)
                            if due(k - 1):
                                dve.wait_ge(logit_made.sem, logit_made.at(stage, k - 1))
                            vec.scalar_tensor_tensor(junk[:, j % 2, :], PS[4 + j % 4][:, 0:D], float(D) ** -0.5,
                                                     rows[:, j, 0:D], ALU.mult, ALU.mult,
                                                     accum_out=LG[:, bass.ds(k, 1), 0]).then_inc(logit_made.sem, 1)
                hots(0, 0)
                each(dve, ITERS, body)

            def softmax(stage):
                heads = HEADS_OF[stage]
                n = [0]

                def step(instruction):
                    n[0] += 1
                    instruction.then_inc(softmax_v.sem, 1)

                def settled():
                    dve.wait_ge(softmax_v.sem, softmax_v.at(stage, n[0]))

                L = LG[:, :, 0:heads]
                vb = valid[:].unsqueeze(2).to_broadcast([P, STEPS, heads])
                dve.wait_ge(logit_made.sem, logit_made.at(stage, CHUNKS if stage in GAT else STEPS))
                if stage == "L3":
                    step(vec.scalar_tensor_tensor(LG[:, :, 0], wK[:], scal[:, 1:2], LG[:, :, 0], ALU.mult, ALU.add))
                    settled()
                    step(vec.tensor_scalar(LG[:, :, 0], LG[:, :, 0], scal[:, 2:3], None, ALU.add))
                    settled()
                else:
                    step(vec.scalar_tensor_tensor(L, L, SLOPE[stage], L, ALU.mult, ALU.max))
                    settled()
                if stage == "L1":
                    z = PX[:, :, 0:heads]
                    step(vec.tensor_scalar(z, L, 0.0, -1000.0, ALU.is_equal, ALU.mult))
                    settled()
                    step(vec.tensor_tensor(L, L, z, ALU.add))
                    settled()
                step(vec.tensor_tensor(L, L, vb, ALU.mult))
                settled()
                step(vec.tensor_tensor(L, L, maskneg[:].unsqueeze(2).to_broadcast([P, STEPS, heads]), ALU.add))
                assert n[0] == LOGITS_AT[stage]
                dve.wait_ge(softmax_a.sem, softmax_a.at(stage, 1))
                for h in range(heads):
                    step(vec.tensor_tensor_scan(FT[:, h, :], breakF[:], LT[:, h, :], -BIG, ALU.add, ALU.max))
                assert n[0] == LOGITS_AT[stage] + heads
                dve.wait_ge(softmax_p.sem, softmax_p.at(stage, 2))
                settled()
                step(vec.tensor_tensor_scan(carryF[0:heads, 1:SPARTS + 1], spanF[0:heads, :], PS[4][0:heads, 0:SPARTS],
                                            -BIG, ALU.add, ALU.max))
                dve.wait_ge(softmax_p.sem, softmax_p.at(stage, 3))
                step(vec.tensor_copy(startF[:, 0:heads], PS[5][0:SPARTS, 0:heads]))
                settled()
                for h in range(heads):
                    step(vec.tensor_tensor_scan(FT[:, h, :], breakF[:], LT[:, h, :], startF[:, h:h + 1],
                                                ALU.add, ALU.max))
                settled()
                for h in range(heads):
                    step(vec.tensor_tensor_scan(BT[:, h, ::-1], breakB[:, ::-1], FT[:, h, ::-1], -BIG,
                                                ALU.add, ALU.max))
                dve.wait_ge(softmax_p.sem, softmax_p.at(stage, 4))
                settled()
                step(vec.tensor_tensor_scan(carryB[0:heads, SPARTS - 1::-1], spanB[0:heads, ::-1],
                                            PS[6][0:heads, SPARTS - 1::-1], -BIG, ALU.add, ALU.max))
                dve.wait_ge(softmax_p.sem, softmax_p.at(stage, 5))
                step(vec.tensor_copy(startB[:, 0:heads], PS[7][0:SPARTS, 0:heads]))
                settled()
                for h in range(heads):
                    step(vec.tensor_tensor_scan(BT[:, h, ::-1], breakB[:, ::-1], FT[:, h, ::-1],
                                                startB[:, h:h + 1], ALU.add, ALU.max))
                settled()
                step(vec.tensor_tensor(LT[:, 0:heads, :], LT[:, 0:heads, :], BT[:, 0:heads, :], ALU.subtract))
                assert n[0] == SHIFTED_AT[stage]
                if stage in ("L2a", "L2b"):
                    step(vec.tensor_tensor(FT[:, 0:heads, :], BT[:, 0:heads, :],
                                           first[:].unsqueeze(1).to_broadcast([SPARTS, heads, ROW]), ALU.mult))
                    assert n[0] == MAXIMA_AT[stage]
                dve.wait_ge(softmax_a.sem, softmax_a.at(stage, 2 + len(back_columns(stage))))

            def combine(stage):
                heads = HEADS_OF[stage]
                width = WIDTH[stage] - (stage == "L3")
                n = [0]

                def step(instruction):
                    n[0] += 1
                    instruction.then_inc(combined_v.sem, 1)

                def settled():
                    dve.wait_ge(combined_v.sem, combined_v.at(stage, n[0]))

                dve.wait_ge(sum_added.sem, sum_added.at(stage, STEPS))
                if stage in ("L1", "L3"):
                    den = ACC[:, :, D:D + heads]
                    step(vec.tensor_scalar(nodeA[:, :, 0:heads], den, 1e-12, None, ALU.max))
                    settled()
                    step(vec.reciprocal(nodeA[:, :, 0:heads], nodeA[:, :, 0:heads]))
                    settled()
                    for h in range(heads):
                        f = D // heads
                        a = ACC[:, :, h * f:(h + 1) * f]
                        step(vec.tensor_tensor(a, a, nodeA[:, :, h:h + 1].to_broadcast([P, BLOCKS, f]), ALU.mult))
                    settled()
                    if stage == "L1":
                        step(vec.tensor_tensor(X[:], X[:], ACC[:, :, 0:D], ALU.add))
                    else:
                        step(vec.tensor_tensor(ACC[:, :, 0:D], X[:], ACC[:, :, 0:D], ALU.add))
                    settled()
                    assert n[0] == COMBINED[stage]
                    return
                den = ACC[:, :, width:width + heads]
                top = ACC[:, :, width + heads:width + 2 * heads]
                has = ACC[:, :, width + 2 * heads:width + 2 * heads + 1].to_broadcast([P, BLOCKS, heads])
                A, B, C = (t[:, :, 0:heads] for t in (nodeA, nodeB, nodeC))
                step(vec.tensor_scalar(A, has, -1.0, BIG, ALU.add, ALU.mult))
                step(vec.tensor_tensor(B, by_head(tabS, heads), by_head(tabD, heads), ALU.add))
                settled()
                step(vec.tensor_tensor(A, A, top, ALU.add))
                step(vec.scalar_tensor_tensor(B, B, SLOPE[stage], B, ALU.mult, ALU.max))
                settled()
                step(vec.tensor_tensor(C, A, B, ALU.max))
                settled()
                step(vec.tensor_tensor(A, A, C, ALU.subtract))
                step(vec.tensor_tensor(B, B, C, ALU.subtract))
                assert n[0] == 7
                dve.wait_ge(combined_a.sem, combined_a.at(stage, 2))
                step(vec.tensor_tensor(C, den, A, ALU.mult))
                settled()
                step(vec.tensor_tensor(C, C, B, ALU.add))
                settled()
                step(vec.reciprocal(C, C))
                settled()
                step(vec.tensor_tensor(A, A, C, ALU.mult))
                step(vec.tensor_tensor(B, B, C, ALU.mult))
                settled()
                f = width // heads
                for h in range(heads):
                    a, y = ACC[:, :, h * f:(h + 1) * f], Y[:, :, h * f:(h + 1) * f]
                    step(vec.tensor_tensor(a, a, A[:, :, h:h + 1].to_broadcast([P, BLOCKS, f]), ALU.mult))
                    step(vec.tensor_tensor(y, y, B[:, :, h:h + 1].to_broadcast([P, BLOCKS, f]), ALU.mult))
                settled()
                y, a = Y[:, :, 0:width], ACC[:, :, 0:width]
                step(vec.tensor_tensor(y, y, a, ALU.add))
                settled()
                bv = bias["b3" if stage == "L2a" else "b4"][:].unsqueeze(1).to_broadcast([P, BLOCKS, width])
                step(vec.tensor_tensor(y, y, bv, ALU.add))
                settled()
                if stage == "L2a":
                    step(vec.tensor_scalar(y, y, 0.0, None, ALU.max))
                    settled()
                assert n[0] == COMBINED[stage]

            def norm(stage, buf, gain=None, shift=None):
                def stats(it):
                    for v in range(V):
                        b = V * it + v
                        vec.bn_stats(at_block(stat, b), at_block(buf, b)).then_inc(stats_made.sem, 1)
                each(dve, VITERS, stats)
                dve.wait_ge(stats_made.sem, stats_made.at(stage, BLOCKS))
                n = [0]

                def step(instruction):
                    n[0] += 1
                    instruction.then_inc(norm_step.sem, 1)

                def settled():
                    dve.wait_ge(norm_step.sem, norm_step.at(stage, n[0]))
                mean_e, sq_e, mean_o, sq_o = (stat[:, :, c] for c in (1, 2, 4, 5))
                step(vec.tensor_tensor(mean[:], mean_e, mean_o, ALU.add))
                step(vec.tensor_tensor(root[:], mean_e, mean_o, ALU.subtract))
                step(vec.tensor_tensor(rstd[:], sq_e, sq_o, ALU.add))
                settled()
                step(vec.tensor_scalar(mean[:], mean[:], 0.5, None, ALU.mult))
                step(vec.scalar_tensor_tensor(root[:], root[:], 0.25, root[:], ALU.mult, ALU.mult))
                step(vec.tensor_scalar(rstd[:], rstd[:], 1.0 / D, EPS, ALU.mult, ALU.add))
                settled()
                step(vec.tensor_tensor(rstd[:], rstd[:], root[:], ALU.add))
                assert n[0] == VARIANCE_AT
                dve.wait_ge(norm_root.sem, norm_root.at(stage, 1))
                step(vec.reciprocal(rstd[:], root[:]))
                settled()

                def apply(it):
                    for v in range(V):
                        b = V * it + v
                        vec.tensor_scalar(at_block(buf, b), at_block(buf, b), mean[:, bass.ds(b, 1)],
                                          rstd[:, bass.ds(b, 1)], ALU.subtract, ALU.mult).then_inc(normed.sem, 1)
                each(dve, VITERS, apply)
                if gain is not None:
                    for i, (op, w) in enumerate(((ALU.mult, gain), (ALU.add, shift))):
                        def apply(it):
                            for v in range(V):
                                b = V * it + v
                                dve.wait_ge(normed.sem, normed.at(stage, BLOCKS * i + b + 1))
                                vec.tensor_tensor(at_block(buf, b), at_block(buf, b), w[:], op)\
                                    .then_inc(normed.sem, 1)
                        each(dve, VITERS, apply)

            def residual(loop, terms, buf):
                nt = len(terms)

                def body(it):
                    for v in range(V):
                        b = V * it + v
                        dve.wait_ge(product_made.sem, product_made.at(loop, b + 1))
                        for i, t in enumerate(terms):
                            if i:
                                dve.wait_ge(product_added.sem, product_added.at(loop, nt * b + i))
                            other = t(b)
                            first_in = PS[4 + BANK[v]][:, 0:D] if i == 0 else at_block(buf, b)
                            ins = vec.tensor_tensor(at_block(buf, b), first_in, other, ALU.add)
                            ins.then_inc(product_added.sem, 1)
                each(dve, VITERS, body)
                dve.wait_ge(product_added.sem, product_added.at(loop, nt * BLOCKS))

            sum_edges("L0")
            dve.wait_ge(sum_added.sem, sum_added.at("L0", STEPS))
            dve.wait_ge(features_in.sem, 32)

            def scale_input(it):
                for v in range(V):
                    b = V * it + v
                    vec.scalar_tensor_tensor(at_block(ACC, b)[:, 0:D], at_block(X, b), onePeps[:],
                                             at_block(ACC, b)[:, 0:D], ALU.mult, ALU.add)\
                        .then_inc(input_made.sem, 1)
            each(dve, VITERS, scale_input)
            residual("mlp", [lambda b: at_block(X, b), lambda b: bias["b2"][:]], X)
            norm("mlp", X)
            rows_free("z1")
            logits_gat("L1")
            softmax("L1")
            sum_edges("L1")
            combine("L1")
            norm("gat", X)
            rows_free("z2")
            logits_gat("L2a")
            softmax("L2a")
            sum_edges("L2a")
            combine("L2a")
            rows_free("z3")
            logits_gat("L2b")
            softmax("L2b")
            sum_edges("L2b")
            combine("L2b")
            residual("wf", [lambda b: at_block(X, b), lambda b: bias["bf"][:]], X)
            norm("wf", X)

            def project(it):
                for v in range(V):
                    b = V * it + v
                    for i, (w, o) in enumerate((("bq", at_block(Y, b)), ("bk", zrow[:, v, 0:D]),
                                                ("bv", hidT[:, v, 0:KC, :].rearrange("p m n -> p (m n)")))):
                        dve.wait_ge(product_made.sem, product_made.at("qkv", 3 * b + i + 1))
                        if not is_first(it) and i:
                            dve.wait_ge(table_stored[v].sem, table_stored[v].at("qkv", 32 * it))
                        vec.tensor_tensor(o, PS[4 + i][:, 0:D], bias[w][:], ALU.add)\
                            .then_inc(product_copied.sem, 1)
            each(dve, VITERS, project)
            rows_free("qkv")
            logits_dot("L3")
            softmax("L3")
            sum_edges("L3")
            combine("L3")
            residual("ws", [lambda b: at_block(ACC, b)[:, 0:D], lambda b: bias["bs"][:]], ACC3)
            norm("ws", ACC3, bias["g1"], bias["h1"])
            residual("ffn", [lambda b: at_block(ACC3, b), lambda b: bias["bff2"][:]], ACC3)
            norm("ffn", ACC3, bias["g2"], bias["h2"])
            dve.wait_ge(normed.sem, normed.at("ffn", 3 * BLOCKS))
            vec.tensor_tensor(X[:], X[:], ACC3, ALU.add).then_inc(residual_added.sem, 1)
            dve.wait_ge(residual_added.sem, residual_added.at("last", 1))
            norm("last", X)

        @block.tensor
        def _(pe):
            mm = nc.tensor.matmul
            pe.wait_ge(setup_v.sem, STEP_GE_AT)
            for g in range(G):
                last = mm(PS[0][:, 0:STEPS], ones[0:EP, :], step_ge[:, g, :], start=g == 0, stop=g == G - 1)
            last.then_inc(setup_p.sem, 1)
            pe.wait_ge(setup_v.sem, EDGES_AT)
            for i, t in enumerate((srcT, dstT, wT)):
                for g in range(G):
                    last = mm(PS[1 + i][:, 0:STEPS], t[:, g * P:(g + 1) * P], pick[:, g, :],
                              start=g == 0, stop=g == G - 1)
            last.then_inc(setup_p.sem, 1)
            pe.wait_ge(setup_v.sem, DSTM_AT)
            for g in range(G):
                last = nc.tensor.transpose(PS[4][0:SPARTS, g * P:(g + 1) * P], dstM[:, g::G], ident[:])
            last.then_inc(setup_p.sem, 1)
            pe.wait_ge(setup_v.sem, DT_AT)
            mm(PS[5][0:SPARTS, 0:1], up[0:SPARTS, 0:SPARTS], DT[:, ROW - 1:ROW], start=True, stop=True)\
                .then_inc(setup_p.sem, 1)
            pe.wait_ge(setup_v.sem, BREAK_AT)
            mm(PS[5][0:SPARTS, 1:2], down[0:SPARTS, 0:SPARTS], breakF[:, 0:1], start=True, stop=True)\
                .then_inc(setup_p.sem, 1)
            pe.wait_ge(setup_v.sem, SPAN_AT)
            for i in range(2):
                last = mm(PS[6][0:HEADS, i * SPARTS:(i + 1) * SPARTS], brk[:, i, :], ident[0:SPARTS, 0:SPARTS],
                          start=True, stop=True)
            last.then_inc(setup_p.sem, 1)
            pe.wait_ge(setup_v.sem, PLACES_AT)
            for bank, source in ((1, srcF), (3, dlocF)):
                for g in range(G):
                    last = nc.tensor.transpose(PS[bank][0:SPARTS, g * P:(g + 1) * P], source[:, g::G], ident[:])
            last.then_inc(setup_p.sem, 1)
            pe.wait_ge(setup_v.sem, SETUP_V)

            def sum_edges(stage):
                g = SUM_PASS[stage]
                cols = WIDTH[stage] + EXTRAS.get(stage, 0)

                def body(it):
                    for j in range(U):
                        k = U * it + j
                        pe.wait_ge(onehot_made.sem, onehot_made.at(stage, k + 1))
                        if stage in SCALED:
                            pe.wait_ge(row_scaled.sem, row_scaled.at(stage, k + 1))
                            pe.wait_ge(extras_put.sem, extras_put.at(stage, k + 1))
                            moving = R[:, j % 4, 0:cols]
                        else:
                            landed(pe, g, it, j)
                            moving = rows[:, j, 0:cols]
                        if due(k - 3):
                            pe.wait_ge(sum_added.sem, sum_added.at(stage, k - 3))
                        mm(PS[j % 4][:, 0:cols], M[:, j % 4, :], moving, start=True, stop=True)\
                            .then_inc(step_summed.sem, 1)
                each(pe, ITERS, body)

            def logits_gat(stage):
                heads = HEADS_OF[stage]
                n, cols = BLOCKS * heads, PICK * heads
                pe.wait_ge(parts_made.sem, parts_made.at(stage, PARTS_AT))

                def body(it):
                    blocks = load_blocks(pe, it)
                    for s in range(4):
                        c = 4 * it + s
                        pe.wait_ge(lowhot_made.sem, lowhot_made.at(stage, c + 1))
                        if due(c - 3):
                            pe.wait_ge(values_masked.sem, values_masked.at(stage, c - 3))
                        for g in range(G):
                            for i in range(PARTS):
                                mm(PS[s][:, g * cols:g * cols + n], lowhot[:, s % 2, g * P:(g + 1) * P],
                                   partsS[:, i * n:(i + 1) * n], start=i == 0, stop=i == PARTS - 1)
                        pe.wait_ge(dsthot_made.sem, dsthot_made.at(stage, c + 1))
                        for g in range(G):
                            last = mm(PS[s][:, g * cols + n:(g + 1) * cols], dsthot[:, s % 2, g * P:(g + 1) * P],
                                      at_block(partsD[:, 0:PARTS * n].rearrange("p (b c) -> p b c", c=PARTS * heads),
                                               blocks[4 * s + g]), start=True, stop=True)
                        last.then_inc(values_picked.sem, 1)
                each(pe, ITERS, body)

            def logits_dot(stage):
                def body(it):
                    blocks = load_blocks(pe, it)
                    for j in range(U):
                        k = U * it + j
                        if j % G == 0:
                            pe.wait_ge(dsthot_made.sem, dsthot_made.at(stage, 4 * it + j // G + 1))
                        if due(k - 3):
                            pe.wait_ge(logit_made.sem, logit_made.at(stage, k - 3))
                        mm(PS[4 + j % 4][:, 0:D], dsthotF[:, j // G % 2, j % G * P:(j % G + 1) * P],
                           at_block(Y, blocks[j]), start=True, stop=True).then_inc(query_spread.sem, 1)
                each(pe, ITERS, body)

            def softmax(stage):
                heads = HEADS_OF[stage]
                pe.wait_ge(softmax_v.sem, softmax_v.at(stage, LOGITS_AT[stage]))
                for h in range(heads):
                    for g in range(G):
                        last = nc.tensor.transpose(PS[h][0:SPARTS, g * P:(g + 1) * P], LG[:, g::G, h], ident[:])
                last.then_inc(softmax_p.sem, 1)
                pe.wait_ge(softmax_v.sem, softmax_v.at(stage, LOGITS_AT[stage] + heads))
                nc.tensor.transpose(PS[4][0:heads, 0:SPARTS], FT[:, 0:heads, ROW - 1], ident[0:SPARTS, 0:SPARTS])\
                    .then_inc(softmax_p.sem, 1)
                pe.wait_ge(softmax_v.sem, softmax_v.at(stage, LOGITS_AT[stage] + heads + 1))
                nc.tensor.transpose(PS[5][0:SPARTS, 0:heads], carryF[0:heads, 0:SPARTS], ident[0:heads, 0:heads])\
                    .then_inc(softmax_p.sem, 1)
                pe.wait_ge(softmax_v.sem, softmax_v.at(stage, LOGITS_AT[stage] + 3 * heads + 2))
                nc.tensor.transpose(PS[6][0:heads, 0:SPARTS], BT[:, 0:heads, 0], ident[0:SPARTS, 0:SPARTS])\
                    .then_inc(softmax_p.sem, 1)
                pe.wait_ge(softmax_v.sem, softmax_v.at(stage, LOGITS_AT[stage] + 3 * heads + 3))
                nc.tensor.transpose(PS[7][0:SPARTS, 0:heads], carryB[0:heads, 1:SPARTS + 1], ident[0:heads, 0:heads])\
                    .then_inc(softmax_p.sem, 1)
                pe.wait_ge(softmax_a.sem, softmax_a.at(stage, 2))
                for c, source in enumerate(back_columns(stage)):
                    if c >= 4:
                        if due(3 + c - 4):
                            pe.wait_ge(softmax_a.sem, softmax_a.at(stage, 3 + c - 4))
                    if stage in MAXIMA_AT and c == heads:
                        pe.wait_ge(softmax_v.sem, softmax_v.at(stage, MAXIMA_AT[stage]))
                    for g in range(G):
                        last = nc.tensor.transpose(PS[c % 4][:, g * SPARTS:(g + 1) * SPARTS],
                                                   source[:, g * P:(g + 1) * P], ident[0:SPARTS, 0:SPARTS])
                    last.then_inc(softmax_p.sem, 1)

            def turn_in(loop, chunks=KC):
                def turn(b, v):
                    pe.wait_ge(input_staged.sem, input_staged.at(loop, b + 1))
                    if due(b - 1 if v else b):
                        pe.wait_ge(in_copied.sem, in_copied.at(loop, b - 1 if v else b))
                    for k in range(chunks):
                        last = nc.tensor.transpose(PS[v % 2][:, k * P:(k + 1) * P], rows[:, v, k * P:(k + 1) * P], ident[:])
                    last.then_inc(in_turned.sem, 1)
                return turn

            def product(loop, turn, use):
                def body(it):
                    for v in range(V):
                        b = V * it + v
                        if v < V - 1:
                            turn(b + 1, v + 1)
                        elif not is_last(it, VITERS):
                            turn(b + 1, 0)
                        pe.wait_ge(in_copied.sem, in_copied.at(loop, b + 1))
                        use(b, v)
                turn(0, 0)
                each(pe, VITERS, body)

            def linear(loop, weights, cols, chunks, taken, width=P):
                nw = len(weights)

                def use(b, v):
                    for i, w in enumerate(weights):
                        slot = BANK[v] if nw == 1 else i
                        taken(b, v, i)
                        for k in range(chunks):
                            last = mm(PS[4 + slot][:, 0:cols], inT[0:width, v, k, :], w[:, k, 0:cols] if width == P else w,
                                      start=k == 0, stop=k == chunks - 1)
                        last.then_inc(product_made.sem, 1)
                return use

            def hidden(loop, first_w, second_w, mids, taken):
                def use(b, v):
                    if due(b):
                        pe.wait_ge(hidden_acted.sem, hidden_acted.at(loop, b))
                    for m in range(mids):
                        for k in range(KC):
                            last = mm(PS[2][:, m * P:(m + 1) * P], first_w[:, k, m * P:(m + 1) * P],
                                      inT[:, v, k, :], start=k == 0, stop=k == KC - 1)
                    last.then_inc(hidden_made.sem, 1)
                    pe.wait_ge(hidden_acted.sem, hidden_acted.at(loop, b + 1))
                    taken(b, v, 0)
                    for m in range(mids):
                        last = mm(PS[4 + BANK[v]][:, 0:D], hidT[:, v, m, :], second_w[:, m, :],
                                  start=m == 0, stop=m == mids - 1)
                    last.then_inc(product_made.sem, 1)
                return use

            def copied(loop, per):
                return lambda b, v, i: due(per * (b - BANK_AGE[v] + 1)) and pe.wait_ge(product_copied.sem, product_copied.at(loop, per * (b - BANK_AGE[v] + 1)))

            def added(loop):
                return lambda b, v, i: due(2 * (b - BANK_AGE[v] + 1)) and pe.wait_ge(product_added.sem, product_added.at(loop, 2 * (b - BANK_AGE[v] + 1)))

            sum_edges("L0")
            product("mlp", turn_in("mlp"), hidden("mlp", w1, w2, KC, added("mlp")))
            product("z1", turn_in("z1"), linear("z1", [wz1], ZW, KC, copied("z1", 1)))
            pe.wait_ge(product_copied.sem, product_copied.at("z1", BLOCKS))
            logits_gat("L1")
            softmax("L1")
            sum_edges("L1")
            product("z2", turn_in("z2"), linear("z2", [wz2], ZW, KC, copied("z2", 2)))
            pe.wait_ge(product_copied.sem, product_copied.at("z2", 2 * BLOCKS))
            logits_gat("L2a")
            softmax("L2a")
            sum_edges("L2a")
            product("z3", turn_in("z3"), linear("z3", [wz3], HID + 2, KC, copied("z3", 2)))
            pe.wait_ge(product_copied.sem, product_copied.at("z3", 2 * BLOCKS))
            logits_gat("L2b")
            softmax("L2b")
            sum_edges("L2b")
            product("wf", turn_in("wf", 1), linear("wf", [wf[:]], D, 1, added("wf"), width=HID))
            product("qkv", turn_in("qkv"), linear("qkv", [wq, wk, wv], D, KC,
                                                  lambda b, v, i: due(3 * b + i - 2) and pe.wait_ge(product_copied.sem, product_copied.at("qkv", 3 * b + i - 2))))
            pe.wait_ge(product_copied.sem, product_copied.at("qkv", 3 * BLOCKS))
            logits_dot("L3")
            softmax("L3")
            sum_edges("L3")
            product("ws", turn_in("ws"), linear("ws", [ws], D, KC, added("ws")))
            product("ffn", turn_in("ffn"), hidden("ffn", wff1, wff2, FF // P, added("ffn")))

        @block.scalar
        def _(act):
            sc = nc.scalar

            def put_indices(k, half):
                cols = bass.ds(k, HALF)
                sc.activation(idx[:, half, :], srcK[:, cols], ACT.Copy).then_inc(indices_put.sem, 1)

            act.wait_ge(setup_v.sem, SOURCES_AT)
            put_indices(0, 0)
            put_indices(HALF, 1)

            def edge_loop(g, per_step):
                def body(it):
                    for j in range(U):
                        if per_step:
                            per_step(it, j)
                        if j % HALF == HALF - 1:
                            for i in range(j + 1 - HALF, j + 1):
                                landed(act, g, it, i)
                            put_indices(U * it + U + j + 1 - HALF, j // HALF)
                each(act, ITERS, body)

            def sum_edges(stage):
                if stage not in SCALED:
                    edge_loop(SUM_PASS[stage], None)
                    return
                width, extra = WIDTH[stage], EXTRAS[stage]

                def per_step(it, j):
                    k = U * it + j
                    col = bass.ds(k, 1)
                    if due(k - 3):
                        act.wait_ge(step_summed.sem, step_summed.at(stage, k - 3))
                    sc.activation(R[:, j % 4, width:width + extra], PX[:, col, 0:extra].rearrange("p o c -> p (o c)"),
                                  ACT.Copy).then_inc(extras_put.sem, 1)
                edge_loop(SUM_PASS[stage], per_step)

            def logits_gat(stage):
                def distance(it, s):
                    c = 4 * it + s
                    act.wait_ge(spread_landed[s].sem, spread_landed[s].at(stage, 16 * (it + 1)))
                    if due(c - 1):
                        act.wait_ge(dsthot_made.sem, dsthot_made.at(stage, c - 1))
                    sc.activation(apart[:, s % 2, :], spread8[:, s, 1, :], ACT.Abs, bias=minus[:])\
                        .then_inc(dst_apart.sem, 1)

                def body(it):
                    for s in range(4):
                        c = 4 * it + s
                        if s < 3:
                            distance(it, s + 1)
                        elif not is_last(it, ITERS):
                            distance(it + 1, 0)
                        act.wait_ge(dst_apart.sem, dst_apart.at(stage, c + 1))
                        if due(c - 1):
                            act.wait_ge(values_picked.sem, values_picked.at(stage, c - 1))
                        sc.activation(dsthot[:, s % 2, :], apart[:, s % 2, :], ACT.Relu, bias=1.0, scale=-1.0)\
                            .then_inc(dsthot_made.sem, 1)
                distance(0, 0)
                each(act, ITERS, body)

            def softmax(stage):
                heads = HEADS_OF[stage]
                n = [0]

                def step(instruction):
                    n[0] += 1
                    instruction.then_inc(softmax_a.sem, 1)
                act.wait_ge(softmax_p.sem, softmax_p.at(stage, 1))
                for h in range(heads):
                    last = sc.activation(LT[:, h, :], PS[h][0:SPARTS, :], ACT.Copy)
                step(last)
                act.wait_ge(softmax_v.sem, softmax_v.at(stage, SHIFTED_AT[stage]))
                step(sc.activation(LT[:, 0:heads, :], LT[:, 0:heads, :], ACT.Exp))
                for c, _ in enumerate(back_columns(stage)):
                    act.wait_ge(softmax_p.sem, softmax_p.at(stage, 6 + c))
                    step(sc.activation(PX[:, :, c].rearrange("p (q g) -> p g q", g=G),
                                       PS[c % 4][:, 0:STEPS].rearrange("p (g q) -> p g q", g=G), ACT.Copy))
                act.wait_ge(softmax_a.sem, softmax_a.at(stage, n[0]))

            def copy_in(loop, chunks=KC, width=P):
                def copy(b, v):
                    act.wait_ge(in_turned.sem, in_turned.at(loop, b + 1))
                    if due((3 if loop == "qkv" else 1) * (b - V + 1)):
                        act.wait_ge(product_made.sem, product_made.at(loop, (3 if loop == "qkv" else 1) * (b - V + 1)))
                    sc.activation(inT[0:width, v, 0:chunks, :], PS[v % 2][0:width, 0:chunks * P].rearrange("p (k n) -> p k n", k=chunks),
                                  ACT.Copy).then_inc(in_copied.sem, 1)
                return copy

            def node_loop(copy, then=None):
                def body(it):
                    for v in range(V):
                        b = V * it + v
                        if v < V - 1:
                            copy(b + 1, v + 1)
                        elif not is_last(it, VITERS):
                            copy(b + 1, 0)
                        if then:
                            then(b, v, it)
                copy(0, 0)
                each(act, VITERS, body)

            def activate(loop, mids, func, biases):
                def then(b, v, it):
                    act.wait_ge(hidden_made.sem, hidden_made.at(loop, b + 1))
                    if due(b - V + 1):
                        act.wait_ge(product_made.sem, product_made.at(loop, b - V + 1))
                    for m in range(mids):
                        last = sc.activation(hidT[:, v, m, :], PS[2][:, m * P:(m + 1) * P], func, bias=biases[:, m:m + 1])
                    last.then_inc(hidden_acted.sem, 1)
                return then

            def copy_out(loop, cols, tabs, keep):
                def then(b, v, it):
                    act.wait_ge(product_made.sem, product_made.at(loop, b + 1))
                    if not is_first(it):
                        act.wait_ge(table_stored[v].sem, table_stored[v].at(loop, 16 * it))
                    bank = PS[4 + BANK[v]]
                    h = (cols - tabs) // 2
                    sc.activation(at_block(by_head(tabS, h), b), bank[:, tabs:tabs + h], ACT.Copy)
                    sc.activation(at_block(by_head(tabD, h), b), bank[:, tabs + h:cols], ACT.Copy)
                    ins = sc.activation(zrow[:, v, 0:cols], bank[:, 0:cols], ACT.Copy)
                    ins.then_inc(product_copied.sem, 1)
                    if keep:
                        sc.activation(at_block(Y, b)[:, 0:tabs], bank[:, 0:tabs], ACT.Copy).then_inc(product_copied.sem, 1)
                return then

            def combine(stage):
                heads = HEADS_OF[stage]
                act.wait_ge(combined_v.sem, combined_v.at(stage, 7))
                for t in (nodeA, nodeB):
                    sc.activation(t[:, :, 0:heads], t[:, :, 0:heads], ACT.Exp).then_inc(combined_a.sem, 1)

            def root_of(stage):
                act.wait_ge(norm_step.sem, norm_step.at(stage, VARIANCE_AT))
                sc.activation(root[:], rstd[:], ACT.Sqrt).then_inc(norm_root.sem, 1)

            def rows_free(loop):
                for v in range(V):
                    act.wait_ge(table_stored[v].sem, table_stored[v].at(loop, TABLE_LOOPS[loop]))

            edge_loop(0, None)
            act.wait_ge(edges_stored.sem, 16)
            act.wait_ge(weights_in.sem, 16 * len(weight_loads))
            node_loop(copy_in("mlp"), activate("mlp", KC, ACT.Relu, b1c))
            root_of("mlp")
            node_loop(copy_in("z1"), copy_out("z1", ZW, D, False))
            rows_free("z1")
            logits_gat("L1")
            softmax("L1")
            sum_edges("L1")
            root_of("gat")
            node_loop(copy_in("z2"), copy_out("z2", ZW, D, True))
            rows_free("z2")
            logits_gat("L2a")
            softmax("L2a")
            sum_edges("L2a")
            combine("L2a")
            node_loop(copy_in("z3"), copy_out("z3", HID + 2, HID, True))
            rows_free("z3")
            logits_gat("L2b")
            softmax("L2b")
            sum_edges("L2b")
            combine("L2b")
            node_loop(copy_in("wf", 1, HID))
            root_of("wf")
            node_loop(copy_in("qkv"))
            edge_loop(LOGIT_PASS["L3"], None)
            softmax("L3")
            sum_edges("L3")
            node_loop(copy_in("ws"))
            root_of("ws")
            node_loop(copy_in("ffn"), activate("ffn", FF // P, ACT.Gelu_apprx_tanh, bff1c))
            root_of("ffn")
            root_of("last")


INPUTS = ["x", "src", "dst", "edge_weight", "L0_gnn_eps", "L0_gnn_w1", "L0_gnn_b1", "L0_gnn_w2", "L0_gnn_b2",
          "L1_gnn_W", "L1_gnn_att", "L2_gnn_W1", "L2_gnn_att_src1", "L2_gnn_att_dst1", "L2_gnn_b1", "L2_gnn_W2",
          "L2_gnn_att_src2", "L2_gnn_att_dst2", "L2_gnn_b2", "L2_gnn_Wf", "L2_gnn_bf", "L3_gnn_wq", "L3_gnn_bq",
          "L3_gnn_wk", "L3_gnn_bk", "L3_gnn_wv", "L3_gnn_bv", "L3_gnn_ws", "L3_gnn_bs", "L3_gnn_we", "L3_gnn_be",
          "L3_gnn_g1", "L3_gnn_b1", "L3_gnn_g2", "L3_gnn_b2", "L3_gnn_w_ff1", "L3_gnn_b_ff1", "L3_gnn_w_ff2",
          "L3_gnn_b_ff2"]


def kernel(**inputs):
    import concourse.bacc as bacc
    from concourse.bass_utils import run_bass_kernel_spmd

    nc = bacc.Bacc("TRN2", target_bir_lowering=False, num_devices=1)
    arrays, args = {}, []
    for name in INPUTS:
        a = np.ascontiguousarray(inputs[name])
        arrays["in_" + name] = a
        args.append(nc.dram_tensor("in_" + name, a.shape, mybir.dt.from_np(a.dtype), kind="ExternalInput").ap())
    args.append(nc.dram_tensor("result", (N, D), F32, kind="ExternalOutput").ap())
    build(nc, *args)
    ran = run_bass_kernel_spmd(nc, [arrays], core_ids=[0])
    return ran.results[0]["result"]
```

```python
from contextlib import ExitStack

import numpy as np

import concourse.bass as bass
from concourse import mybir

F32 = mybir.dt.float32
I32 = mybir.dt.int32
U8 = mybir.dt.uint8
ALU = mybir.AluOpType
ACT = mybir.ActivationFunctionType
AX = mybir.AxisListType.X

P = 128
N, E, D = 3125, 50000, 256
KC = D // P
BLOCKS = -(-N // P)
FULL = N // P
REST = N - FULL * P
TILES = -(-E // P)
G = 4
EP = -(-TILES // G)
ROW = G * P
EFULL = E // ROW
EREST = E - EFULL * ROW
STEPS = EP * G + BLOCKS - 1
SPARTS = STEPS // G
U = 16
ITERS = STEPS // U
HALF = U // 2
V = 5
VITERS = BLOCKS // V
HEADS, HID = 4, 64
FF = 2 * D
BIG = 1e30
NOWHERE = 255.0
NODST = 4000.0
EPS = 1e-5
ACCW = D + 2 * HEADS + 1
assert STEPS % U == 0 and STEPS % G == 0 and BLOCKS % V == 0 and TILES + BLOCKS - 1 <= STEPS


class Signal:

    def __init__(self, sem, totals):
        self.sem, self.base, total = sem, {}, 0
        for stage, n in totals.items():
            self.base[stage], total = total, total + n

    def at(self, stage, n):
        return self.base[stage] + n


def due(n):
    return not isinstance(n, int) or n > 0


def each(eng, iters, body):
    body(0)
    with eng.Fori(1, iters - 1) as it:
        body(it)
    body(iters - 1)


def flow(eng, iters, width, hops, peeled=1):
    blocks = iters * width

    def body(it):
        for v in range(width):
            for lag, work in hops:
                b = width * it + v - lag
                if not isinstance(b, int) or 0 <= b < blocks:
                    work(b, (v - lag) % width, it + (v - lag) // width)
    for it in range(peeled):
        body(it)
    with eng.Fori(peeled, iters) as it:
        body(it)
    most = max(lag for lag, _ in hops)
    assert most <= width * peeled
    for it in range(iters, iters + -(-most // width)):
        body(it)


def is_last(it, iters):
    return isinstance(it, int) and it == iters - 1


def is_first(it):
    return isinstance(it, int) and it == 0


def build(nc, x, src, dst, edge_weight, L0_gnn_eps, L0_gnn_w1, L0_gnn_b1, L0_gnn_w2, L0_gnn_b2,
          L1_gnn_W, L1_gnn_att, L2_gnn_W1, L2_gnn_att_src1, L2_gnn_att_dst1, L2_gnn_b1, L2_gnn_W2,
          L2_gnn_att_src2, L2_gnn_att_dst2, L2_gnn_b2, L2_gnn_Wf, L2_gnn_bf, L3_gnn_wq, L3_gnn_bq,
          L3_gnn_wk, L3_gnn_bk, L3_gnn_wv, L3_gnn_bv, L3_gnn_ws, L3_gnn_bs, L3_gnn_we, L3_gnn_be,
          L3_gnn_g1, L3_gnn_b1, L3_gnn_g2, L3_gnn_b2, L3_gnn_w_ff1, L3_gnn_b_ff1, L3_gnn_w_ff2,
          L3_gnn_b_ff2, out):
    ctx = ExitStack()
    with ctx:
        def sb(name, shape, dt=F32):
            return ctx.enter_context(nc.sbuf_tensor(name, shape, dt))

        def sem(name):
            return ctx.enter_context(nc.semaphore(name))

        def dram(name, shape):
            return nc.dram_tensor(name, shape, F32, kind="Internal").ap()

        rows_total = BLOCKS * P
        t_z1, t_z2, t_z3 = dram("t_z1", [rows_total, D]), dram("t_z2", [rows_total, D]), dram("t_z3", [rows_total, HID])
        t_kv = dram("t_kv", [rows_total, 2 * D])
        t_breaks = dram("t_breaks", [SPARTS, 2 * ROW])

        X = sb("X", [P, BLOCKS, D])
        ACC = sb("ACC", [P, BLOCKS, ACCW])
        Y = sb("Y", [P, BLOCKS, D])
        Yf = Y[:].rearrange("p b d -> p (b d)")
        srcblock = sb("srcblock", [P, STEPS])
        tabS = sb("tabS", [P, BLOCKS * HEADS])
        tabD = sb("tabD", [P, BLOCKS * HEADS])
        nodeA = sb("nodeA", [P, BLOCKS, HEADS])
        nodeB = sb("nodeB", [P, BLOCKS, HEADS])
        nodeC = sb("nodeC", [P, BLOCKS, HEADS])

        widths = [U * (D + 1), STEPS * (2 * HEADS + 1), STEPS * HEADS]
        edgework = sb("edgework", [P, sum(widths)])
        rows = edgework[:, 0:widths[0]].rearrange("p (j c) -> p j c", j=U)
        PX = edgework[:, widths[0]:widths[0] + widths[1]].rearrange("p (k c) -> p k c", k=STEPS)
        LG = edgework[:, widths[0] + widths[1]:sum(widths)].rearrange("p (k h) -> p k h", k=STEPS)
        kv = edgework[:, 0:U * (2 * D + 1)].rearrange("p (j c) -> p j c", j=U)
        idx = sb("idx", [P, 2, HALF], I32)
        srcK = sb("srcK", [P, STEPS + U], I32)
        dloc = sb("dloc", [P, STEPS])
        wK = sb("wK", [P, STEPS])
        valid = sb("valid", [P, STEPS])
        blockI = sb("blockI", [1, STEPS], I32)
        M = sb("M", [P, 4, P])
        R = sb("R", [P, 4, ACCW])
        apartF = R[:].rearrange("p j c -> p (j c)")[:, 0:2 * ROW].rearrange("p (s j) -> p s j", s=2)
        junk = sb("junk", [P, 2, D])

        rowbuf = sb("rowbuf", [P, 3, HEADS * ROW])
        LT, FT, BT = (rowbuf[0:SPARTS, i, :].rearrange("p (h j) -> p h j", h=HEADS) for i in range(3))
        breakF = sb("breakF", [SPARTS, ROW])
        breakB = sb("breakB", [SPARTS, ROW])
        first = sb("first", [SPARTS, ROW])
        brk = sb("brk", [SPARTS, 2, HEADS])
        spanF = sb("spanF", [HEADS, SPARTS])
        spanB = sb("spanB", [HEADS, SPARTS])
        carryF = sb("carryF", [HEADS, SPARTS + 1])
        carryB = sb("carryB", [HEADS, SPARTS + 1])
        startF = sb("startF", [SPARTS, HEADS])
        startB = sb("startB", [SPARTS, HEADS])
        flat = rowbuf[:].rearrange("p a b -> p (a b)")
        inT = flat[:, 0:V * D].rearrange("p (v k n) -> p v k n", v=V, k=KC)
        hidT = flat[:, V * D:V * (D + FF)].rearrange("p (v m n) -> p v m n", v=V, m=FF // P)
        ZW = D + 2 * HEADS
        keys = flat[:, V * (D + FF):V * (2 * D + FF)].rearrange("p (v c) -> p v c", v=V)
        assert V * (2 * D + FF) <= 3 * HEADS * ROW
        midT = {"L0": hidT[:, :, KC:2 * KC, :], "L2b": hidT[:, :, KC:2 * KC, :],
                "L3": keys.rearrange("p v (k n) -> p v k n", k=KC)}
        values = hidT[:, :, 0:KC, :].rearrange("p v m n -> p v (m n)")

        BF = mybir.dt.bfloat16
        PARTS = 3
        PICK = BLOCKS + PARTS
        place = [0]

        def lay(shape, dt=F32):
            words = int(np.prod(shape)) // (4 // mybir.dt.size(dt))
            v = flat[:, place[0]:place[0] + words]
            place[0] += words
            return v.bitcast(dt) if dt != F32 else v

        spread8 = lay([4, 2, ROW], U8).rearrange("p (s t j) -> p s t j", s=4, t=2)
        lowhot = lay([4, ROW], BF).rearrange("p (s j) -> p s j", s=4)
        apart = lay([2, ROW], BF).rearrange("p (s j) -> p s j", s=2)
        dsthot = lay([4, ROW], BF).rearrange("p (s j) -> p s j", s=4)
        blockhot = lay([2, G, PICK]).rearrange("p (s g b) -> p s g b", s=2, g=G)
        masked = lay([2, G, PICK * HEADS]).rearrange("p (s c) -> p s c", s=2)
        partsS = lay([PARTS * BLOCKS * HEADS], BF)
        partsD = lay([PARTS * BLOCKS * HEADS], BF)
        assert place[0] <= 3 * HEADS * ROW

        place[0] = 4 * 2 * ROW // 4
        dsthotF = lay([2, ROW]).rearrange("p (s j) -> p s j", s=2)
        breaks = lay([2, 2, ROW]).rearrange("p (s t j) -> p s t j", s=2, t=2)
        forward = lay([2, ROW]).rearrange("p (s j) -> p s j", s=2)
        segmax = lay([2, ROW]).rearrange("p (s j) -> p s j", s=2)
        assert place[0] <= 3 * HEADS * ROW
        score = sb("score", [P, 4, G])
        scored = sb("scored", [P, 4, G])
        shifted = sb("shifted", [P, 2, G + 1])
        weight = sb("weight", [P, 2, G + 1])
        minus_weight = sb("minus_weight", [P, 2, G])
        rise = sb("rise", [1, 2])
        begins = sb("begins", [P, SPARTS])
        minus_dloc = wK
        edge_bias = srcblock
        PW = 2 * ROW // 4

        at = [0]

        def temp(parts, words, dt=F32):
            v = Yf[0:parts, at[0]:at[0] + words]
            at[0] += words
            return v.bitcast(dt) if dt != F32 else v

        step_ge = temp(EP, (G + 1) * STEPS).rearrange("p (g k) -> p g k", g=G + 1)
        pick = temp(EP, G * STEPS).rearrange("p (g k) -> p g k", g=G)
        dstT, srcT, wT = temp(EP, ROW), temp(EP, ROW), temp(EP, ROW)
        dstI, srcI = temp(EP, ROW, I32), temp(EP, ROW, I32)
        assert at[0] <= BLOCKS * D
        dstM = LG[:, :, 0]
        stepB = LG[:, :, 1]
        vtmp = LG[:, :, 2]
        FT0 = rowbuf[:, 1, ROW:2 * ROW]
        srcF = LG[:, :, 2]
        dlocF = LG[:, :, 3]
        rowI, partsI = (BT[:, i, :].bitcast(I32) for i in range(2))
        srcblockI = FT0[:, 0:STEPS].bitcast(I32)
        edge8 = BT[:, 2, 0:PW].bitcast(U8).rearrange("p (t j) -> p t j", t=2)
        t_edge8 = nc.dram_tensor("t_edge8", [SPARTS, 2 * ROW], U8, kind="Internal").ap()
        DT = LT[:, 0, :]
        nextI = sb("nextI", [EP, 1], I32)
        brk1 = sb("brk1", [SPARTS, 2])
        maskneg = sb("maskneg", [P, STEPS])
        onePeps = sb("onePeps", [P, 1])
        stat = sb("stat", [P, 3 * V, 6])
        moments = sb("moments", [P, 3 * V, 2])
        variance = sb("variance", [P, 3 * V])
        rstd = sb("rstd", [P, 3 * V])
        minus_half = sb("minus_half", [P, 1])
        BLOCK_SHIFT = P.bit_length() - 1
        tileI = sb("tileI", [EP, G + 1], I32)
        tileC = sb("tileC", [EP, G + 1])

        iota = sb("iota", [P, P])
        stepno = junk[:].rearrange("p a d -> p (a d)")[:, 0:STEPS]
        tileno = sb("tileno", [EP, G + 1])
        minus = sb("minus", [P, 1])
        part = sb("part", [P, 3])
        ident = sb("ident", [P, P])
        up = rowbuf[:, 1, 2 * ROW:2 * ROW + P]
        down = rowbuf[:, 1, 2 * ROW + P:2 * ROW + 2 * P]
        ones = sb("ones", [P, P])

        w1, w2 = sb("w1", [P, KC, D]), sb("w2", [P, KC, D])
        wz1, wz2 = sb("wz1", [P, KC, ZW]), sb("wz2", [P, KC, ZW])
        wz3 = sb("wz3", [P, KC, HID + 2])
        wf = sb("wf", [HID, D])
        wq, wk = sb("wq", [P, KC, D]), sb("wk", [P, KC, D])
        wv, ws = sb("wv", [P, KC, D]), sb("ws", [P, KC, D])
        wff1, wff2 = sb("wff1", [P, KC, FF]), sb("wff2", [P, FF // P, D])
        near = w1[:].rearrange("p k (i n) -> p (k i) n", n=P)
        ACCf = ACC[:].rearrange("p b c -> p (b c)")
        att = ACCf[:, 0:4 * D].rearrange("p (a d) -> p a d", a=4)
        att2 = ACCf[:, 4 * D:4 * D + 2 * HID].rearrange("p (a d) -> p a d", a=2)
        bias = {}
        vectors = [("b2", L0_gnn_b2), ("b3", L2_gnn_b1), ("bf", L2_gnn_bf), ("bq", L3_gnn_bq),
                   ("bk", L3_gnn_bk), ("bv", L3_gnn_bv), ("bs", L3_gnn_bs), ("g1", L3_gnn_g1),
                   ("h1", L3_gnn_b1), ("g2", L3_gnn_g2), ("h2", L3_gnn_b2), ("bff2", L3_gnn_b_ff2),
                   ("b4", L2_gnn_b2)]
        for name, v in vectors:
            bias[name] = sb("v_" + name, [P, v.shape[0]])
        b1c = sb("b1c", [P, KC])
        bff1c = sb("bff1c", [P, FF // P])
        scal = sb("scal", [P, 3])

        PS = [ctx.enter_context(nc.psum_tensor(f"PS{i}", [P, 512], F32)) for i in range(8)]

        def by_chunk(w):
            return w.rearrange("(k p) n -> p k n", p=P)

        weight_loads = [(w1[:], by_chunk(L0_gnn_w1)), (w2[:], by_chunk(L0_gnn_w2)),
                        (b1c[:], L0_gnn_b1.rearrange("(k p) -> p k", p=P)),
                        (bff1c[:], L3_gnn_b_ff1.rearrange("(k p) -> p k", p=P))]
        weight_loads += [(scal[:, c:c + 1], v.partition_broadcast(P))
                         for c, v in enumerate((L0_gnn_eps, L3_gnn_we[0], L3_gnn_be))]
        for h in range(HEADS):
            head = slice(h * HID, (h + 1) * HID)
            weight_loads += [(wz1[:, :, head], by_chunk(L1_gnn_W[h])),
                             (att[:, 0, head], L1_gnn_att[h, 0:HID].partition_broadcast(P)),
                             (att[:, 1, head], L1_gnn_att[h, HID:2 * HID].partition_broadcast(P)),
                             (att[:, 2, head], L2_gnn_att_src1[h].partition_broadcast(P)),
                             (att[:, 3, head], L2_gnn_att_dst1[h].partition_broadcast(P))]
        weight_loads += [(wz2[:, :, 0:D], by_chunk(L2_gnn_W1)), (wz3[:, :, 0:HID], by_chunk(L2_gnn_W2)),
                         (att2[:, 0, :], L2_gnn_att_src2[0].partition_broadcast(P)),
                         (att2[:, 1, :], L2_gnn_att_dst2[0].partition_broadcast(P)), (wf[:], L2_gnn_Wf),
                         (wq[:], by_chunk(L3_gnn_wq)), (wk[:], by_chunk(L3_gnn_wk)),
                         (wv[:], by_chunk(L3_gnn_wv)), (ws[:], by_chunk(L3_gnn_ws)),
                         (wff1[:], by_chunk(L3_gnn_w_ff1)), (wff2[:], by_chunk(L3_gnn_w_ff2))]
        weight_loads += [(bias[name][:], v.partition_broadcast(P)) for name, v in vectors]

        HEADS_OF = {"L1": HEADS, "L2a": HEADS, "L2b": 1, "L3": 1}
        WIDTH = {"L0": D, "L1": D, "L2a": D, "L2b": HID, "L3": D + 1}
        EXTRAS = {"L1": HEADS, "L2a": 2 * HEADS + 1, "L2b": 3}
        SLOPE = {"L1": 0.01, "L2a": 0.2, "L2b": 0.2}
        STEP_GE_AT, EDGES_AT, SOURCES_AT, DSTM_AT, PLACES_AT, DT_AT, BREAK_AT, SPAN_AT, BYTES_AT, SETUP_V = (
            17, 23, 28, 34, 38, 39, 44, 50, 56, 84)
        LOGITS_AT = {"L1": 4, "L2a": 2, "L2b": 2}
        SHIFTED_AT = {s: at + 4 * HEADS_OF[s] + 5 for s, at in LOGITS_AT.items()}
        MAXIMA_AT = {s: SHIFTED_AT[s] + 1 for s in ("L2a", "L2b")}
        SCALES = {"L1": 2, "L2a": 12, "L2b": 12, "L3": 2}
        AGE = [1, 3, 2, 2, 2]
        INPUT, MIDDLE, TERM = 0, V, 2 * V
        assert 3 * V <= U
        PARTS_AT = 2 * (2 * PARTS - 1)
        LOWHOTS = {"L1": 3, "L2a": 3, "L2b": 2}
        QUERY_BANK, SUM_BANK, FREED = [3, 4, 5, 6], [0, 1, 7, 0], [0, -2, -1, 1]

        def back_columns(stage):
            heads = HEADS_OF[stage]
            cols = [LT[:, h, :] for h in range(heads)]
            if stage in MAXIMA_AT:
                cols += [FT[:, h, :] for h in range(heads)] + [first[:]]
            return cols

        def at_block(buf, b):
            return buf[:, bass.ds(b, 1), :].rearrange("p o c -> p (o c)")

        def by_head(table, heads):
            return table[:, 0:BLOCKS * heads].rearrange("p (b h) -> p b h", h=heads)

        def load_blocks(eng, it):
            k = U * it
            _, values = nc.values_load_multi_w_load_instructions(
                blockI[0:1, bass.ds(k, U)], engines=(eng.engine,), min_val=0, max_val=BLOCKS - 1,
                skip_runtime_bounds_check_because="the table was clamped to the blocks")
            return values

        def signal(name, totals):
            return Signal(ctx.enter_context(nc.semaphore(name)), totals)

        def each_of(stages, n):
            return {s: n for s in stages}

        SUMMING = ["L0", "L1", "L2a", "L2b", "L3"]
        SCALED = ["L1", "L2a", "L2b"]
        GAT = ["L1", "L2a", "L2b"]
        CHUNKS = SPARTS
        LAYERS = ["L0", "L1", "L2a", "L2b", "L3"]
        DEEP = ["L0", "L2b", "L3"]
        NORMS = {"L0": ("mlp",), "L1": ("gat",), "L2b": ("self",), "L3": ("attended", "fed", "last")}
        NORM_PLACE = {n: V * i for names in NORMS.values() for i, n in enumerate(names)}

        edges_padded = signal("edges_padded", {"setup": 1})
        edges_in = signal("edges_in", {"setup": 16 * 8})
        features_in = signal("features_in", {"setup": 32})
        weights_in = signal("weights_in", {"setup": 0})
        consts_made = signal("consts_made", {"setup": 7})
        setup_v = signal("setup_v", {"setup": 0})
        setup_p = signal("setup_p", {"setup": 0})
        indices_put = signal("indices_put", {"all": 0})
        slot_opened = signal("slot_opened", {"all": 0})
        wait_carried = signal("wait_carried", {"all": 0})
        pool_wait_carried = signal("pool_wait_carried", {"all": 0})
        half_opened = signal("half_opened", {"all": 0})
        row_landed = [signal(f"row_landed{j}", {"all": 0}) for j in range(U)]
        sums_zeroed = signal("sums_zeroed", each_of(SUMMING, 1))
        onehot_made = signal("onehot_made", each_of(SUMMING, STEPS))
        row_scaled = signal("row_scaled", each_of(SCALED, STEPS))
        extras_put = signal("extras_put", each_of(SCALED, STEPS))
        step_summed = signal("step_summed", each_of(SUMMING, STEPS))
        sum_added = signal("sum_added", each_of(SUMMING, STEPS))
        spread_landed = [signal(f"spread_landed{i}", each_of(GAT + ["L3"], 16 * ITERS)) for i in range(4)]
        lowhot_made = [signal(f"lowhot_made{i}", each_of(GAT, ITERS)) for i in range(4)]
        dst_apart = signal("dst_apart", each_of(GAT + ["L3"], CHUNKS))
        dsthot_made = signal("dsthot_made", each_of(GAT + ["L3"], CHUNKS))
        values_picked = signal("values_picked", each_of(GAT, CHUNKS))
        blockhot_made = signal("blockhot_made", each_of(GAT, CHUNKS + 1))
        values_masked = signal("values_masked", each_of(GAT, CHUNKS))
        parts_made = signal("parts_made", each_of(GAT, PARTS_AT))
        query_spread = signal("query_spread", {"L3": STEPS})
        logit_made = signal("logit_made", each_of(GAT, CHUNKS) | {"L3": STEPS})
        edges_stored = signal("edges_stored", {"setup": 16 * 3})
        breaks_landed = [signal(f"breaks_landed{i}", {"L3": 16 * CHUNKS // 2}) for i in range(2)]
        ends_set = signal("ends_set", {"L3": 1})
        bias_made = signal("bias_made", {"L3": 5})
        near_made = signal("near_made", {"L3": STEPS})
        weights_negated = signal("weights_negated", {"L3": CHUNKS})
        begins_spread = signal("begins_spread", {"L3": 1})
        scores_ready = signal("scores_ready", {"L3": CHUNKS})
        scores_turned = signal("scores_turned", {"L3": CHUNKS})
        forward_made = signal("forward_made", {"L3": CHUNKS})
        segmax_made = signal("segmax_made", {"L3": CHUNKS})
        rise_made = signal("rise_made", {"L3": CHUNKS})
        maxima_turned = signal("maxima_turned", {"L3": CHUNKS})
        scores_shifted = signal("scores_shifted", {"L3": 2 * CHUNKS})
        weights_made = signal("weights_made", {"L3": CHUNKS})
        softmax_v = signal("softmax_v", {s: MAXIMA_AT.get(s, SHIFTED_AT[s]) for s in GAT})
        softmax_p = signal("softmax_p", {s: 5 + len(back_columns(s)) for s in GAT})
        softmax_a = signal("softmax_a", {s: 2 + len(back_columns(s)) for s in GAT})
        scales_made = signal("scales_made", SCALES)
        scales_exp = signal("scales_exp", each_of(("L2a", "L2b"), 2))
        term_made = signal("term_made", each_of(LAYERS, BLOCKS))
        sums_scaled = signal("sums_scaled", each_of(("L2a", "L2b", "L3"), BLOCKS))
        loop_added = signal("loop_added", each_of(("L2a", "L2b"), BLOCKS))
        bias_added = signal("bias_added", {"L2a": BLOCKS})
        input_ready = signal("input_ready", each_of(LAYERS, BLOCKS))
        in_turned = signal("in_turned", each_of(LAYERS, BLOCKS))
        in_copied = signal("in_copied", each_of(LAYERS, BLOCKS))
        branch_made = signal("branch_made", each_of(DEEP, BLOCKS))
        middle_ready = signal("middle_ready", each_of(DEEP, BLOCKS))
        mid_turned = signal("mid_turned", each_of(DEEP, BLOCKS))
        mid_copied = signal("mid_copied", each_of(DEEP, BLOCKS))
        hidden_made = signal("hidden_made", each_of(("L0", "L3"), BLOCKS))
        hidden_acted = signal("hidden_acted", each_of(("L0", "L3"), BLOCKS))
        fed_made = signal("fed_made", {"L3": BLOCKS})
        fed_term_made = signal("fed_term_made", {"L3": BLOCKS})
        last_term_made = signal("last_term_made", {"L3": BLOCKS})
        projected = signal("projected", {"L0": BLOCKS, "L1": BLOCKS, "L2a": BLOCKS, "L2b": 3 * BLOCKS})
        projection_copied = signal("projection_copied", {"L0": BLOCKS, "L1": BLOCKS, "L2a": BLOCKS, "L2b": 3 * BLOCKS})
        norms_of = {}
        for layer, names in NORMS.items():
            for name in names:
                norms_of[name] = {what: signal(f"{name}_{what}", {name: BLOCKS}) for what in
                                  ("summed", "stats", "moments", "variance", "rstd", "centred")}
        kept = signal("kept", each_of(("L0", "L1", "L2b", "L3"), BLOCKS))
        TABLES = {"L0": 1, "L1": 1, "L2a": 1, "L2b": 2}
        TABLE_LOOPS = {s: 16 * n * VITERS for s, n in TABLES.items()}
        table_stored = [signal(f"table_stored{v}", TABLE_LOOPS) for v in range(V)]
        out_stored = signal("out_stored", {"out": 16 * BLOCKS})

        PASSES = [(x, D, None, step_summed, "L0"), (t_z1, D, "L0", row_scaled, "L1"),
                  (t_z2, D, "L1", row_scaled, "L2a"), (t_z3, HID, "L2a", row_scaled, "L2b"),
                  (t_kv, 2 * D, "L2b", step_summed, "L3")]
        SUM_PASS = {"L0": 0, "L1": 1, "L2a": 2, "L2b": 3, "L3": 4}

        def landed(eng, g, it, j):
            eng.wait_ge(row_landed[j].sem, 16 * (ITERS * g + 1) + 16 * it)

        block = ctx.enter_context(nc.Block())

        @block.gpsimd
        def _(pool):
            for t, pattern, base, mult in (
                    (iota[:], [[1, P]], 0, 0), (stepno, [[1, STEPS]], 0, 0), (tileno[:], [[1, G + 1]], 0, G),
                    (part[:, 0:1], [[0, 1]], 0, 1), (part[:, 1:2], [[0, 1]], 1, 1), (part[:, 2:3], [[0, 1]], -1, 1),
                    (minus[:], [[0, 1]], 0, -1)):
                nc.gpsimd.iota(t, pattern, base=base, channel_multiplier=mult,
                               allow_small_or_imprecise_dtypes=True).then_inc(consts_made.sem, 1)
            def zero_sums():
                nc.gpsimd.memset(ACC[:], 0.0).then_inc(sums_zeroed.sem, 1)

            def power(name):
                sig = norms_of[name]

                def work(b, v, r):
                    i = NORM_PLACE[name] + v
                    pool.wait_ge(sig["variance"].sem, sig["variance"].at(name, b + 1))
                    nc.gpsimd.tensor_tensor(rstd[:, i:i + 1], variance[:, i:i + 1], minus_half[:], ALU.pow)\
                        .then_inc(sig["rstd"].sem, 1)
                return work

            def mlp_term(b, v, r):
                if due(b - V + 1):
                    sig = norms_of["mlp"]["summed"]
                    pool.wait_ge(sig.sem, sig.at("mlp", b - V + 1))
                nc.gpsimd.tensor_tensor(rows[:, TERM + v, 0:D], at_block(X, b), bias["b2"][:], ALU.add)\
                    .then_inc(term_made.sem, 1)

            def keep(layer):
                def work(b, v, r):
                    pool.wait_ge(middle_ready.sem, middle_ready.at(layer, b + 1))
                    pool.sem_inc(pool_wait_carried.sem, 1)
                    nc.gpsimd.tensor_copy(at_block(X, b), rows[:, MIDDLE + v, 0:D]).then_inc(kept.sem, 1)
                return work

            def scale_sums(b, v, r):
                nc.gpsimd.tensor_tensor(
                    at_block(ACC, b)[:, 0:D].rearrange("p (h f) -> p h f", h=HEADS),
                    at_block(ACC, b)[:, 0:D].rearrange("p (h f) -> p h f", h=HEADS),
                    at_block(nodeA, b).unsqueeze(2).to_broadcast([P, HEADS, HID]), ALU.mult).then_inc(term_made.sem, 1)

            def scale_loops(b, v, r):
                y = at_block(Y, b).rearrange("p (h f) -> p h f", h=HEADS)
                nc.gpsimd.tensor_tensor(y, y, at_block(nodeB, b).unsqueeze(2).to_broadcast([P, HEADS, HID]),
                                        ALU.mult).then_inc(term_made.sem, 1)

            def self_term(b, v, r):
                nc.gpsimd.tensor_tensor(at_block(X, b), at_block(X, b), bias["bf"][:], ALU.add)\
                    .then_inc(term_made.sem, 1)

            def attended_term(b, v, r):
                nc.gpsimd.tensor_tensor(at_block(Y, b), at_block(X, b), bias["bs"][:], ALU.add)\
                    .then_inc(term_made.sem, 1)

            def last_term(b, v, r):
                pool.wait_ge(input_ready.sem, input_ready.at("L3", b + 1))
                pool.sem_inc(pool_wait_carried.sem, 1)
                nc.gpsimd.tensor_tensor(at_block(X, b), at_block(X, b), bias["h2"][:], ALU.add)\
                    .then_inc(last_term_made.sem, 1)

            def fed_term(b, v, r):
                pool.wait_ge(middle_ready.sem, middle_ready.at("L3", b + 1))
                if due(b - V + 1):
                    sig = norms_of["fed"]["summed"]
                    pool.wait_ge(sig.sem, sig.at("fed", b - V + 1))
                nc.gpsimd.tensor_tensor(rows[:, TERM + v, 0:D], rows[:, MIDDLE + v, 0:D], bias["bff2"][:], ALU.add)\
                    .then_inc(fed_term_made.sem, 1)

            def lowhots(stage):
                def work(c, s, r):
                    if s >= LOWHOTS[stage]:
                        return
                    pool.wait_ge(spread_landed[s].sem, spread_landed[s].at(stage, 16 * (r + 1)))
                    if due(c - 3):
                        pool.wait_ge(values_picked.sem, values_picked.at(stage, c - 3))
                    pool.sem_inc(pool_wait_carried.sem, 1)
                    nc.gpsimd.tensor_scalar(lowhot[:, s, :], spread8[:, s, 0, :], part[:, 0:1], None, ALU.is_equal)\
                        .then_inc(lowhot_made[s].sem, 1)
                flow(pool, ITERS, 4, [(0, work)])

            def gather(g):
                table, width, writer, used, stage = PASSES[g]
                if writer:
                    for v in range(V):
                        pool.wait_ge(table_stored[v].sem, table_stored[v].at(writer, TABLE_LOOPS[writer]))
                    if writer in NORMS:
                        pool.wait_ge(kept.sem, kept.at(writer, BLOCKS))

                slots = kv if stage == "L3" else rows
                lot = G if stage == "L3" else HALF
                if stage == "L3":
                    nc.gpsimd.memset(kv[:, :, 2 * D:2 * D + 1], 1.0).then_inc(ends_set.sem, 1)
                    pool.wait_ge(ends_set.sem, 1)

                def body(it):
                    for j in range(U):
                        if j % lot == 0:
                            if not is_first(it):
                                pool.wait_ge(used.sem, used.at(stage, U * it - U + j + lot))
                            elif g:
                                _, _, _, before, before_stage = PASSES[g - 1]
                                pool.wait_ge(before.sem, before.at(before_stage, STEPS - U + j + lot))
                            if j % HALF == 0:
                                pool.wait_ge(indices_put.sem, 2 * ITERS * g + j // HALF + 1 + 2 * it)
                            pool.sem_inc(half_opened.sem, 1)
                        pool.indirect_dma_start(
                            out=slots[:, j, 0:width], out_offset=None, in_=table[:, :],
                            in_offset=bass.IndirectOffsetOnAxis(
                                ap=idx[:, j // HALF, j % HALF:j % HALF + 1], axis=0)).then_inc(row_landed[j].sem, 16)
                each(pool, ITERS, body)

            gather(0)
            pool.wait_ge(sum_added.sem, sum_added.at("L0", STEPS))
            pool.wait_ge(features_in.sem, 32)
            pool.wait_ge(weights_in.sem, 16 * len(weight_loads))
            flow(pool, VITERS, V, [(0, mlp_term), (3, power("mlp")), (5, keep("L0"))], 2)
            lowhots("L1")
            pool.wait_ge(input_ready.sem, input_ready.at("L0", BLOCKS))
            zero_sums()
            gather(1)
            pool.wait_ge(scales_made.sem, scales_made.at("L1", SCALES["L1"]))
            flow(pool, VITERS, V, [(0, scale_sums), (1, power("gat"))])
            lowhots("L2a")
            pool.wait_ge(kept.sem, kept.at("L1", BLOCKS))
            zero_sums()
            gather(2)
            pool.wait_ge(scales_made.sem, scales_made.at("L2a", SCALES["L2a"]))
            flow(pool, VITERS, V, [(0, scale_loops)])
            lowhots("L2b")
            pool.wait_ge(input_ready.sem, input_ready.at("L2a", BLOCKS))
            zero_sums()
            gather(3)
            flow(pool, VITERS, V, [(0, self_term), (2, power("self")), (4, keep("L2b"))])
            gather(4)
            pool.wait_ge(sum_added.sem, sum_added.at("L3", STEPS))
            flow(pool, VITERS, V, [(0, attended_term), (1, power("attended")), (5, power("fed")), (6, power("last")),
                                   (1, last_term), (2, fed_term)], 2)

        @block.sync
        def _(sp):
            sp.wait_ge(edges_padded.sem, edges_padded.at("setup", 1))
            for tile, vec in ((dstI, dst), (srcI, src), (wT, edge_weight)):
                sp.dma_start(tile[0:EFULL, :], vec[0:EFULL * ROW].rearrange("(p j) -> p j", j=ROW))\
                    .then_inc(edges_in.sem, 16)
                sp.dma_start(tile[EFULL:EFULL + 1, 0:EREST],
                             vec[EFULL * ROW:E].rearrange("(o j) -> o j", o=1)).then_inc(edges_in.sem, 16)
            sp.dma_start(nextI[0:EFULL - 1, :], dst[ROW:EFULL * ROW].rearrange("(p j) -> p j", j=ROW)[:, 0:1],
                         allow_slow_non_contiguous=True).then_inc(edges_in.sem, 16)
            sp.dma_start(nextI[EFULL - 1:EFULL, :], dst[EFULL * ROW:EFULL * ROW + 1].rearrange("(o j) -> o j", o=1))\
                .then_inc(edges_in.sem, 16)
            sp.dma_start(X[:, 0:FULL, :], x[0:FULL * P, :].rearrange("(b p) d -> p b d", p=P))\
                .then_inc(features_in.sem, 16)
            sp.dma_start(X[0:REST, FULL, :], x[FULL * P:N, :]).then_inc(features_in.sem, 16)

            for tile, source in weight_loads:
                sp.dma_start(tile, source, allow_slow_non_contiguous=True).then_inc(weights_in.sem, 16)

            def store(layer, parts, copies):
                def work(b, v, r):
                    sp.wait_ge(projection_copied.sem, projection_copied.at(layer, copies * (b + 1)))
                    for table, rows_of in parts:
                        sp.dma_start(table[bass.ds(b * P, P), :], rows_of(b, v)).then_inc(table_stored[v].sem, 16)
                flow(sp, VITERS, V, [(0, work)])

            def spread_edges(stage):
                def body(it):
                    for s in range(4):
                        c = 4 * it + s
                        if due(c - 3):
                            sp.wait_ge(lowhot_made[s].sem, lowhot_made[s].at(stage, it))
                            sp.sem_inc(slot_opened.sem, 1)
                            sp.wait_ge(dsthot_made.sem, dsthot_made.at(stage, c - 3))
                            sp.sem_inc(slot_opened.sem, 1)
                        sp.dma_start(spread8[:, s, :, :].rearrange("p t j -> p (t j)"),
                                     t_edge8[bass.ds(c, 1), :].rearrange("o j -> (o j)").partition_broadcast(P))\
                            .then_inc(spread_landed[s].sem, 16)
                each(sp, ITERS, body)

            sp.wait_ge(setup_v.sem, BYTES_AT)
            sp.dma_start(t_edge8[:, :], edge8.rearrange("p t j -> p (t j)")).then_inc(edges_stored.sem, 16)
            sp.dma_start(t_breaks[:, 0:ROW], breakF[:]).then_inc(edges_stored.sem, 16)
            sp.dma_start(t_breaks[:, ROW:2 * ROW], breakB[:]).then_inc(edges_stored.sem, 16)
            sp.wait_ge(edges_stored.sem, 16 * 3)
            store("L0", [(t_z1, lambda b, v: at_block(Y, b))], 1)
            spread_edges("L1")
            store("L1", [(t_z2, lambda b, v: at_block(Y, b))], 1)
            spread_edges("L2a")
            store("L2a", [(t_z3, lambda b, v: at_block(Y, b)[:, 0:HID])], 1)
            spread_edges("L2b")
            store("L2b", [(t_kv[:, 0:D], lambda b, v: keys[:, v, :]),
                          (t_kv[:, D:2 * D], lambda b, v: values[:, v, :])], 3)
            for v in range(V):
                sp.wait_ge(table_stored[v].sem, table_stored[v].at("L2b", TABLE_LOOPS["L2b"]))

            def spread_bytes(c, s, r):
                if due(c - 3):
                    sp.wait_ge(dsthot_made.sem, dsthot_made.at("L3", c - 3))
                    sp.sem_inc(slot_opened.sem, 1)
                sp.dma_start(spread8[:, s, :, :].rearrange("p t j -> p (t j)"),
                             t_edge8[bass.ds(c, 1), :].rearrange("o j -> (o j)").partition_broadcast(P))\
                    .then_inc(spread_landed[s].sem, 16)

            def load_breaks(c, s, r):
                if due(c - 1):
                    sp.wait_ge(segmax_made.sem, segmax_made.at("L3", c - 1))
                    sp.sem_inc(slot_opened.sem, 1)
                sp.dma_start(breaks[0:1, s % 2, :, :].rearrange("p t j -> p (t j)"), t_breaks[bass.ds(c, 1), :])\
                    .then_inc(breaks_landed[s % 2].sem, 16)
            flow(sp, ITERS, 4, [(0, spread_bytes), (2, load_breaks)])

            def store_out(b, v, r):
                sp.wait_ge(kept.sem, kept.at("L3", b + 1))
                if isinstance(b, int) and b == FULL:
                    sp.dma_start(out[FULL * P:N, :], X[0:REST, FULL, :]).then_inc(out_stored.sem, 16)
                else:
                    sp.dma_start(out[bass.ds(b * P, P), :], at_block(X, b)).then_inc(out_stored.sem, 16)
            flow(sp, VITERS, V, [(1, store_out)])
            sp.wait_ge(out_stored.sem, 16 * BLOCKS)

        @block.vector
        def _(dve):
            vec = nc.vector
            done = [0]

            def step(instruction):
                done[0] += 1
                instruction.then_inc(setup_v.sem, 1)
                return done[0]

            def settled():
                dve.wait_ge(setup_v.sem, done[0])

            vec.memset(dstI, int(NODST))
            vec.memset(srcI, 0)
            vec.memset(wT, 0.0)
            vec.memset(X[:, FULL, :], 0.0)
            vec.memset(nextI[:], int(NODST)).then_inc(edges_padded.sem, 1)
            step(vec.memset(rows[:, :, D:D + 1], 1.0))
            step(vec.memset(ones[:], 1.0))
            step(vec.memset(minus_half[:], -0.5))
            step(vec.memset(carryF[:], -BIG))
            step(vec.memset(carryB[:], -BIG))
            dve.wait_ge(consts_made.sem, consts_made.at("setup", 7))
            step(vec.tensor_scalar(ident[:], iota[:], part[:, 0:1], None, ALU.is_equal))
            step(vec.tensor_scalar(up, iota[:], part[:, 1:2], None, ALU.is_equal))
            step(vec.tensor_scalar(down, iota[:], part[:, 2:3], None, ALU.is_equal))

            dve.wait_ge(edges_in.sem, 16 * 8)
            step(vec.tensor_scalar(tileI[:, 0:G], dstI[:, ::P], BLOCK_SHIFT, None, ALU.arith_shift_right))
            step(vec.tensor_scalar(tileI[:, G:G + 1], nextI[:], BLOCK_SHIFT, None, ALU.arith_shift_right))
            settled()
            step(vec.tensor_tensor(tileC[:], tileI[:], tileno[:], ALU.add))
            settled()
            step(vec.memset(tileC[0:1, 0:1], 0.0))
            settled()
            for g in range(G + 1):
                step(vec.tensor_scalar(step_ge[:, g, :], stepno[0:EP, :], tileC[:, g:g + 1], None, ALU.is_ge))
            settled()
            assert done[0] == STEP_GE_AT
            for g in range(G):
                step(vec.tensor_tensor(pick[:, g, :], step_ge[:, g, :], step_ge[:, g + 1, :], ALU.subtract))
            step(vec.tensor_copy(dstT, dstI))
            step(vec.tensor_copy(srcT, srcI))
            assert done[0] == EDGES_AT
            dve.wait_ge(setup_p.sem, 1)
            step(vec.scalar_tensor_tensor(stepB, PS[0][:, 0:STEPS], -1.0, stepno, ALU.mult, ALU.add))
            settled()
            step(vec.tensor_scalar(stepB, stepB, 1.0, None, ALU.add))
            settled()
            step(vec.tensor_scalar(blockI[:], stepB[0:1, :], float(BLOCKS - 1), None, ALU.min))
            dve.wait_ge(setup_p.sem, 2)
            step(vec.tensor_copy(srcK[:, 0:STEPS], PS[1][:, 0:STEPS]))
            step(vec.tensor_copy(srcK[:, STEPS:STEPS + U], PS[1][:, 0:U]))
            assert done[0] == SOURCES_AT
            step(vec.scalar_tensor_tensor(dloc[:], stepB, -float(P), PS[2][:, 0:STEPS], ALU.mult, ALU.add))
            settled()
            step(vec.tensor_copy(wK[:], PS[3][:, 0:STEPS]))
            step(vec.tensor_scalar(vtmp, dloc[:], 0.0, None, ALU.is_ge))
            settled()
            step(vec.scalar_tensor_tensor(valid[:], dloc[:], float(P), vtmp, ALU.is_lt, ALU.mult))
            settled()
            step(vec.tensor_tensor(vtmp, PS[2][:, 0:STEPS], valid[:], ALU.mult))
            settled()
            step(vec.scalar_tensor_tensor(dstM, valid[:], -1.0, vtmp, ALU.add, ALU.add))
            assert done[0] == DSTM_AT
            settled()
            step(vec.tensor_copy(srcF, PS[1][:, 0:STEPS]))
            step(vec.tensor_tensor(dlocF, dloc[:], valid[:], ALU.mult))
            settled()
            step(vec.scalar_tensor_tensor(dlocF, valid[:], -NOWHERE, dlocF, ALU.mult, ALU.add))
            settled()
            step(vec.tensor_scalar(dlocF, dlocF, NOWHERE, None, ALU.add))
            assert done[0] == PLACES_AT
            dve.wait_ge(setup_p.sem, 3)
            step(vec.tensor_copy(DT, PS[4][0:SPARTS, :]))
            assert done[0] == DT_AT
            settled()
            same = FT[:, 0, :]
            step(vec.tensor_tensor(same[:, 1:ROW], DT[:, 1:ROW], DT[:, 0:ROW - 1], ALU.is_equal))
            dve.wait_ge(setup_p.sem, 4)
            step(vec.tensor_tensor(same[:, 0:1], DT[:, 0:1], PS[5][0:SPARTS, 0:1], ALU.is_equal))
            settled()
            step(vec.memset(same[0:1, 0:1], 0.0))
            settled()
            step(vec.tensor_scalar(breakF[:], same, -1.0, BIG, ALU.add, ALU.mult))
            step(vec.tensor_scalar(first[:], same, -1.0, 1.0, ALU.mult, ALU.add))
            settled()
            assert done[0] == BREAK_AT
            step(vec.tensor_copy(breakB[:, 0:ROW - 1], breakF[:, 1:ROW]))
            dve.wait_ge(setup_p.sem, 5)
            step(vec.tensor_copy(breakB[:, ROW - 1:ROW], PS[5][0:SPARTS, 1:2]))
            settled()
            step(vec.tensor_reduce(brk1[:, 0:1], breakF[:], AX, ALU.add))
            step(vec.tensor_reduce(brk1[:, 1:2], breakB[:], AX, ALU.add))
            settled()
            for i in range(2):
                step(vec.tensor_copy(brk[:, i, :], brk1[:, i:i + 1].to_broadcast([SPARTS, HEADS])))
            assert done[0] == SPAN_AT
            dve.wait_ge(setup_p.sem, 6)
            step(vec.tensor_copy(spanF[:], PS[6][0:HEADS, 0:SPARTS]))
            step(vec.tensor_copy(spanB[:], PS[6][0:HEADS, SPARTS:2 * SPARTS]))
            dve.wait_ge(setup_p.sem, 7)
            step(vec.tensor_copy(rowI, PS[1][0:SPARTS, :]))
            step(vec.tensor_copy(edge8[:, 1, :], PS[3][0:SPARTS, :]))
            settled()
            step(vec.tensor_scalar(partsI, rowI, P - 1, None, ALU.bitwise_and))
            settled()
            step(vec.tensor_copy(edge8[:, 0, :], partsI))
            assert done[0] == BYTES_AT
            step(vec.tensor_scalar(srcblockI, srcK[:, 0:STEPS], BLOCK_SHIFT, None, ALU.arith_shift_right))
            settled()
            step(vec.tensor_copy(srcblock[:], srcblockI))
            dve.wait_ge(weights_in.sem, 16 * len(weight_loads))
            for wz, a0 in ((wz1, 0), (wz2, 2)):
                for which in range(2):
                    settled()
                    for k in range(KC):
                        step(vec.tensor_tensor(junk[:, k, :], wz[:, k, 0:D], att[:, a0 + which, :], ALU.mult))
                    settled()
                    for k in range(KC):
                        step(vec.tensor_reduce(wz[:, k, D + which * HEADS:D + (which + 1) * HEADS],
                                               junk[:, k, :].rearrange("p (h f) -> p h f", h=HEADS), AX, ALU.add))
            for which in range(2):
                settled()
                for k in range(KC):
                    step(vec.tensor_tensor(junk[:, k, 0:HID], wz3[:, k, 0:HID], att2[:, which, :], ALU.mult))
                settled()
                for k in range(KC):
                    step(vec.tensor_reduce(wz3[:, k, HID + which:HID + which + 1], junk[:, k, 0:HID], AX, ALU.add))
            step(vec.tensor_scalar(maskneg[:], valid[:], -1.0, BIG, ALU.add, ALU.mult))
            step(vec.tensor_scalar(onePeps[:], scal[:, 0:1], 1.0, None, ALU.add))
            settled()
            assert done[0] == SETUP_V

            def sum_edges(stage):
                width = WIDTH[stage]
                scaled = stage in SCALED
                heads = HEADS_OF.get(stage, 1)
                cols = width + EXTRAS.get(stage, 0)
                g = SUM_PASS[stage]
                if stage == "L0":
                    vec.memset(ACC[:], 0.0).then_inc(sums_zeroed.sem, 1)

                def prepare(it, j):
                    k = U * it + j
                    col = bass.ds(k, 1)
                    if due(k - 3):
                        dve.wait_ge(step_summed.sem, step_summed.at(stage, k - 3))
                    if scaled:
                        vec.tensor_scalar(M[:, j % 4, :], iota[:], dloc[:, col], None, ALU.is_equal)\
                            .then_inc(onehot_made.sem, 1)
                        landed(dve, g, it, j)
                        vec.tensor_tensor(
                            R[:, j % 4, 0:width].rearrange("p (h f) -> p h f", h=heads),
                            rows[:, j, 0:width].rearrange("p (h f) -> p h f", h=heads),
                            PX[:, col, 0:heads].rearrange("p o h -> p (o h)").unsqueeze(2).to_broadcast([P, heads, width // heads]),
                            ALU.mult).then_inc(row_scaled.sem, 1)
                    else:
                        vec.tensor_scalar(M[:, j % 4, :], iota[:], dloc[:, col], wK[:, col], ALU.is_equal, ALU.mult)\
                            .then_inc(onehot_made.sem, 1)

                def add(k, j, b):
                    dve.wait_ge(step_summed.sem, step_summed.at(stage, k + 1))
                    if due(k):
                        dve.wait_ge(sum_added.sem, sum_added.at(stage, k))
                    a = ACC[:, bass.ds(b, 1), 0:cols].rearrange("p o c -> p (o c)")
                    vec.tensor_tensor(a, a, PS[j % 4][:, 0:cols], ALU.add).then_inc(sum_added.sem, 1)

                prepare(0, 0)
                dve.wait_ge(sums_zeroed.sem, sums_zeroed.at(stage, 1))

                def body(it):
                    blocks = load_blocks(dve, it)
                    for j in range(U):
                        if j < U - 1:
                            prepare(it, j + 1)
                        elif not is_last(it, ITERS):
                            prepare(it + 1, 0)
                        add(U * it + j, j, blocks[j])
                each(dve, ITERS, body)

            def logits_gat(stage):
                heads = HEADS_OF[stage]
                n = BLOCKS * heads
                before = {"L1": "L0", "L2a": "L1", "L2b": "L2a"}[stage]
                dve.wait_ge(projection_copied.sem, projection_copied.at(before, BLOCKS))
                vec.memset(blockhot[:, :, :, BLOCKS:PICK], 1.0).then_inc(blockhot_made.sem, 1)
                made = 0
                for tab, parts in ((tabS, lambda i: partsS[:, i * n:(i + 1) * n]),
                                   (tabD, lambda i: partsD[:, 0:PARTS * n].rearrange(
                                       "p (b c h) -> p c b h", c=PARTS, h=heads)[:, i, :, :])):
                    rest = nodeA[:].rearrange("p b h -> p (b h)")[:, 0:n]
                    left = tab[:, 0:n]
                    for i in range(PARTS):
                        shaped = left if tab is tabS else left.rearrange("p (b h) -> p b h", h=heads)
                        vec.tensor_copy(parts(i), shaped).then_inc(parts_made.sem, 1)
                        made += 1
                        dve.wait_ge(parts_made.sem, parts_made.at(stage, made))
                        if i < PARTS - 1:
                            o = rest if tab is tabS else rest.rearrange("p (b h) -> p b h", h=heads)
                            vec.tensor_tensor(o, shaped, parts(i), ALU.subtract).then_inc(parts_made.sem, 1)
                            made += 1
                            dve.wait_ge(parts_made.sem, parts_made.at(stage, made))
                            left = rest
                assert made == PARTS_AT
                hot = lambda s: blockhot[:, s % 2, :, 0:BLOCKS]

                def sources(c, s, r):
                    if s >= LOWHOTS[stage]:
                        dve.wait_ge(spread_landed[s].sem, spread_landed[s].at(stage, 16 * (r + 1)))
                        if due(c - 3):
                            dve.wait_ge(values_picked.sem, values_picked.at(stage, c - 3))
                        vec.tensor_scalar(lowhot[:, s, :], spread8[:, s, 0, :], part[:, 0:1], None, ALU.is_equal)\
                            .then_inc(lowhot_made[s].sem, 1)

                def source_blocks(c, s, r):
                    if due(c - 1):
                        dve.wait_ge(values_masked.sem, values_masked.at(stage, c - 1))
                    vec.tensor_tensor(hot(s), iota[:, 0:BLOCKS].unsqueeze(1).to_broadcast([P, G, BLOCKS]),
                                      srcblock[:, bass.ds(4 * c, G)].unsqueeze(2).to_broadcast([P, G, BLOCKS]),
                                      ALU.is_equal).then_inc(blockhot_made.sem, 1)

                def mask(c, s, r):
                    dve.wait_ge(values_picked.sem, values_picked.at(stage, c + 1))
                    dve.wait_ge(blockhot_made.sem, blockhot_made.at(stage, c + 2))
                    if due(c - 1):
                        dve.wait_ge(logit_made.sem, logit_made.at(stage, c - 1))
                    vec.tensor_tensor(masked[:, s % 2, 0:G * PICK * heads].rearrange("p (r h) -> p r h", h=heads),
                                      PS[s][:, 0:G * PICK * heads].rearrange("p (r h) -> p r h", h=heads),
                                      blockhot[:, s % 2, :, :].rearrange("p g b -> p (g b)").unsqueeze(2)
                                      .to_broadcast([P, G * PICK, heads]), ALU.mult).then_inc(values_masked.sem, 1)

                def add_up(c, s, r):
                    dve.wait_ge(values_masked.sem, values_masked.at(stage, c + 1))
                    vec.tensor_reduce(LG[:, bass.ds(4 * c, G), 0:heads],
                                      masked[:, s % 2, 0:G * PICK * heads].rearrange("p (g b h) -> p g h b", g=G, h=heads),
                                      AX, ALU.add).then_inc(logit_made.sem, 1)
                flow(dve, ITERS, 4, [(0, sources), (2, mask), (1, source_blocks), (3, add_up)])

            def softmax(stage):
                heads = HEADS_OF[stage]
                n = [0]

                def step(instruction):
                    n[0] += 1
                    instruction.then_inc(softmax_v.sem, 1)

                def settled():
                    dve.wait_ge(softmax_v.sem, softmax_v.at(stage, n[0]))

                L = LG[:, :, 0:heads]
                dve.wait_ge(logit_made.sem, logit_made.at(stage, CHUNKS))
                step(vec.scalar_tensor_tensor(L, L, SLOPE[stage], L, ALU.mult, ALU.max))
                settled()
                if stage == "L1":
                    z = PX[:, :, 0:heads]
                    step(vec.tensor_scalar(z, L, 0.0, -1000.0, ALU.is_equal, ALU.mult))
                    settled()
                    step(vec.tensor_tensor(L, L, z, ALU.add))
                    settled()
                step(vec.tensor_tensor(L, L, maskneg[:].unsqueeze(2).to_broadcast([P, STEPS, heads]), ALU.add))
                assert n[0] == LOGITS_AT[stage]
                dve.wait_ge(softmax_a.sem, softmax_a.at(stage, 1))
                for h in range(heads):
                    step(vec.tensor_tensor_scan(FT[:, h, :], breakF[:], LT[:, h, :], -BIG, ALU.add, ALU.max))
                assert n[0] == LOGITS_AT[stage] + heads
                dve.wait_ge(softmax_p.sem, softmax_p.at(stage, 2))
                settled()
                step(vec.tensor_tensor_scan(carryF[0:heads, 1:SPARTS + 1], spanF[0:heads, :], PS[4][0:heads, 0:SPARTS],
                                            -BIG, ALU.add, ALU.max))
                dve.wait_ge(softmax_p.sem, softmax_p.at(stage, 3))
                step(vec.tensor_copy(startF[:, 0:heads], PS[5][0:SPARTS, 0:heads]))
                settled()
                for h in range(heads):
                    step(vec.tensor_tensor_scan(FT[:, h, :], breakF[:], LT[:, h, :], startF[:, h:h + 1],
                                                ALU.add, ALU.max))
                settled()
                for h in range(heads):
                    step(vec.tensor_tensor_scan(BT[:, h, ::-1], breakB[:, ::-1], FT[:, h, ::-1], -BIG,
                                                ALU.add, ALU.max))
                dve.wait_ge(softmax_p.sem, softmax_p.at(stage, 4))
                settled()
                step(vec.tensor_tensor_scan(carryB[0:heads, SPARTS - 1::-1], spanB[0:heads, ::-1],
                                            PS[6][0:heads, SPARTS - 1::-1], -BIG, ALU.add, ALU.max))
                dve.wait_ge(softmax_p.sem, softmax_p.at(stage, 5))
                step(vec.tensor_copy(startB[:, 0:heads], PS[7][0:SPARTS, 0:heads]))
                settled()
                for h in range(heads):
                    step(vec.tensor_tensor_scan(BT[:, h, ::-1], breakB[:, ::-1], FT[:, h, ::-1],
                                                startB[:, h:h + 1], ALU.add, ALU.max))
                settled()
                step(vec.tensor_tensor(LT[:, 0:heads, :], LT[:, 0:heads, :], BT[:, 0:heads, :], ALU.subtract))
                assert n[0] == SHIFTED_AT[stage]
                if stage in ("L2a", "L2b"):
                    step(vec.tensor_tensor(FT[:, 0:heads, :], BT[:, 0:heads, :],
                                           first[:].unsqueeze(1).to_broadcast([SPARTS, heads, ROW]), ALU.mult))
                    assert n[0] == MAXIMA_AT[stage]
                dve.wait_ge(softmax_a.sem, softmax_a.at(stage, 2 + len(back_columns(stage))))

            def attend():
                g = SUM_PASS["L3"]
                vec.memset(ACC[:], 0.0).then_inc(sums_zeroed.sem, 1)
                vec.tensor_scalar(edge_bias[:], wK[:], scal[:, 1:2], scal[:, 2:3], ALU.mult, ALU.add).then_inc(bias_made.sem, 1)
                dve.wait_ge(bias_made.sem, 1)
                vec.tensor_tensor(edge_bias[:], edge_bias[:], valid[:], ALU.mult).then_inc(bias_made.sem, 1)
                dve.wait_ge(bias_made.sem, 2)
                vec.tensor_tensor(edge_bias[:], edge_bias[:], maskneg[:], ALU.add).then_inc(bias_made.sem, 1)
                dve.wait_ge(bias_made.sem, 3)
                dve.wait_ge(begins_spread.sem, 1)
                vec.tensor_scalar(begins[:], PS[3][:, 0:SPARTS], part[:, 0:1], None, ALU.is_equal).then_inc(bias_made.sem, 1)
                vec.tensor_scalar(minus_dloc[:], dloc[:], -1.0, None, ALU.mult).then_inc(bias_made.sem, 1)
                dve.wait_ge(bias_made.sem, 5)
                dve.wait_ge(sums_zeroed.sem, sums_zeroed.at("L3", 1))
                blocks = [None]

                def load(c, s, r):
                    if s == 0:
                        blocks[0] = load_blocks(dve, r)

                def dot(i):
                    def work(c, s, r):
                        k, j = 4 * c + i, 4 * s + i
                        dve.wait_ge(query_spread.sem, query_spread.at("L3", k + 1))
                        landed(dve, g, r, j)
                        if due(k - 1):
                            dve.wait_ge(logit_made.sem, logit_made.at("L3", k - 1))
                        vec.scalar_tensor_tensor(junk[:, i % 2, :], PS[QUERY_BANK[i]][:, 0:D], float(D) ** -0.5, kv[:, j, 0:D],
                                                 ALU.mult, ALU.mult, accum_out=score[:, s, i:i + 1]).then_inc(logit_made.sem, 1)
                    return work

                def add_bias(c, s, r):
                    dve.wait_ge(logit_made.sem, logit_made.at("L3", 4 * c + 4))
                    vec.tensor_tensor(scored[:, s, :], score[:, s, :], edge_bias[:, bass.ds(4 * c, G)], ALU.add)\
                        .then_inc(scores_ready.sem, 1)

                def scan_forward(c, s, r):
                    dve.wait_ge(scores_turned.sem, scores_turned.at("L3", c + 1))
                    dve.wait_ge(breaks_landed[s % 2].sem, breaks_landed[s % 2].at("L3", 32 * r + 16 * (s // 2) + 16))
                    start = -BIG
                    if not is_first(c):
                        dve.wait_ge(forward_made.sem, forward_made.at("L3", c))
                        start = forward[0:1, (s - 1) % 2, ROW - 1:ROW]
                    vec.tensor_tensor_scan(forward[0:1, s % 2, :], breaks[0:1, s % 2, 0, :], PS[2][0:1, :], start,
                                           ALU.add, ALU.max).then_inc(forward_made.sem, 1)

                def scan_back(c, s, r):
                    dve.wait_ge(forward_made.sem, forward_made.at("L3", c + 1))
                    if due(c - 1):
                        dve.wait_ge(maxima_turned.sem, maxima_turned.at("L3", c - 1))
                    vec.tensor_tensor_scan(segmax[0:1, s % 2, ::-1], breaks[0:1, s % 2, 1, ::-1], forward[0:1, s % 2, ::-1],
                                           -BIG, ALU.add, ALU.max).then_inc(segmax_made.sem, 1)

                def take_rise(c, s, r):
                    dve.wait_ge(segmax_made.sem, segmax_made.at("L3", c + 1))
                    if is_first(c):
                        vec.memset(rise[0:1, 0:1], 0.0).then_inc(rise_made.sem, 1)
                    else:
                        vec.tensor_scalar(rise[0:1, s % 2:s % 2 + 1], forward[0:1, (s - 1) % 2, ROW - 1:ROW],
                                          segmax[0:1, s % 2, 0:1], 0.0, ALU.subtract, ALU.min).then_inc(rise_made.sem, 1)

                def shift(c, s, r):
                    dve.wait_ge(maxima_turned.sem, maxima_turned.at("L3", c + 1))
                    if due(c - 1):
                        dve.wait_ge(weights_made.sem, weights_made.at("L3", c - 1))
                    vec.tensor_tensor(shifted[:, s % 2, 0:G], scored[:, s, :], PS[2][:, 0:G], ALU.subtract)\
                        .then_inc(scores_shifted.sem, 1)
                    vec.tensor_tensor(shifted[:, s % 2, G:G + 1], PS[2][:, G:G + 1], begins[:, bass.ds(c, 1)], ALU.mult)\
                        .then_inc(scores_shifted.sem, 1)

                def add(i):
                    def work(c, s, r):
                        k = 4 * c + i
                        dve.wait_ge(step_summed.sem, step_summed.at("L3", k + 1))
                        if due(k):
                            dve.wait_ge(sum_added.sem, sum_added.at("L3", k))
                        a = ACC[:, bass.ds(blocks[0][4 * s + i], 1), 0:D + 1].rearrange("p o c -> p (o c)")
                        if i == 0:
                            ins = vec.scalar_tensor_tensor(a, a, weight[:, s % 2, G:G + 1], PS[SUM_BANK[i]][:, 0:D + 1],
                                                           ALU.mult, ALU.add)
                        else:
                            ins = vec.tensor_tensor(a, a, PS[SUM_BANK[i]][:, 0:D + 1], ALU.add)
                        ins.then_inc(sum_added.sem, 1)
                    return work
                flow(dve, ITERS, 4, [(3, add_bias), (2, dot(0)), (2, dot(1)), (4, load), (2, dot(2)),
                                     (3, scan_forward), (4, add(0)), (3, scan_back), (4, add(1)), (3, take_rise),
                                     (4, add(2)), (2, dot(3)), (4, add(3)), (3, shift)])

            def scales(stage):
                heads = HEADS_OF[stage]
                width = WIDTH[stage] - (stage == "L3")
                n = [0]

                def step(instruction):
                    n[0] += 1
                    instruction.then_inc(scales_made.sem, 1)

                def settled():
                    dve.wait_ge(scales_made.sem, scales_made.at(stage, n[0]))

                dve.wait_ge(sum_added.sem, sum_added.at(stage, STEPS))
                den = ACC[:, :, width:width + heads]
                A, B, C = (t[:, :, 0:heads] for t in (nodeA, nodeB, nodeC))
                if stage in ("L1", "L3"):
                    step(vec.tensor_scalar(A, den, 1e-12, None, ALU.max))
                    settled()
                    step(vec.reciprocal(A, A))
                else:
                    top = ACC[:, :, width + heads:width + 2 * heads]
                    has = ACC[:, :, width + 2 * heads:width + 2 * heads + 1].to_broadcast([P, BLOCKS, heads])
                    step(vec.tensor_scalar(A, has, -1.0, BIG, ALU.add, ALU.mult))
                    step(vec.tensor_tensor(B, by_head(tabS, heads), by_head(tabD, heads), ALU.add))
                    settled()
                    step(vec.tensor_tensor(A, A, top, ALU.add))
                    step(vec.scalar_tensor_tensor(B, B, SLOPE[stage], B, ALU.mult, ALU.max))
                    settled()
                    step(vec.tensor_tensor(C, A, B, ALU.max))
                    settled()
                    step(vec.tensor_tensor(A, A, C, ALU.subtract))
                    step(vec.tensor_tensor(B, B, C, ALU.subtract))
                    assert n[0] == 7
                    dve.wait_ge(scales_exp.sem, scales_exp.at(stage, 2))
                    step(vec.tensor_tensor(C, den, A, ALU.mult))
                    settled()
                    step(vec.tensor_tensor(C, C, B, ALU.add))
                    settled()
                    step(vec.reciprocal(C, C))
                    settled()
                    step(vec.tensor_tensor(A, A, C, ALU.mult))
                    step(vec.tensor_tensor(B, B, C, ALU.mult))
                settled()
                assert n[0] == SCALES[stage]

            def statistics(name, buf):
                sig = norms_of[name]

                def work(b, v, r):
                    dve.wait_ge(sig["summed"].sem, sig["summed"].at(name, b + 1))
                    dve.sem_inc(wait_carried.sem, 1)
                    vec.bn_stats(stat[:, NORM_PLACE[name] + v, :], buf(b)).then_inc(sig["stats"].sem, 1)
                return work

            def mean_variance(name):
                sig = norms_of[name]

                def work(b, v, r):
                    i = NORM_PLACE[name] + v
                    dve.wait_ge(sig["stats"].sem, sig["stats"].at(name, b + 1))
                    dve.sem_inc(wait_carried.sem, 1)
                    vec.bn_aggr(moments[:, i, :], stat[:, i, :]).then_inc(sig["moments"].sem, 1)
                return work

            def add_eps(name):
                sig = norms_of[name]

                def work(b, v, r):
                    i = NORM_PLACE[name] + v
                    dve.wait_ge(sig["moments"].sem, sig["moments"].at(name, b + 1))
                    vec.tensor_scalar(variance[:, i:i + 1], moments[:, i, 1:2], EPS, None, ALU.add)\
                        .then_inc(sig["variance"].sem, 1)
                return work

            def apply(name, buf, o, done):
                sig = norms_of[name]

                def work(b, v, r):
                    i = NORM_PLACE[name] + v
                    dve.wait_ge(sig["rstd"].sem, sig["rstd"].at(name, b + 1))
                    vec.tensor_scalar(o(b, v), buf(b), moments[:, i, 0:1], rstd[:, i:i + 1], ALU.subtract, ALU.mult)\
                        .then_inc(done.sem, 1)
                return work

            def centre(name, buf, gain):
                sig = norms_of[name]

                def work(b, v, r):
                    dve.wait_ge(sig["moments"].sem, sig["moments"].at(name, b + 1))
                    vec.scalar_tensor_tensor(buf(b), buf(b), moments[:, NORM_PLACE[name] + v, 0:1], gain[:],
                                             ALU.subtract, ALU.mult).then_inc(sig["centred"].sem, 1)
                return work

            def finish(name, buf, term, o, done):
                sig = norms_of[name]

                def work(b, v, r):
                    i = NORM_PLACE[name] + v
                    dve.wait_ge(sig["centred"].sem, sig["centred"].at(name, b + 1))
                    dve.wait_ge(sig["rstd"].sem, sig["rstd"].at(name, b + 1))
                    vec.scalar_tensor_tensor(o(b, v), buf(b), rstd[:, i:i + 1], term(b), ALU.mult, ALU.add)\
                        .then_inc(done.sem, 1)
                return work

            def x_block(b, v=None):
                return at_block(X, b)

            def acc_block(b, v=None):
                return at_block(ACC, b)[:, 0:D]

            def row_at(place):
                return lambda b, v: rows[:, place + v, 0:D]

            def mlp_input(b, v, r):
                if due(b - V + 1):
                    dve.wait_ge(in_turned.sem, in_turned.at("L0", b - V + 1))
                vec.scalar_tensor_tensor(rows[:, INPUT + v, 0:D], at_block(X, b), onePeps[:], acc_block(b),
                                         ALU.mult, ALU.add).then_inc(input_ready.sem, 1)

            def mlp_sum(b, v, r):
                dve.wait_ge(branch_made.sem, branch_made.at("L0", b + 1))
                dve.wait_ge(term_made.sem, term_made.at("L0", b + 1))
                vec.tensor_tensor(acc_block(b), PS[4 + v % 2][:, 0:D], rows[:, TERM + v, 0:D], ALU.add)\
                    .then_inc(norms_of["mlp"]["summed"].sem, 1)

            def middle_free(layer):
                def work(b, v, r):
                    if due(b - V + 1):
                        dve.wait_ge(mid_turned.sem, mid_turned.at(layer, b - V + 1))
                        if layer == "L3":
                            dve.wait_ge(fed_term_made.sem, fed_term_made.at(layer, b - V + 1))
                        else:
                            dve.wait_ge(kept.sem, kept.at(layer, b - V + 1))
                return work

            sum_edges("L0")
            dve.wait_ge(sum_added.sem, sum_added.at("L0", STEPS))
            dve.wait_ge(features_in.sem, 32)
            flow(dve, VITERS, V, [(0, mlp_input), (3, mlp_sum), (3, statistics("mlp", acc_block)), (4, middle_free("L0")),
                                  (4, apply("mlp", acc_block, row_at(MIDDLE), middle_ready)),
                                  (3, mean_variance("mlp")), (3, add_eps("mlp"))], 2)
            logits_gat("L1")
            softmax("L1")
            sum_edges("L1")
            scales("L1")

            def gat_sum(b, v, r):
                dve.wait_ge(term_made.sem, term_made.at("L1", b + 1))
                vec.tensor_tensor(at_block(X, b), at_block(X, b), acc_block(b), ALU.add)\
                    .then_inc(norms_of["gat"]["summed"].sem, 1)

            def input_free(b, v, r):
                if due(b - V + 1):
                    dve.wait_ge(in_turned.sem, in_turned.at("L1", b - V + 1))
                    dve.wait_ge(kept.sem, kept.at("L1", b - V + 1))
            flow(dve, VITERS, V, [(0, gat_sum), (0, statistics("gat", x_block)), (1, input_free),
                                  (1, apply("gat", x_block, row_at(INPUT), input_ready)),
                                  (0, mean_variance("gat")), (0, add_eps("gat"))])
            logits_gat("L2a")
            softmax("L2a")
            sum_edges("L2a")
            scales("L2a")

            def self_scale(b, v, r):
                ah = acc_block(b).rearrange("p (h f) -> p h f", h=HEADS)
                vec.tensor_tensor(ah, ah, at_block(nodeA, b).unsqueeze(2).to_broadcast([P, HEADS, HID]), ALU.mult)\
                    .then_inc(sums_scaled.sem, 1)

            def self_add(b, v, r):
                dve.wait_ge(sums_scaled.sem, sums_scaled.at("L2a", b + 1))
                dve.wait_ge(term_made.sem, term_made.at("L2a", b + 1))
                vec.tensor_tensor(acc_block(b), acc_block(b), at_block(Y, b), ALU.add).then_inc(loop_added.sem, 1)

            def self_bias(b, v, r):
                dve.wait_ge(loop_added.sem, loop_added.at("L2a", b + 1))
                vec.tensor_tensor(acc_block(b), acc_block(b), bias["b3"][:], ALU.add).then_inc(bias_added.sem, 1)
            flow(dve, VITERS, V, [(0, self_scale), (1, self_bias), (0, self_add)])
            logits_gat("L2b")
            softmax("L2b")
            sum_edges("L2b")
            scales("L2b")

            def sums_block(b):
                return at_block(ACC, b)[:, 0:HID]

            def out_scale(b, v, r):
                vec.tensor_scalar(sums_block(b), sums_block(b), at_block(nodeA, b)[:, 0:1], None, ALU.mult)\
                    .then_inc(sums_scaled.sem, 1)

            def out_add(b, v, r):
                dve.wait_ge(sums_scaled.sem, sums_scaled.at("L2b", b + 1))
                vec.scalar_tensor_tensor(sums_block(b), at_block(Y, b)[:, 0:HID], at_block(nodeB, b)[:, 0:1], sums_block(b),
                                         ALU.mult, ALU.add).then_inc(loop_added.sem, 1)

            def out_bias(b, v, r):
                dve.wait_ge(loop_added.sem, loop_added.at("L2b", b + 1))
                if due(b - V + 1):
                    dve.wait_ge(in_turned.sem, in_turned.at("L2b", b - V + 1))
                vec.tensor_tensor(rows[:, INPUT + v, 0:HID], sums_block(b), bias["b4"][:], ALU.add)\
                    .then_inc(input_ready.sem, 1)

            def self_sum(b, v, r):
                dve.wait_ge(branch_made.sem, branch_made.at("L2b", b + 1))
                dve.wait_ge(term_made.sem, term_made.at("L2b", b + 1))
                vec.tensor_tensor(acc_block(b), PS[2][:, 0:D], at_block(X, b), ALU.add)\
                    .then_inc(norms_of["self"]["summed"].sem, 1)

            def add_bias(i, w, o):
                def work(b, v, r):
                    dve.wait_ge(projected.sem, projected.at("L2b", 3 * b + i + 1))
                    if i == 1 and due(b - V + 1):
                        dve.wait_ge(table_stored[v].sem, table_stored[v].at("L2b", 32 * r))
                    vec.tensor_tensor(o(b, v), PS[3 + (3 * v + i) % 5][:, 0:D], bias[w][:], ALU.add)\
                        .then_inc(projection_copied.sem, 1)
                return work
            flow(dve, VITERS, V, [(0, out_scale), (2, self_sum), (0, out_add),
                                  (6, add_bias(0, "bq", lambda b, v: at_block(Y, b))),
                                  (0, out_bias), (2, statistics("self", acc_block)), (3, middle_free("L2b")),
                                  (3, apply("self", acc_block, row_at(MIDDLE), middle_ready)),
                                  (6, add_bias(1, "bk", lambda b, v: keys[:, v, :])), (2, mean_variance("self")),
                                  (6, add_bias(2, "bv", lambda b, v: values[:, v, :])), (2, add_eps("self"))], 2)
            for v in range(V):
                dve.wait_ge(table_stored[v].sem, table_stored[v].at("L2b", TABLE_LOOPS["L2b"]))
            attend()
            scales("L3")

            def attended(b, v, r):
                dve.wait_ge(term_made.sem, term_made.at("L3", b + 1))
                vec.scalar_tensor_tensor(acc_block(b), acc_block(b), at_block(nodeA, b)[:, 0:1], at_block(Y, b),
                                         ALU.mult, ALU.add).then_inc(sums_scaled.sem, 1)

            def attended_sum(b, v, r):
                dve.wait_ge(branch_made.sem, branch_made.at("L3", b + 1))
                dve.wait_ge(sums_scaled.sem, sums_scaled.at("L3", b + 1))
                vec.tensor_tensor(acc_block(b), PS[4 + v % 2][:, 0:D], acc_block(b), ALU.add)\
                    .then_inc(norms_of["attended"]["summed"].sem, 1)

            def fed_sum(b, v, r):
                dve.wait_ge(fed_made.sem, fed_made.at("L3", b + 1))
                dve.wait_ge(fed_term_made.sem, fed_term_made.at("L3", b + 1))
                vec.tensor_tensor(acc_block(b), PS[6 + v % 2][:, 0:D], rows[:, TERM + v, 0:D], ALU.add)\
                    .then_inc(norms_of["fed"]["summed"].sem, 1)

            def last_term_ready(b, v, r):
                dve.wait_ge(last_term_made.sem, last_term_made.at("L3", b + 1))

            flow(dve, VITERS, V, [(1, attended_sum), (5, fed_sum), (1, statistics("attended", acc_block)),
                                  (5, statistics("fed", acc_block)), (6, statistics("last", acc_block)),
                                  (1, mean_variance("attended")), (5, mean_variance("fed")), (6, mean_variance("last")),
                                  (1, add_eps("attended")), (5, add_eps("fed")), (6, add_eps("last")),
                                  (1, centre("attended", acc_block, bias["g1"])), (5, centre("fed", acc_block, bias["g2"])),
                                  (1, middle_free("L3")),
                                  (1, finish("attended", acc_block, lambda b: bias["h1"][:], row_at(MIDDLE), middle_ready)),
                                  (0, attended), (5, last_term_ready),
                                  (5, finish("fed", acc_block, x_block, acc_block, norms_of["last"]["summed"])),
                                  (6, apply("last", acc_block, x_block, kept))], 2)

        @block.tensor
        def _(pe):
            mm = nc.tensor.matmul
            pe.wait_ge(setup_v.sem, STEP_GE_AT)
            for g in range(G):
                last = mm(PS[0][:, 0:STEPS], ones[0:EP, :], step_ge[:, g, :], start=g == 0, stop=g == G - 1)
            last.then_inc(setup_p.sem, 1)
            pe.wait_ge(setup_v.sem, EDGES_AT)
            for i, t in enumerate((srcT, dstT, wT)):
                for g in range(G):
                    last = mm(PS[1 + i][:, 0:STEPS], t[:, g * P:(g + 1) * P], pick[:, g, :],
                              start=g == 0, stop=g == G - 1)
            last.then_inc(setup_p.sem, 1)
            pe.wait_ge(setup_v.sem, DSTM_AT)
            for g in range(G):
                last = nc.tensor.transpose(PS[4][0:SPARTS, g * P:(g + 1) * P], dstM[:, g::G], ident[:])
            last.then_inc(setup_p.sem, 1)
            pe.wait_ge(setup_v.sem, DT_AT)
            mm(PS[5][0:SPARTS, 0:1], up[0:SPARTS, 0:SPARTS], DT[:, ROW - 1:ROW], start=True, stop=True)\
                .then_inc(setup_p.sem, 1)
            pe.wait_ge(setup_v.sem, BREAK_AT)
            mm(PS[5][0:SPARTS, 1:2], down[0:SPARTS, 0:SPARTS], breakF[:, 0:1], start=True, stop=True)\
                .then_inc(setup_p.sem, 1)
            pe.wait_ge(setup_v.sem, SPAN_AT)
            for i in range(2):
                last = mm(PS[6][0:HEADS, i * SPARTS:(i + 1) * SPARTS], brk[:, i, :], ident[0:SPARTS, 0:SPARTS],
                          start=True, stop=True)
            last.then_inc(setup_p.sem, 1)
            pe.wait_ge(setup_v.sem, PLACES_AT)
            for bank, source in ((1, srcF), (3, dlocF)):
                for g in range(G):
                    last = nc.tensor.transpose(PS[bank][0:SPARTS, g * P:(g + 1) * P], source[:, g::G], ident[:])
            last.then_inc(setup_p.sem, 1)
            pe.wait_ge(setup_v.sem, SETUP_V)

            def sum_edges(stage):
                g = SUM_PASS[stage]
                cols = WIDTH[stage] + EXTRAS.get(stage, 0)

                def body(it):
                    for j in range(U):
                        k = U * it + j
                        pe.wait_ge(onehot_made.sem, onehot_made.at(stage, k + 1))
                        if stage in SCALED:
                            pe.wait_ge(row_scaled.sem, row_scaled.at(stage, k + 1))
                            pe.wait_ge(extras_put.sem, extras_put.at(stage, k + 1))
                            moving = R[:, j % 4, 0:cols]
                        else:
                            landed(pe, g, it, j)
                            moving = rows[:, j, 0:cols]
                        if due(k - 3):
                            pe.wait_ge(sum_added.sem, sum_added.at(stage, k - 3))
                        mm(PS[j % 4][:, 0:cols], M[:, j % 4, :], moving, start=True, stop=True)\
                            .then_inc(step_summed.sem, 1)
                each(pe, ITERS, body)

            def logits_gat(stage):
                heads = HEADS_OF[stage]
                n, cols = BLOCKS * heads, PICK * heads
                pe.wait_ge(parts_made.sem, parts_made.at(stage, PARTS_AT))

                def body(it):
                    blocks = load_blocks(pe, it)
                    for s in range(4):
                        c = 4 * it + s
                        pe.wait_ge(lowhot_made[s].sem, lowhot_made[s].at(stage, it + 1))
                        if due(c - 3):
                            pe.wait_ge(values_masked.sem, values_masked.at(stage, c - 3))
                        for g in range(G):
                            for i in range(PARTS):
                                mm(PS[s][:, g * cols:g * cols + n], lowhot[:, s, g * P:(g + 1) * P],
                                   partsS[:, i * n:(i + 1) * n], start=i == 0, stop=i == PARTS - 1)
                        pe.wait_ge(dsthot_made.sem, dsthot_made.at(stage, c + 1))
                        for g in range(G):
                            last = mm(PS[s][:, g * cols + n:(g + 1) * cols], dsthot[:, s, g * P:(g + 1) * P],
                                      at_block(partsD[:, 0:PARTS * n].rearrange("p (b c) -> p b c", c=PARTS * heads),
                                               blocks[4 * s + g]), start=True, stop=True)
                        last.then_inc(values_picked.sem, 1)
                each(pe, ITERS, body)

            def attend():
                mm(PS[3][:, 0:SPARTS], ones[0:1, :], dloc[0:1, ::G], start=True, stop=True).then_inc(begins_spread.sem, 1)
                pe.wait_ge(bias_made.sem, 4)
                pe.wait_ge(ends_set.sem, 1)
                blocks = [None]

                def load(c, s, r):
                    if s == 0:
                        blocks[0] = load_blocks(pe, r)

                def spread_query(i):
                    def work(c, s, r):
                        if i == 0:
                            pe.wait_ge(dsthot_made.sem, dsthot_made.at("L3", c + 1))
                        if due(4 * c + i - 3):
                            pe.wait_ge(logit_made.sem, logit_made.at("L3", 4 * c + i - 3))
                        mm(PS[QUERY_BANK[i]][:, 0:D], dsthotF[:, s % 2, i * P:(i + 1) * P], at_block(Y, blocks[0][4 * s + i]),
                           start=True, stop=True).then_inc(query_spread.sem, 1)
                    return work

                def turn_scores(c, s, r):
                    pe.wait_ge(scores_ready.sem, scores_ready.at("L3", c + 1))
                    if due(2 * c):
                        pe.wait_ge(scores_shifted.sem, scores_shifted.at("L3", 2 * c))
                    for i in range(G):
                        last = nc.tensor.transpose(PS[2][0:1, i * P:(i + 1) * P], scored[:, s, i:i + 1], ident[:])
                    last.then_inc(scores_turned.sem, 1)

                def turn_maxima(c, s, r):
                    pe.wait_ge(rise_made.sem, rise_made.at("L3", c + 1))
                    pe.wait_ge(forward_made.sem, forward_made.at("L3", c + 1))
                    mm(PS[2][:, G:G + 1], ones[0:1, :], rise[0:1, s % 2:s % 2 + 1], start=True, stop=True)
                    for i in range(G):
                        last = nc.tensor.transpose(PS[2][:, i:i + 1], segmax[0:1, s % 2, i * P:(i + 1) * P], ident[0:1, 0:1])
                    last.then_inc(maxima_turned.sem, 1)

                def sum_step(i):
                    def work(c, s, r):
                        k, j = 4 * c + i, 4 * s + i
                        pe.wait_ge(onehot_made.sem, onehot_made.at("L3", k + 1))
                        if due(4 * c + FREED[i]):
                            pe.wait_ge(sum_added.sem, sum_added.at("L3", 4 * c + FREED[i]))
                        mm(PS[SUM_BANK[i]][:, 0:D + 1], M[:, i, :], kv[:, j, D:2 * D + 1], start=True, stop=True)\
                            .then_inc(step_summed.sem, 1)
                    return work
                flow(pe, ITERS, 4, [(2, turn_scores), (3, sum_step(0)), (3, sum_step(1)), (3, sum_step(2)),
                                    (0, load), (0, spread_query(0)), (3, sum_step(3)), (0, spread_query(1)),
                                    (2, turn_maxima), (0, spread_query(2)), (0, spread_query(3))])

            def softmax(stage):
                heads = HEADS_OF[stage]
                pe.wait_ge(softmax_v.sem, softmax_v.at(stage, LOGITS_AT[stage]))
                for h in range(heads):
                    for g in range(G):
                        last = nc.tensor.transpose(PS[h][0:SPARTS, g * P:(g + 1) * P], LG[:, g::G, h], ident[:])
                last.then_inc(softmax_p.sem, 1)
                pe.wait_ge(softmax_v.sem, softmax_v.at(stage, LOGITS_AT[stage] + heads))
                nc.tensor.transpose(PS[4][0:heads, 0:SPARTS], FT[:, 0:heads, ROW - 1], ident[0:SPARTS, 0:SPARTS])\
                    .then_inc(softmax_p.sem, 1)
                pe.wait_ge(softmax_v.sem, softmax_v.at(stage, LOGITS_AT[stage] + heads + 1))
                nc.tensor.transpose(PS[5][0:SPARTS, 0:heads], carryF[0:heads, 0:SPARTS], ident[0:heads, 0:heads])\
                    .then_inc(softmax_p.sem, 1)
                pe.wait_ge(softmax_v.sem, softmax_v.at(stage, LOGITS_AT[stage] + 3 * heads + 2))
                nc.tensor.transpose(PS[6][0:heads, 0:SPARTS], BT[:, 0:heads, 0], ident[0:SPARTS, 0:SPARTS])\
                    .then_inc(softmax_p.sem, 1)
                pe.wait_ge(softmax_v.sem, softmax_v.at(stage, LOGITS_AT[stage] + 3 * heads + 3))
                nc.tensor.transpose(PS[7][0:SPARTS, 0:heads], carryB[0:heads, 1:SPARTS + 1], ident[0:heads, 0:heads])\
                    .then_inc(softmax_p.sem, 1)
                pe.wait_ge(softmax_a.sem, softmax_a.at(stage, 2))
                for c, source in enumerate(back_columns(stage)):
                    if c >= 4:
                        if due(3 + c - 4):
                            pe.wait_ge(softmax_a.sem, softmax_a.at(stage, 3 + c - 4))
                    if stage in MAXIMA_AT and c == heads:
                        pe.wait_ge(softmax_v.sem, softmax_v.at(stage, MAXIMA_AT[stage]))
                    for g in range(G):
                        last = nc.tensor.transpose(PS[c % 4][:, g * SPARTS:(g + 1) * SPARTS],
                                                   source[:, g * P:(g + 1) * P], ident[0:SPARTS, 0:SPARTS])
                    last.then_inc(softmax_p.sem, 1)

            def turned(layer, place, ready, signal, copied, bank, chunks=KC):
                def work(b, v, r):
                    pe.wait_ge(ready.sem, ready.at(layer, b + 1))
                    if due(b):
                        pe.wait_ge(copied.sem, copied.at(layer, b))
                    for k in range(chunks):
                        last = nc.tensor.transpose(PS[bank][:, k * P:(k + 1) * P],
                                                   rows[:, place + v, k * P:(k + 1) * P], ident[:])
                    last.then_inc(signal.sem, 1)
                return work

            def turned_input(layer, chunks=KC):
                return turned(layer, INPUT, input_ready, in_turned, in_copied, 0, chunks)

            def turned_middle(layer):
                return turned(layer, MIDDLE, middle_ready, mid_turned, mid_copied, 1)

            def product(b, v, bank, left, right, cols, signal):
                for k, (lhsT, rhs) in enumerate(zip(left, right)):
                    last = mm(PS[bank][:, 0:cols], lhsT, rhs, start=k == 0, stop=k == len(left) - 1)
                last.then_inc(signal.sem, 1)

            def projection(layer, source, copied, weights, cols):
                def work(b, v, r):
                    pe.wait_ge(copied.sem, copied.at(layer, b + 1))
                    if due(b - AGE[v] + 1):
                        pe.wait_ge(projection_copied.sem, projection_copied.at(layer, b - AGE[v] + 1))
                    product(b, v, 6 + v % 2, [source[:, v, k, :] for k in range(KC)],
                            [weights[:, k, 0:cols] for k in range(KC)], cols, projected)
                return work

            def hidden(layer, source, copied, weights, mids):
                def work(b, v, r):
                    pe.wait_ge(copied.sem, copied.at(layer, b + 1))
                    if due(b - AGE[v] + 1):
                        pe.wait_ge(hidden_acted.sem, hidden_acted.at(layer, b - AGE[v] + 1))
                    for m in range(mids):
                        for k in range(KC):
                            last = mm(PS[2 + v % 2][:, m * P:(m + 1) * P], weights[:, k, m * P:(m + 1) * P],
                                      source[:, v, k, :], start=k == 0, stop=k == KC - 1)
                    last.then_inc(hidden_made.sem, 1)
                return work

            def from_hidden(layer, weights, mids, bank, added, signal):
                sig = norms_of[added]["summed"]

                def work(b, v, r):
                    pe.wait_ge(hidden_acted.sem, hidden_acted.at(layer, b + 1))
                    if due(b - AGE[v] + 1):
                        pe.wait_ge(sig.sem, sig.at(added, b - AGE[v] + 1))
                    product(b, v, bank + v % 2, [hidT[:, v, m, :] for m in range(mids)],
                            [weights[:, m, :] for m in range(mids)], D, signal)
                return work

            def branch(layer, left, right, bank, banks, added):
                sig = norms_of[added]["summed"]

                def work(b, v, r):
                    age = AGE[v] if banks == 2 else 1
                    pe.wait_ge(in_copied.sem, in_copied.at(layer, b + 1))
                    if due(b - age + 1):
                        pe.wait_ge(sig.sem, sig.at(added, b - age + 1))
                    product(b, v, bank + v % banks, left(v), right, D, branch_made)
                return work

            def queries_keys_values(b, v, r):
                pe.wait_ge(mid_copied.sem, mid_copied.at("L2b", b + 1))
                for i, w in enumerate((wq, wk, wv)):
                    if due(3 * b + i - 4):
                        pe.wait_ge(projection_copied.sem, projection_copied.at("L2b", 3 * b + i - 4))
                    for k in range(KC):
                        last = mm(PS[3 + (3 * v + i) % 5][:, 0:D], midT["L2b"][:, v, k, :], w[:, k, :],
                                  start=k == 0, stop=k == KC - 1)
                    last.then_inc(projected.sem, 1)

            def sums_done(stage):
                pe.wait_ge(sum_added.sem, sum_added.at(stage, STEPS))

            sum_edges("L0")
            sums_done("L0")
            flow(pe, VITERS, V, [(0, turned_input("L0")), (1, hidden("L0", inT, in_copied, w1, KC)),
                                 (2, from_hidden("L0", w2, KC, 4, "mlp", branch_made)),
                                 (5, projection("L0", midT["L0"], mid_copied, wz1, ZW)),
                                 (4, turned_middle("L0"))], 2)
            pe.wait_ge(projection_copied.sem, projection_copied.at("L0", BLOCKS))
            logits_gat("L1")
            softmax("L1")
            sum_edges("L1")
            sums_done("L1")
            flow(pe, VITERS, V, [(0, turned_input("L1")), (1, projection("L1", inT, in_copied, wz2, ZW))])
            pe.wait_ge(projection_copied.sem, projection_copied.at("L1", BLOCKS))
            logits_gat("L2a")
            softmax("L2a")
            sum_edges("L2a")
            sums_done("L2a")
            flow(pe, VITERS, V, [(0, turned_input("L2a")), (1, projection("L2a", inT, in_copied, wz3, HID + 2))])
            pe.wait_ge(projection_copied.sem, projection_copied.at("L2a", BLOCKS))
            logits_gat("L2b")
            softmax("L2b")
            sum_edges("L2b")
            sums_done("L2b")
            flow(pe, VITERS, V, [(0, turned_input("L2b", 1)),
                                 (1, branch("L2b", lambda v: [inT[0:HID, v, 0, :]], [wf[:]], 2, 1, "self")),
                                 (5, queries_keys_values), (4, turned_middle("L2b"))])
            pe.wait_ge(projection_copied.sem, projection_copied.at("L2b", 3 * BLOCKS))
            attend()
            sums_done("L3")
            flow(pe, VITERS, V, [(0, turned_input("L3")), (3, turned_middle("L3")),
                                 (4, hidden("L3", midT["L3"], mid_copied, wff1, FF // P)),
                                 (1, branch("L3", lambda v: [inT[:, v, k, :] for k in range(KC)],
                                            [ws[:, k, :] for k in range(KC)], 4, 2, "attended")),
                                 (5, from_hidden("L3", wff2, FF // P, 6, "fed", fed_made))], 2)

        @block.scalar
        def _(act):
            sc = nc.scalar

            def put_indices(k, half):
                cols = bass.ds(k, HALF)
                sc.activation(idx[:, half, :], srcK[:, cols], ACT.Copy).then_inc(indices_put.sem, 1)

            act.wait_ge(setup_v.sem, SOURCES_AT)
            put_indices(0, 0)
            put_indices(HALF, 1)

            def edge_loop(g, per_step):
                def body(it):
                    for j in range(U):
                        if per_step:
                            per_step(it, j)
                        if j % HALF == HALF - 1:
                            for i in range(j + 1 - HALF, j + 1):
                                landed(act, g, it, i)
                            put_indices(U * it + U + j + 1 - HALF, j // HALF)
                each(act, ITERS, body)

            def sum_edges(stage):
                if stage not in SCALED:
                    edge_loop(SUM_PASS[stage], None)
                    return
                width, extra = WIDTH[stage], EXTRAS[stage]

                def per_step(it, j):
                    k = U * it + j
                    col = bass.ds(k, 1)
                    if due(k - 3):
                        act.wait_ge(step_summed.sem, step_summed.at(stage, k - 3))
                    sc.activation(R[:, j % 4, width:width + extra], PX[:, col, 0:extra].rearrange("p o c -> p (o c)"),
                                  ACT.Copy).then_inc(extras_put.sem, 1)
                edge_loop(SUM_PASS[stage], per_step)

            def logits_gat(stage):
                def distance(it, s):
                    c = 4 * it + s
                    act.wait_ge(spread_landed[s].sem, spread_landed[s].at(stage, 16 * (it + 1)))
                    if due(c - 1):
                        act.wait_ge(dsthot_made.sem, dsthot_made.at(stage, c - 1))
                    sc.activation(apart[:, s % 2, :], spread8[:, s, 1, :], ACT.Abs, bias=minus[:])\
                        .then_inc(dst_apart.sem, 1)

                def body(it):
                    for s in range(4):
                        c = 4 * it + s
                        if s < 3:
                            distance(it, s + 1)
                        elif not is_last(it, ITERS):
                            distance(it + 1, 0)
                        act.wait_ge(dst_apart.sem, dst_apart.at(stage, c + 1))
                        if due(c - 3):
                            act.wait_ge(values_picked.sem, values_picked.at(stage, c - 3))
                        sc.activation(dsthot[:, s, :], apart[:, s % 2, :], ACT.Relu, bias=1.0, scale=-1.0)\
                            .then_inc(dsthot_made.sem, 1)
                distance(0, 0)
                each(act, ITERS, body)

            def softmax(stage):
                heads = HEADS_OF[stage]
                n = [0]

                def step(instruction):
                    n[0] += 1
                    instruction.then_inc(softmax_a.sem, 1)
                act.wait_ge(softmax_p.sem, softmax_p.at(stage, 1))
                for h in range(heads):
                    last = sc.activation(LT[:, h, :], PS[h][0:SPARTS, :], ACT.Copy)
                step(last)
                act.wait_ge(softmax_v.sem, softmax_v.at(stage, SHIFTED_AT[stage]))
                step(sc.activation(LT[:, 0:heads, :], LT[:, 0:heads, :], ACT.Exp))
                for c, _ in enumerate(back_columns(stage)):
                    act.wait_ge(softmax_p.sem, softmax_p.at(stage, 6 + c))
                    step(sc.activation(PX[:, :, c].rearrange("p (q g) -> p g q", g=G),
                                       PS[c % 4][:, 0:STEPS].rearrange("p (g q) -> p g q", g=G), ACT.Copy))
                act.wait_ge(softmax_a.sem, softmax_a.at(stage, n[0]))

            def attend():
                g = SUM_PASS["L3"]

                def next_indices(c, s, r):
                    if s % 2:
                        half = s // 2
                        for j in range(HALF * half, HALF * (half + 1)):
                            landed(act, g, r, j)
                        put_indices(U * r + U + HALF * half, half)

                def distance(c, s, r):
                    act.wait_ge(spread_landed[s].sem, spread_landed[s].at("L3", 16 * (r + 1)))
                    if due(c - 1):
                        act.wait_ge(dsthot_made.sem, dsthot_made.at("L3", c - 1))
                    sc.activation(apartF[:, s % 2, :], spread8[:, s, 1, :], ACT.Abs, bias=minus[:]).then_inc(dst_apart.sem, 1)

                def hots(c, s, r):
                    act.wait_ge(dst_apart.sem, dst_apart.at("L3", c + 1))
                    if due(4 * (c - 1)):
                        act.wait_ge(query_spread.sem, query_spread.at("L3", 4 * (c - 1)))
                    sc.activation(dsthotF[:, s % 2, :], apartF[:, s % 2, :], ACT.Relu, bias=1.0, scale=-1.0)\
                        .then_inc(dsthot_made.sem, 1)

                def nearness(c, s, r):
                    if due(4 * c):
                        act.wait_ge(onehot_made.sem, onehot_made.at("L3", 4 * c))
                    for i in range(G):
                        sc.activation(near[:, i, :], iota[:], ACT.Abs, bias=minus_dloc[:, bass.ds(4 * c + i, 1)])\
                            .then_inc(near_made.sem, 1)

                def weigh(c, s, r):
                    act.wait_ge(scores_shifted.sem, scores_shifted.at("L3", 2 * (c + 1)))
                    if due(4 * (c - 1)):
                        act.wait_ge(sum_added.sem, sum_added.at("L3", 4 * (c - 1)))
                    sc.activation(weight[:, s % 2, :], shifted[:, s % 2, :], ACT.Exp).then_inc(weights_made.sem, 1)
                    act.wait_ge(weights_made.sem, weights_made.at("L3", c + 1))
                    sc.activation(minus_weight[:, s % 2, :], weight[:, s % 2, 0:G], ACT.Copy, scale=-1.0)\
                        .then_inc(weights_negated.sem, 1)

                def onehot(i):
                    def work(c, s, r):
                        k = 4 * c + i
                        if i == 0:
                            act.wait_ge(near_made.sem, near_made.at("L3", 4 * c + 4))
                            act.wait_ge(weights_negated.sem, weights_negated.at("L3", c + 1))
                        if due(k - 3):
                            act.wait_ge(step_summed.sem, step_summed.at("L3", k - 3))
                        sc.activation(M[:, i, :], near[:, i, :], ACT.Relu, scale=minus_weight[:, s % 2, i:i + 1],
                                      bias=weight[:, s % 2, i:i + 1]).then_inc(onehot_made.sem, 1)
                    return work
                act.wait_ge(bias_made.sem, 5)
                flow(act, ITERS, 4, [(4, weigh), (4, onehot(0)), (4, onehot(1)), (4, onehot(2)), (4, onehot(3)),
                                     (2, next_indices), (0, distance), (0, hots), (3, nearness)])

            def copied(layer, o, turned_by, signal, used, bank, chunks=KC, width=P):
                def work(b, v, r):
                    act.wait_ge(turned_by.sem, turned_by.at(layer, b + 1))
                    if due(b - V + 1):
                        used(b - V + 1)
                    sc.activation(o[0:width, v, 0:chunks, :], PS[bank][0:width, 0:chunks * P]
                                  .rearrange("p (k n) -> p k n", k=chunks), ACT.Copy).then_inc(signal.sem, 1)
                return work

            def copied_input(layer, used, chunks=KC, width=P):
                return copied(layer, inT, in_turned, in_copied, used, 0, chunks, width)

            def copied_middle(layer, used):
                return copied(layer, midT[layer], mid_turned, mid_copied, used, 1)

            def activate(layer, mids, func, biases, used):
                def work(b, v, r):
                    act.wait_ge(hidden_made.sem, hidden_made.at(layer, b + 1))
                    if due(b - V + 1):
                        act.wait_ge(used.sem, used.at(layer, b - V + 1))
                    for m in range(mids):
                        last = sc.activation(hidT[:, v, m, :], PS[2 + v % 2][:, m * P:(m + 1) * P], func, bias=biases[:, m:m + 1])
                    last.then_inc(hidden_acted.sem, 1)
                return work

            def copy_out(layer, cols, tabs):
                h = (cols - tabs) // 2

                def work(b, v, r):
                    act.wait_ge(projected.sem, projected.at(layer, b + 1))
                    bank = PS[6 + v % 2]
                    sc.activation(at_block(by_head(tabS, h), b), bank[:, tabs:tabs + h], ACT.Copy)
                    sc.activation(at_block(by_head(tabD, h), b), bank[:, tabs + h:cols], ACT.Copy)
                    sc.activation(at_block(Y, b)[:, 0:tabs], bank[:, 0:tabs], ACT.Copy).then_inc(projection_copied.sem, 1)
                return work

            def scales(stage):
                heads = HEADS_OF[stage]
                act.wait_ge(scales_made.sem, scales_made.at(stage, 7))
                for t in (nodeA, nodeB):
                    sc.activation(t[:, :, 0:heads], t[:, :, 0:heads], ACT.Exp).then_inc(scales_exp.sem, 1)

            def keep_input(b, v, r):
                act.wait_ge(input_ready.sem, input_ready.at("L1", b + 1))
                sc.activation(at_block(X, b), rows[:, INPUT + v, 0:D], ACT.Copy).then_inc(kept.sem, 1)

            def clip(b, v, r):
                act.wait_ge(bias_added.sem, bias_added.at("L2a", b + 1))
                if due(b - V + 1):
                    act.wait_ge(in_turned.sem, in_turned.at("L2a", b - V + 1))
                sc.activation(rows[:, INPUT + v, 0:D], at_block(ACC, b)[:, 0:D], ACT.Relu).then_inc(input_ready.sem, 1)

            def stage_input(b, v, r):
                if due(b - V + 1):
                    act.wait_ge(in_turned.sem, in_turned.at("L3", b - V + 1))
                sc.activation(rows[:, INPUT + v, 0:D], at_block(X, b), ACT.Copy).then_inc(input_ready.sem, 1)

            def by(signal, layer, times=1):
                return lambda n: act.wait_ge(signal.sem, signal.at(layer, times * n))

            edge_loop(0, None)
            act.wait_ge(edges_stored.sem, 16 * 3)
            act.wait_ge(weights_in.sem, 16 * len(weight_loads))
            flow(act, VITERS, V, [(0, copied_input("L0", by(hidden_made, "L0"))),
                                  (1, activate("L0", KC, ACT.Relu, b1c, branch_made)), (5, copy_out("L0", ZW, D)),
                                  (4, copied_middle("L0", by(projected, "L0")))], 2)
            logits_gat("L1")
            softmax("L1")
            sum_edges("L1")
            flow(act, VITERS, V, [(0, copied_input("L1", by(projected, "L1"))), (1, keep_input), (1, copy_out("L1", ZW, D))])
            logits_gat("L2a")
            softmax("L2a")
            sum_edges("L2a")
            scales("L2a")
            flow(act, VITERS, V, [(0, clip), (1, copied_input("L2a", by(projected, "L2a"))), (2, copy_out("L2a", HID + 2, HID))])
            logits_gat("L2b")
            softmax("L2b")
            sum_edges("L2b")
            scales("L2b")
            flow(act, VITERS, V, [(0, copied_input("L2b", by(branch_made, "L2b"), 1, HID)),
                                  (4, copied_middle("L2b", by(projected, "L2b", 3)))])
            attend()
            act.wait_ge(sum_added.sem, sum_added.at("L3", STEPS))
            flow(act, VITERS, V, [(0, stage_input), (1, copied_input("L3", by(branch_made, "L3"))),
                                  (4, copied_middle("L3", by(hidden_made, "L3"))),
                                  (5, activate("L3", FF // P, ACT.Gelu_apprx_tanh, bff1c, fed_made))], 2)


INPUTS = ["x", "src", "dst", "edge_weight", "L0_gnn_eps", "L0_gnn_w1", "L0_gnn_b1", "L0_gnn_w2", "L0_gnn_b2",
          "L1_gnn_W", "L1_gnn_att", "L2_gnn_W1", "L2_gnn_att_src1", "L2_gnn_att_dst1", "L2_gnn_b1", "L2_gnn_W2",
          "L2_gnn_att_src2", "L2_gnn_att_dst2", "L2_gnn_b2", "L2_gnn_Wf", "L2_gnn_bf", "L3_gnn_wq", "L3_gnn_bq",
          "L3_gnn_wk", "L3_gnn_bk", "L3_gnn_wv", "L3_gnn_bv", "L3_gnn_ws", "L3_gnn_bs", "L3_gnn_we", "L3_gnn_be",
          "L3_gnn_g1", "L3_gnn_b1", "L3_gnn_g2", "L3_gnn_b2", "L3_gnn_w_ff1", "L3_gnn_b_ff1", "L3_gnn_w_ff2",
          "L3_gnn_b_ff2"]


def kernel(**inputs):
    import concourse.bacc as bacc
    from concourse.bass_utils import run_bass_kernel_spmd

    nc = bacc.Bacc("TRN2", target_bir_lowering=False, num_devices=1)
    arrays, args = {}, []
    for name in INPUTS:
        a = np.ascontiguousarray(inputs[name])
        arrays["in_" + name] = a
        args.append(nc.dram_tensor("in_" + name, a.shape, mybir.dt.from_np(a.dtype), kind="ExternalInput").ap())
    args.append(nc.dram_tensor("result", (N, D), F32, kind="ExternalOutput").ap())
    build(nc, *args)
    ran = run_bass_kernel_spmd(nc, [arrays], core_ids=[0])
    return ran.results[0]["result"]
```
